# Optimizing a Trainium2 kernel written in Bass

```python
import numpy as np
import jax
import jax.numpy as jnp

def _softmax(x, axis=-1):
    return jax.nn.softmax(x, axis=axis)

def _gelu(x):
    return jax.nn.gelu(x, approximate=True)

def _silu(x):
    return jax.nn.silu(x)

def _sigmoid(x):
    return jax.nn.sigmoid(x)

def _layernorm(x, axis=-1, eps=1e-05):
    m = jnp.mean(x, axis=axis, keepdims=True)
    v = jnp.var(x, axis=axis, keepdims=True)
    return (x - m) / jnp.sqrt(v + eps)

def _scatter_add(tgt, idx, src, axis=0):
    return tgt.at[idx].add(src)

def _segment_sum(src, seg, n):
    return jax.ops.segment_sum(src, seg, n)
kernel_name = 'mk_sandwich_d1_jaxref_r8_5f1181'

def setup_inputs(seed: int=0):
    np.random.seed(seed)
    _w = jnp.asarray

    def _L0_attn_setup():
        import jax, jax.numpy as jnp
        import numpy as np
        D_MODEL = 256
        N_HEADS = 16
        D_HEAD = D_MODEL // N_HEADS
        key = jax.random.key(seed)
        kx, kq, kk, kv, ko = jax.random.split(key, 5)
        s = 1.0 / np.sqrt(D_MODEL)
        return {'x': jax.random.normal(kx, (4, 256, D_MODEL), dtype=jnp.float32), 'Wq': jax.random.normal(kq, (D_MODEL, D_MODEL), dtype=jnp.float32) * s, 'Wk': jax.random.normal(kk, (D_MODEL, D_MODEL), dtype=jnp.float32) * s, 'Wv': jax.random.normal(kv, (D_MODEL, D_MODEL), dtype=jnp.float32) * s, 'Wo': jax.random.normal(ko, (D_MODEL, D_MODEL), dtype=jnp.float32) * s}
    _L0_attn_in = _L0_attn_setup()

    def _L0_ffn_setup():
        import jax, jax.numpy as jnp
        import numpy as np
        H = 256
        NH = 16
        NOPE = 128
        ROPE = 64
        VD = 128
        QHD = NOPE + ROPE
        E = 16
        I = 176
        TOPK = 4
        NSH = 2
        SHI = I * NSH
        EPS = 1e-06
        B, S = (2, 128)

        def rmsnorm(x, w):
            return x * jax.lax.rsqrt(jnp.mean(x * x, axis=-1, keepdims=True) + EPS) * w
        key = jax.random.key(seed)
        ks = jax.random.split(key, 12)
        sd = lambda fan_in: 1.0 / np.sqrt(fan_in)
        return {'hidden_states': jax.random.normal(ks[0], (B, S, H), jnp.float32), 'positions': jnp.broadcast_to(jnp.arange(S, dtype=jnp.int32), (B, S)), 'ln1_w': jnp.ones((H,), jnp.float32), 'ln2_w': jnp.ones((H,), jnp.float32), 'q_w': jax.random.normal(ks[1], (NH * QHD, H), jnp.float32) * sd(H), 'kv_w': jax.random.normal(ks[2], (NH * (NOPE + VD) + ROPE, H), jnp.float32) * sd(H), 'o_w': jax.random.normal(ks[3], (H, NH * VD), jnp.float32) * sd(NH * VD), 'gate_w': jax.random.normal(ks[4], (E, H), jnp.float32) * sd(H), 'w1': jax.random.normal(ks[5], (E, 2 * I, H), jnp.float32) * sd(H), 'w2': jax.random.normal(ks[6], (E, H, I), jnp.float32) * sd(I), 'sh_gu_w': jax.random.normal(ks[7], (2 * SHI, H), jnp.float32) * sd(H), 'sh_down_w': jax.random.normal(ks[8], (H, SHI), jnp.float32) * sd(SHI)}
    _L0_ffn_in = _L0_ffn_setup()
    _d = {'L0_attn_x': _L0_attn_in['x'], 'L0_attn_Wq': _L0_attn_in['Wq'], 'L0_attn_Wk': _L0_attn_in['Wk'], 'L0_attn_Wv': _L0_attn_in['Wv'], 'L0_attn_Wo': _L0_attn_in['Wo'], 'L0_ffn_positions': _L0_ffn_in['positions'], 'L0_ffn_ln1_w': _L0_ffn_in['ln1_w'], 'L0_ffn_ln2_w': _L0_ffn_in['ln2_w'], 'L0_ffn_q_w': _L0_ffn_in['q_w'], 'L0_ffn_kv_w': _L0_ffn_in['kv_w'], 'L0_ffn_o_w': _L0_ffn_in['o_w'], 'L0_ffn_gate_w': _L0_ffn_in['gate_w'], 'L0_ffn_w1': _L0_ffn_in['w1'], 'L0_ffn_w2': _L0_ffn_in['w2'], 'L0_ffn_sh_gu_w': _L0_ffn_in['sh_gu_w'], 'L0_ffn_sh_down_w': _L0_ffn_in['sh_down_w']}
    _x0 = _d['L0_attn_x']
    _d['L0_attn_x'] = jax.random.normal(jax.random.fold_in(jax.random.key(seed), 1), (4, 512, 256), dtype=_x0.dtype)
    del _x0
    return _d

def reference(L0_attn_x, L0_attn_Wq, L0_attn_Wk, L0_attn_Wv, L0_attn_Wo, L0_ffn_positions, L0_ffn_ln1_w, L0_ffn_ln2_w, L0_ffn_q_w, L0_ffn_kv_w, L0_ffn_o_w, L0_ffn_gate_w, L0_ffn_w1, L0_ffn_w2, L0_ffn_sh_gu_w, L0_ffn_sh_down_w):

    def _L0_attn_ref(x, Wq, Wk, Wv, Wo):
        import jax, jax.numpy as jnp
        import numpy as np
        D_MODEL = 256
        N_HEADS = 16
        D_HEAD = D_MODEL // N_HEADS
        B, S, _ = x.shape
        scale = D_HEAD ** (-0.5)

        def split_heads(t):
            return t.reshape(B, S, N_HEADS, D_HEAD).transpose(0, 2, 1, 3)
        q = split_heads(x @ Wq.T)
        k = split_heads(x @ Wk.T)
        v = split_heads(x @ Wv.T)
        sim = jnp.einsum('bhsd,bhtd->bhst', q, k) * scale
        causal = jnp.tril(jnp.ones((S, S), dtype=bool))
        sim = jnp.where(causal[None, None], sim, -jnp.inf)
        weights = jax.nn.softmax(sim, axis=-1)
        out = jnp.einsum('bhst,bhtd->bhsd', weights, v)
        out = out.transpose(0, 2, 1, 3).reshape(B, S, D_MODEL)
        return out @ Wo.T

    def _L0_ffn_ref(hidden_states, positions, ln1_w, ln2_w, q_w, kv_w, o_w, gate_w, w1, w2, sh_gu_w, sh_down_w):
        import jax, jax.numpy as jnp
        import numpy as np
        H = 256
        NH = 16
        NOPE = 128
        ROPE = 64
        VD = 128
        QHD = NOPE + ROPE
        E = 16
        I = 176
        TOPK = 4
        NSH = 2
        SHI = I * NSH
        EPS = 1e-06
        B, S = (2, 128)

        def rmsnorm(x, w):
            return x * jax.lax.rsqrt(jnp.mean(x * x, axis=-1, keepdims=True) + EPS) * w
        b, s, h = hidden_states.shape
        x = rmsnorm(hidden_states, ln1_w)
        q = jnp.einsum('bsh,dh->bsd', x, q_w).reshape(b, s, NH, QHD)[..., :NOPE]
        kv = jnp.einsum('bsh,dh->bsd', x, kv_w)
        k = kv[..., :NH * NOPE].reshape(b, s, NH, NOPE)
        v = kv[..., NH * NOPE:NH * (NOPE + VD)].reshape(b, s, NH, VD)
        scale = QHD ** (-0.5)
        scores = jnp.einsum('bqnd,bknd->bnqk', q, k) * scale
        causal = jnp.tril(jnp.ones((s, s), bool))
        scores = jnp.where(causal, scores, -1000000000.0)
        p = jax.nn.softmax(scores, axis=-1)
        attn = jnp.einsum('bnqk,bknd->bqnd', p, v).reshape(b, s, NH * VD)
        attn_out = jnp.einsum('bsd,hd->bsh', attn, o_w)
        hid = hidden_states + attn_out
        x2 = rmsnorm(hid, ln2_w).reshape(-1, h)
        logits = x2 @ gate_w.T
        probs = jax.nn.softmax(logits, axis=-1)
        top_w, top_i = jax.lax.top_k(probs, TOPK)
        top_w = top_w / jnp.sum(top_w, axis=-1, keepdims=True)
        wfull = jnp.sum(jax.nn.one_hot(top_i, E, dtype=x2.dtype) * top_w[..., None], axis=1)
        gu = jnp.einsum('th,eih->tei', x2, w1)
        g, u = (gu[..., :I], gu[..., I:])
        act = jax.nn.silu(g) * u
        down = jnp.einsum('tei,ehi->teh', act, w2)
        routed = jnp.einsum('te,teh->th', wfull, down)
        sgu = x2 @ sh_gu_w.T
        sg, su = (sgu[..., :SHI], sgu[..., SHI:])
        shared = jax.nn.silu(sg) * su @ sh_down_w.T
        return hid + (routed + shared).reshape(b, s, h)
    x = L0_attn_x
    x = x + _layernorm(_L0_attn_ref(_layernorm(x, axis=-1), L0_attn_Wq, L0_attn_Wk, L0_attn_Wv, L0_attn_Wo), axis=-1)
    x = x + _layernorm(_L0_ffn_ref(_layernorm(x, axis=-1), L0_ffn_positions, L0_ffn_ln1_w, L0_ffn_ln2_w, L0_ffn_q_w, L0_ffn_kv_w, L0_ffn_o_w, L0_ffn_gate_w, L0_ffn_w1, L0_ffn_w2, L0_ffn_sh_gu_w, L0_ffn_sh_down_w), axis=-1)
    return x

_drawn_inputs = setup_inputs


def setup_inputs(seed=0):
    import zlib

    import numpy as np

    out = dict(_drawn_inputs(seed))
    spreads = {'L0_ffn_ln1_w': (1.0, 0.2), 'L0_ffn_ln2_w': (1.0, 0.2)}
    factors = {}
    for name, (base, spread) in spreads.items():
        noise = np.random.default_rng([zlib.crc32(name.encode()), seed]).standard_normal(out[name].shape)
        drawn = base * np.exp(spread * noise) if base else spread * noise
        out[name] = jnp.asarray(drawn.astype(out[name].dtype))
    for name, factor in factors.items():
        out[name] = (out[name] * factor).astype(out[name].dtype)
    return out
```

```python
from contextlib import ExitStack

import concourse.bass as bass
from concourse import mybir

F32 = mybir.dt.float32
F32R = mybir.dt.float32r
BF16 = mybir.dt.bfloat16
ALU = mybir.AluOpType
ACT = mybir.ActivationFunctionType
AX = mybir.AxisListType
ds = bass.ds

P = 128
HI, LO = 0, 1
PARTS = ((HI, HI), (LO, HI), (HI, LO))
MASKED = -1e30
LN_EPS = 1e-5
RMS_EPS = 1e-6


def run_steps(eng, step, total, period, first, ahead):
    loops = (total - first - ahead) // period
    for k in range(first):
        step(0, k)
    with eng.Fori(0, loops) as it:
        for k in range(first, first + period):
            step(it, k)
    for k in range(first, total - loops * period):
        step(loops, k)


def first_then_loop(eng, step, total):
    step(0)
    with eng.Fori(1, total) as i:
        step(i)


def later(i):
    return not isinstance(i, int) or i > 0


def sandwich_kernel(nc, x_d, qkv1_d, wo1_d, qkvo2_d, ln_w_d, gate_d, moe_d, stack_d, out_d):
    B, TB, D = x_d.shape
    C = D // P
    T = B * TB // P
    TPB = TB // P
    H1, H2 = 16, qkvo2_d.shape[0]
    DH1 = D // H1
    GH = P // DH1
    G1 = B * H1 // GH
    E = gate_d.shape[2]
    EI = 176
    MG, _, MGC, _ = moe_d.shape
    TOPK = 4
    SCALE1 = float(DH1) ** -0.5
    SCALE2 = 192.0 ** -0.5
    WQKV2 = 3 * C * P
    QOFF = [0]
    for kj in range(TPB):
        QOFF.append(QOFF[-1] + TB - P * kj)
    POFF = [P * qi * (qi + 1) // 2 for qi in range(TPB + 1)]
    CAUSAL = QOFF[TPB]

    ctx = ExitStack()
    with ctx:
        def sb(stack, name, shape, dt=F32):
            return stack.enter_context(nc.sbuf_tensor(name, shape, dt))

        def sem(name):
            return ctx.enter_context(nc.semaphore(name))

        bank = [ctx.enter_context(nc.psum_tensor(f"bank{i}", [P, 512], F32)) for i in range(8)]

        x_sb = sb(ctx, "x_sb", [P, T, D])
        hs = sb(ctx, "hs", [P, T, D])
        acc = sb(ctx, "acc", [P, C, B * TB])
        xT = sb(ctx, "xT", [P, 2, C, B * TB], F32R)
        ident = sb(ctx, "ident", [P, P])
        ident_b = sb(ctx, "ident_b", [P, P], BF16)
        mask_f = sb(ctx, "mask_f", [P, P])
        mask_b = sb(ctx, "mask_b", [P, P], BF16)
        ln_w = sb(ctx, "ln_w", [P, 2, C])
        gate_raw = sb(ctx, "gate_raw", [P, C, E])
        gate_hl = sb(ctx, "gate_hl", [P, 2, C, E], F32R)
        wo1 = sb(ctx, "wo1", [P, C, D])
        raw_qkv = sb(ctx, "raw_qkv", [P, WQKV2])
        raw_o = sb(ctx, "raw_o", [P, D])
        raw_moe = sb(ctx, "raw_moe", [P, MGC, 3 * C * P])
        st6 = sb(ctx, "st6", [P, T, 6])
        sm = sb(ctx, "sm", [P, 12, T])
        v1 = hs[:, :, :].rearrange("p t d -> p (t d)").rearrange("p (g k n) -> p g k n", g=G1, k=TPB)
        oT1 = acc[:, :, :].rearrange("p c t -> p (c t)").rearrange("p (g t) -> p g t", g=G1)
        q1_hl = xT[:, :, :, :].rearrange("p a c t -> p (a c t)").rearrange("p (g a t) -> p g a t", g=G1, a=2)

        with ExitStack() as l1:
            k1_hl = sb(l1, "k1_hl", [P, G1, 2, TB], F32R)
            v1_pad = sb(l1, "v1_pad", [P, TPB, GH, P])
            p1 = sb(l1, "p1", [P, 2, CAUSAL])
            pT1 = sb(l1, "pT1", [P, CAUSAL])
            stk = sb(l1, "stk", [P, 2, 2, TB], F32R)
            sel_raw = sb(l1, "sel_raw", [P, 16 * P])
            sel = sb(l1, "sel", [P, 16 * P], F32R)
            xn1 = sb(l1, "xn1", [P, TPB, D])
            xT1 = sb(l1, "xT1", [P, C, TB])
            qkv1 = sb(l1, "qkv1", [P, C, 3 * D])
            stat1 = sb(l1, "stat1", [P, 3, 2, TPB])
        with ExitStack() as l12:
            y_sb = sb(l12, "y_sb", [P, T, D])
            u_sb = sb(l12, "u_sb", [P, T, D])
        with ExitStack() as l2:
            w2_hl = sb(l2, "w2_hl", [P, 2, WQKV2], F32R)
            wo2_hl = sb(l2, "wo2_hl", [P, 2, D], F32R)
            qk2 = sb(l2, "qk2", [P, 2, 2, TB], F32R)
            v2 = sb(l2, "v2", [P, 2, 2, TB], F32R)
            p2 = sb(l2, "p2", [P, 2, CAUSAL])
            pT2 = sb(l2, "pT2", [P, 2, CAUSAL], F32R)
            o2 = sb(l2, "o2", [P, 2, TB], F32R)
            stat2 = sb(l2, "stat2", [P, 3, 2, TPB])
        with ExitStack() as l3:
            xn2 = sb(l3, "xn2", [P, T, D])
            moe_hl = sb(l3, "moe_hl", [P, MGC, 2, 3 * C * P], F32R)
            sel_c = sb(l3, "sel_c", [64, MGC, P], F32R)
            sel_f = sb(l3, "sel_f", [64, MG, MGC, P])
            wT = sb(l3, "wT", [64, B * TB], F32R)
            h_s = sb(l3, "h_s", [P, 2, TB])
            h_t = sb(l3, "h_t", [P, 2, TB])
            h_hl = sb(l3, "h_hl", [P, 2, 2, TB], F32R)
            lg = sb(l3, "lg", [P, T, E])
            pr = sb(l3, "pr", [P, T, E])
            rk = sb(l3, "rk", [P, T, E, E], BF16)
            wtok = sb(l3, "wtok", [P, T, E + 2])

        x_in = [sem(f"x_in{b}") for b in range(B)]
        w1_in = sem("w1_in"); wo1_in = sem("wo1_in"); sel_in = sem("sel_in"); small_in = sem("small_in")
        const = sem("const")
        chain = sem("chain")
        root_in = sem("root_in"); root = sem("root")
        sel_ok = sem("sel_ok")
        pool_met = sem("pool_met")
        ph1_xn = sem("ph1_xn"); ph1_tp = sem("ph1_tp"); ph1_xT = sem("ph1_xT"); ph1_mm = sem("ph1_mm")
        ph1_hi = sem("ph1_hi"); ph1_lo = sem("ph1_lo"); ph1_v = sem("ph1_v")
        a1_sel = sem("a1_sel"); a1_stk = sem("a1_stk"); a1_s = sem("a1_s"); a1_max = sem("a1_max")
        a1_exp = sem("a1_exp"); a1_rcp = sem("a1_rcp"); a1_norm = sem("a1_norm"); a1_t = sem("a1_t")
        a1_pta = sem("a1_pta"); a1_ptd = sem("a1_ptd"); a1_pv = sem("a1_pv"); a1_vpad = sem("a1_vpad")
        a1_zero = sem("a1_zero"); a1_o = sem("a1_o")
        m_y = sem("m_y"); m_ys = sem("m_ys"); m_u = sem("m_u"); m_nrm = sem("m_nrm"); m_x1 = sem("m_x1")
        m_hs = sem("m_hs"); m_xn = sem("m_xn"); m_tp = sem("m_tp"); m_hi = sem("m_hi"); m_lo = sem("m_lo")
        b_rawqkv = sem("b_rawqkv"); b_rawo = sem("b_rawo"); b_wqkv = sem("b_wqkv"); b_wo = sem("b_wo")
        b_qkv = sem("b_qkv"); b_hi = sem("b_hi"); b_lo = sem("b_lo"); b_s = sem("b_s"); b_max = sem("b_max")
        b_exp = sem("b_exp"); b_rcp = sem("b_rcp"); b_norm = sem("b_norm"); b_t = sem("b_t")
        b_pth = sem("b_pth"); b_ptl = sem("b_ptl"); b_pv = sem("b_pv"); b_oh = sem("b_oh"); b_ol = sem("b_ol")
        b_e = sem("b_e"); b_acc = sem("b_acc")
        r_tp = sem("r_tp"); r_hid = sem("r_hid"); r_xn = sem("r_xn"); r_tp2 = sem("r_tp2"); r_hi = sem("r_hi")
        r_lo = sem("r_lo"); r_lg = sem("r_lg"); r_sub = sem("r_sub"); r_exp = sem("r_exp"); r_w = sem("r_w")
        r_tp3 = sem("r_tp3"); r_wh = sem("r_wh"); r_wl = sem("r_wl"); r_gate = sem("r_gate")
        r_sel = sem("r_sel"); r_zero = sem("r_zero")
        e_raw = sem("e_raw"); e_split = sem("e_split"); e_g = sem("e_g"); e_w = sem("e_w"); e_u = sem("e_u")
        e_silu = sem("e_silu"); e_sw = sem("e_sw"); e_h = sem("e_h"); e_hh = sem("e_hh"); e_hlo = sem("e_hlo")
        e_dn = sem("e_dn"); e_acc = sem("e_acc")
        f_tp = sem("f_tp"); f_y = sem("f_y"); f_u = sem("f_u"); f_nrm = sem("f_nrm"); f_out = sem("f_out")
        stored = sem("stored")
        b_half = sem("b_half"); b_acc0 = sem("b_acc0"); e_half = sem("e_half"); gate_ok = sem("gate_ok"); gate_lo = sem("gate_lo"); gate_in = sem("gate_in")
        fence = [sem(f"fence{i}") for i in range(4)]

        def meet(eng, i):
            eng.drain().then_inc(fence[i], 1)
            eng.wait_ge(fence[i], 5)

        def pool_wait(pool, sem_, value):
            pool.wait_ge(sem_, value)
            if not isinstance(value, int):
                pool.sem_inc(pool_met, 1)

        def f32(ap):
            return ap.bitcast(F32)

        block = ctx.enter_context(nc.Block())
        PAIRS1 = GH // 2
        N1 = G1 * GH
        N2 = H2 * B
        PER3 = B * MGC
        NE = MG * PER3
        u_out = xn2

        @block.sync
        def _(sp):
            for b in range(B):
                sp.dma_start(x_sb[:, TPB * b:TPB * (b + 1), :],
                             x_d[b].rearrange("(j p) d -> p j d", p=P)).then_inc(x_in[b], 16)
            sp.dma_start(qkv1[:, :, :], qkv1_d).then_inc(w1_in, 16)
            sp.dma_start(sel_raw[:, :], stack_d).then_inc(sel_in, 16)
            sp.dma_start(wo1[:, :, :], wo1_d).then_inc(wo1_in, 16)
            sp.dma_start(ln_w[:, :, :], ln_w_d).then_inc(small_in, 16)
            sp.dma_start(gate_raw[:, :, :], gate_d).then_inc(gate_in, 16)
            sp.dma_start(raw_qkv[:, :], qkvo2_d[0, :, 0:WQKV2]).then_inc(b_rawqkv, 16)
            sp.dma_start(raw_o[:, :], qkvo2_d[0, :, WQKV2:]).then_inc(b_rawo, 16)
            sp.dma_start(raw_moe[:, :, :], moe_d[0]).then_inc(e_raw, 16)
            meet(sp, 0)
            meet(sp, 1)
            meet(sp, 2)
            with sp.Fori(1, H2) as h:
                sp.wait_ge(b_wqkv, h * 1)
                sp.dma_start(raw_qkv[:, :], qkvo2_d[ds(h, 1), :, 0:WQKV2].rearrange("a p n -> p (a n)"))\
                    .then_inc(b_rawqkv, 16)
                sp.wait_ge(b_wo, h * 1)
                sp.dma_start(raw_o[:, :], qkvo2_d[ds(h, 1), :, WQKV2:].rearrange("a p n -> p (a n)"))\
                    .then_inc(b_rawo, 16)
            meet(sp, 3)
            with sp.Fori(1, MG) as g:
                sp.wait_ge(e_split, g * MGC)
                sp.dma_start(raw_moe[:, :, :], moe_d[ds(g, 1)].rearrange("a p c n -> p (a c) n"))\
                    .then_inc(e_raw, 16)
            for b in range(B):
                sp.wait_ge(f_out, b + 1)
                sp.dma_start(out_d[b].rearrange("(j p) d -> p j d", p=P),
                             u_out[:, TPB * b:TPB * (b + 1), :]).then_inc(stored, 16)
            sp.wait_ge(stored, 16 * B)

        @block.gpsimd
        def _(pool):
            pool.memset(ident[:, :], 0.0).then_inc(const, 1)
            pool.memset(mask_f[:, :], 0.0).then_inc(const, 1)
            pool.wait_ge(const, 2)
            pool.affine_select(out=ident[:, :], in_=ident[:, :], compare_op=ALU.not_equal, fill=1.0, base=0,
                               pattern=[[-1, P]], channel_multiplier=1).then_inc(const, 1)
            pool.affine_select(out=mask_f[:, :], in_=mask_f[:, :], compare_op=ALU.is_ge, fill=MASKED, base=0,
                               pattern=[[-1, P]], channel_multiplier=1).then_inc(const, 1)
            pool.wait_ge(const, 4)
            pool.tensor_copy(ident_b[:, :], ident[:, :]).then_inc(const, 1)
            pool.tensor_copy(mask_b[:, :], mask_f[:, :]).then_inc(const, 1)
            pool.memset(v1_pad[:, :, :, :], 0.0).then_inc(a1_zero, 1)
            pool.wait_ge(a1_zero, 1)
            meet(pool, 0)

            def fill_v(g, head):
                pool.tensor_copy(v1_pad[:, :, head, DH1 * head:DH1 * (head + 1)],
                                 v1[:, g, :, DH1 * head:DH1 * (head + 1)]).then_inc(a1_vpad, 1)

            for head in range(GH):
                fill_v(0, head)

            def step1(it, k):
                n = it * GH + k
                if isinstance(n, int) and n >= N1:
                    return
                pool_wait(pool, a1_rcp, n + 1)
                for t in range(TPB):
                    qi = TPB - 1 - t
                    pt = p1[:, k % 2, POFF[qi]:POFF[qi + 1]]
                    pool.tensor_scalar(pt, pt, stat1[:, 2, k % 2, t:t + 1], None, ALU.mult).then_inc(a1_norm, 1)
                if not isinstance(n, int) or (n >= 2 and n + GH - 2 < N1):
                    pool_wait(pool, a1_pv, (n - 1) * TPB)
                    fill_v(it + (k + GH - 2) // GH, (k - 2) % GH)

            run_steps(pool, step1, N1, GH, 2, GH - 2)
            meet(pool, 1)
            pool.wait_ge(m_y, T // 2)
            pool.memset(acc[:, :, :], 0.0).then_inc(b_acc0, 1)
            meet(pool, 2)

            def split2(raw, hl, count, done):
                pool.tensor_copy(hl[:, HI, :], raw[:, :]).then_inc(b_half, 1)
                pool_wait(pool, b_half, count)
                pool.tensor_tensor(hl[:, LO, :], raw[:, :], f32(hl[:, HI, :]), ALU.subtract).then_inc(done, 1)

            pool_wait(pool, b_rawqkv, 16)
            split2(raw_qkv, w2_hl, 1, b_wqkv)
            pool_wait(pool, b_rawo, 16)
            split2(raw_o, wo2_hl, 2, b_wo)

            def step2(it, k):
                n = it * B + k
                static = isinstance(n, int)
                if static and n >= N2:
                    return
                if k % B == B - 1 and (not static or n + 1 < N2):
                    head = it + (k + 1) // B
                    pool_wait(pool, b_rawqkv, head * 16 + 16)
                    pool_wait(pool, b_qkv, n * 3 + 3)
                    split2(raw_qkv, w2_hl, head * 2 + 1, b_wqkv)
                pool_wait(pool, b_rcp, n + 1)
                for t in range(TPB):
                    qi = TPB - 1 - t
                    pt = p2[:, k % 2, POFF[qi]:POFF[qi + 1]]
                    pool.tensor_scalar(pt, pt, stat2[:, 2, k % 2, t:t + 1], None, ALU.mult).then_inc(b_norm, 1)
                if k % B == 1 and (not static or n > B):
                    head = it + k // B
                    pool_wait(pool, b_rawo, head * 16 + 16)
                    pool_wait(pool, b_e, (n - 1) * C)
                    split2(raw_o, wo2_hl, head * 2 + 2, b_wo)

            run_steps(pool, step2, N2, B, 2, 2)
            meet(pool, 3)

            pool.memset(sel_f[:, :, :, :], 1.0).then_inc(r_sel, 1)
            pool.memset(f32(wT[:, :]), 0.0).then_inc(r_zero, 1)
            pool.wait_ge(r_sel, 1)
            cnt = 1
            for half in range(2):
                part = sel_f[32 * half:32 * half + 32, :, :, :].rearrange("p g c n -> p (g c n)")
                width = MG * MGC * P
                for base, sign in ((0, 1), (EI - 1, -1)):
                    pool.affine_select(out=part, in_=part, compare_op=ALU.is_ge, fill=0.0, base=base,
                                       pattern=[[sign, width]], channel_multiplier=-sign * EI).then_inc(r_sel, 1)
                    cnt += 1
                    pool.wait_ge(r_sel, cnt)

            def split_moe(g, c, count):
                pool.tensor_copy(sel_c[:, c, :], sel_f[:, g, c, :]).then_inc(e_half, 1)
                pool.tensor_copy(moe_hl[:, c, HI, :], raw_moe[:, c, :]).then_inc(e_half, 1)
                pool_wait(pool, e_half, count)
                pool.tensor_tensor(moe_hl[:, c, LO, :], raw_moe[:, c, :], f32(moe_hl[:, c, HI, :]),
                                   ALU.subtract).then_inc(e_split, 1)

            pool_wait(pool, e_raw, 16)
            for c in range(MGC):
                split_moe(0, c, 2 * c + 2)
            pool.wait_ge(r_tp, T // 2)
            pool.memset(acc[:, :, :], 0.0).then_inc(r_zero, 1)

            def step3(it, k):
                n = it * PER3 + k
                static = isinstance(n, int)
                if not static or n < NE:
                    pool_wait(pool, e_hh, n + 1)
                    pool.tensor_tensor(h_hl[:, k % 2, LO, :], h_t[:, k % 2, :], f32(h_hl[:, k % 2, HI, :]),
                                       ALU.subtract).then_inc(e_hlo, 1)
                m = k - 2
                if 0 <= m < PER3 and m // MGC == B - 1 and (not static or it + 1 < MG):
                    c = m % MGC
                    pool_wait(pool, e_raw, it * 16 + 32)
                    pool_wait(pool, e_dn, (n - 1) * C)
                    split_moe(it + 1, c, it * (2 * MGC) + (2 * MGC + 2 * c + 2))

            run_steps(pool, step3, NE + 2, PER3, 2, 4)

        @block.scalar
        def _(act):
            roots = [0]

            def take_root():
                roots[0] += 1
                act.wait_ge(root_in, roots[0])
                act.activation(sm[:, 5, :], sm[:, 3, :], ACT.Sqrt).then_inc(root, 1)

            take_root()
            act.wait_ge(sel_in, 16)
            act.activation(sel[:, :], sel_raw[:, :], ACT.Copy).then_inc(sel_ok, 1)
            act.wait_ge(gate_in, 16)
            act.activation(gate_hl[:, HI, :, :], gate_raw[:, :, :], ACT.Copy).then_inc(gate_ok, 1)
            def project(b):
                for c in range(C):
                    act.wait_ge(ph1_tp, b * C + (c + 1))
                    if later(b):
                        act.wait_ge(ph1_mm, b * 6)
                    act.activation(xT1[:, c, :], bank[c][:, :], ACT.Copy).then_inc(ph1_xT, 1)
                for m in range(4):
                    dst, scale = (q1_hl, SCALE1) if m < 2 else (k1_hl, 1.0)
                    act.wait_ge(ph1_mm, b * 6 + (m + 1))
                    act.activation(dst[:, b * 2 + m % 2, HI, :], bank[2 + m][:, :], ACT.Copy, scale=scale)\
                       .then_inc(ph1_hi, 1)
                for i in range(2):
                    act.wait_ge(ph1_mm, b * 6 + (5 + i))
                    for c in range(C):
                        ins = act.activation(
                            v1[:, b * 2 + c, 2 * i:2 * i + 2, :],
                            bank[6 + i][:, :].rearrange("p (j c n) -> p c j n", j=2, c=C)[:, c], ACT.Copy)
                    ins.then_inc(ph1_v, 1)
            first_then_loop(act, project, B)
            meet(act, 0)

            def take_stack(m_par, count):
                for w in range(2):
                    act.wait_ge(a1_sel, count + w + 1)
                    act.activation(stk[:, m_par, w, :], bank[4 + w][:, :], ACT.Copy).then_inc(a1_stk, 1)

            def step1(it, k):
                n = it * GH + k
                static = isinstance(n, int)
                if static and n == 0:
                    take_stack(0, 0)
                def exp(t):
                    qi = TPB - 1 - t
                    act.wait_ge(a1_max, n * TPB + (t + 1))
                    if t == 0 and (not static or n >= 2):
                        act.wait_ge(a1_t, (n - 1) * TPB)
                    act.activation(p1[:, k % 2, POFF[qi]:POFF[qi + 1]], bank[t % 2][:, 0:P * (qi + 1)], ACT.Exp,
                                   bias=stat1[:, 0, k % 2, t:t + 1],
                                   accum_out=stat1[:, 1, k % 2, t:t + 1]).then_inc(a1_exp, 1)

                def take_pt(t):
                    kj = TPB - 1 - t
                    act.wait_ge(a1_t, n * TPB + (t + 1 - TPB))
                    if not static or n >= 2:
                        act.wait_ge(a1_pv, n * TPB + (t + 1 - 2 * TPB))
                    act.activation(pT1[:, QOFF[kj]:QOFF[kj + 1]], bank[2 + t % 2][:, 0:TB - P * kj], ACT.Copy)\
                       .then_inc(a1_pta, 1)

                softmax, values = not static or n < N1, not static or n >= 1
                if softmax:
                    exp(0)
                    exp(1)
                if values:
                    take_pt(1)
                if softmax:
                    exp(2)
                    exp(3)
                if values:
                    take_pt(3)
                if k % 2 == 0 and (not static or n // 2 + 1 < N1 // 2):
                    if not static or n >= 2:
                        act.wait_ge(a1_s, n * TPB)
                    take_stack((k // 2 + 1) % 2, n + 2)

            run_steps(act, step1, N1 + 1, GH, 2, 5)
            meet(act, 1)
            for g in range(T // 2):
                act.wait_ge(m_y, g + 1)
                act.activation(y_sb[:, 2 * g:2 * g + 2, :].rearrange("p j d -> p (j d)"), bank[g][:, :], ACT.Copy)\
                   .then_inc(m_ys, 1)
            take_root()
            take_root()
            take_root()
            act.wait_ge(small_in, 16)
            for b in range(B):
                for c in range(C):
                    act.wait_ge(m_tp, b * C + c + 1)
                    act.activation(xT[:, HI, c, TB * b:TB * (b + 1)], bank[b * C + c][:, :], ACT.Copy,
                                   scale=ln_w[:, 0, c:c + 1]).then_inc(m_hi, 1)
            meet(act, 2)

            def step2(it, k):
                n = it * B + k
                static = isinstance(n, int)
                par = (k - 1) % 2
                if not static or n < N2:
                    for i in range(3):
                        act.wait_ge(b_qkv, n * 3 + (i + 1))
                        if i == 0 and (not static or n >= 1):
                            act.wait_ge(b_s, n * TPB)
                        if i == 2 and (not static or n >= 2):
                            act.wait_ge(b_pv, (n - 1) * TPB)
                        dst = v2[:, k % 2, HI, :] if i == 2 else qk2[:, i, HI, :]
                        act.activation(dst, bank[4 + i][:, :], ACT.Copy, scale=(SCALE2 if i == 0 else 1.0))\
                           .then_inc(b_hi, 1)
                for t in range(TPB):
                    if not static or 1 <= n <= N2:
                        kj = TPB - 1 - t
                        act.wait_ge(b_t, n * TPB + (t + 1 - TPB))
                        if not static or n >= 2:
                            act.wait_ge(b_pv, n * TPB + (t + 1 - 2 * TPB))
                        act.activation(pT2[:, HI, QOFF[kj]:QOFF[kj + 1]], bank[2 + t % 2][:, 0:TB - P * kj],
                                       ACT.Copy).then_inc(b_pth, 1)
                if not static or n < N2:
                    for t in range(TPB):
                        qi = TPB - 1 - t
                        act.wait_ge(b_max, n * TPB + (t + 1))
                        if t == 0 and (not static or n >= 2):
                            act.wait_ge(b_t, (n - 1) * TPB)
                        act.activation(p2[:, k % 2, POFF[qi]:POFF[qi + 1]], bank[t % 2][:, 0:P * (qi + 1)],
                                       ACT.Exp, bias=stat2[:, 0, k % 2, t:t + 1],
                                       accum_out=stat2[:, 1, k % 2, t:t + 1]).then_inc(b_exp, 1)
                if not static or 1 <= n <= N2:
                    act.wait_ge(b_pv, n * TPB)
                    if not static or n >= 2:
                        act.wait_ge(b_e, (n - 1) * C)
                    act.activation(o2[:, HI, :], bank[7][:, :], ACT.Copy).then_inc(b_oh, 1)

            run_steps(act, step2, N2 + 2, B, 2, 4)
            meet(act, 3)
            take_root()
            for b in range(B):
                for c in range(C):
                    act.wait_ge(r_tp2, b * C + c + 1)
                    act.activation(xT[:, HI, c, TB * b:TB * (b + 1)], bank[b * C + c][:, :], ACT.Copy,
                                   scale=ln_w[:, 1, c:c + 1]).then_inc(r_hi, 1)
            act.wait_ge(r_sub, 1)
            act.activation(pr[:, :, :], lg[:, :, :], ACT.Exp).then_inc(r_exp, 1)
            act.wait_ge(r_zero, 1)
            for b in range(B):
                act.wait_ge(r_tp3, b + 1)
                act.activation(wT[0:E + 2, TB * b:TB * (b + 1)], bank[1 + b][0:E + 2, :], ACT.Copy)\
                   .then_inc(r_wh, 1)

            def step3(it, k):
                n = it * PER3 + k
                static = isinstance(n, int)
                if static and n >= NE:
                    return
                act.wait_ge(e_g, n + 1)
                act.activation(h_s[:, k % 2, :], bank[k % 2][:, :], ACT.Silu).then_inc(e_silu, 1)
                act.wait_ge(e_h, n + 1)
                if not static or n >= 2:
                    act.wait_ge(e_dn, (n - 1) * C)
                act.activation(h_hl[:, k % 2, HI, :], h_t[:, k % 2, :], ACT.Copy).then_inc(e_hh, 1)

            run_steps(act, step3, NE, PER3, 2, 2)
            take_root()

        @block.vector
        def _(dve):
            links = [0]

            def link(*instructions):
                for ins in instructions:
                    ins.then_inc(chain, 1)
                links[0] += len(instructions)
                dve.wait_ge(chain, links[0])

            roots = [0]
            mean, rstd, dif, var, tmp, rt, sq = (sm[:, i, :] for i in (0, 1, 2, 3, 4, 5, 6))

            def row_stats(eps, square_mean=False):
                link(dve.tensor_tensor(mean, st6[:, :, 1], st6[:, :, 4], ALU.add),
                     dve.tensor_tensor(dif, st6[:, :, 1], st6[:, :, 4], ALU.subtract),
                     dve.tensor_tensor(var, st6[:, :, 2], st6[:, :, 5], ALU.add))
                link(dve.tensor_tensor(dif, dif, dif, ALU.mult),
                     dve.tensor_scalar(mean, mean, 0.5, None, ALU.mult))
                link(dve.scalar_tensor_tensor(var, dif, D / 4.0, var, ALU.mult, ALU.add),
                     dve.tensor_tensor(sq, mean, mean, ALU.mult))
                if square_mean:
                    link(dve.tensor_scalar(var, var, 1.0 / D, eps, ALU.mult, ALU.add))
                    dve.tensor_tensor(var, var, sq, ALU.add).then_inc(root_in, 1)
                else:
                    dve.tensor_scalar(var, var, 1.0 / D, eps, ALU.mult, ALU.add).then_inc(root_in, 1)
                roots[0] += 1
                dve.wait_ge(root, roots[0])
                link(dve.reciprocal(rstd, rt))
                link(dve.tensor_tensor(tmp, rstd, rstd, ALU.mult))
                link(dve.tensor_tensor(tmp, tmp, var, ALU.mult))
                link(dve.tensor_scalar(tmp, tmp, -0.5, 1.5, ALU.mult, ALU.add))
                link(dve.tensor_tensor(rstd, rstd, tmp, ALU.mult))

            def tile_stats(src):
                link(*[dve.bn_stats(st6[:, i, :], src[:, i, :]) for i in range(T)])

            for b in range(B):
                dve.wait_ge(x_in[b], 16)
                link(*[dve.bn_stats(st6[:, i, :], x_sb[:, i, :]) for i in range(TPB * b, TPB * (b + 1))])
            row_stats(LN_EPS)
            dve.wait_ge(gate_ok, 1)
            dve.tensor_tensor(gate_hl[:, LO, :, :], gate_raw[:, :, :], f32(gate_hl[:, HI, :, :]), ALU.subtract)\
               .then_inc(gate_lo, 1)
            def project(b):
                if later(b):
                    dve.wait_ge(ph1_tp, b * C)
                for j in range(TPB):
                    dve.tensor_scalar(xn1[:, j, :], x_sb[:, b * TPB + j, :], sm[:, 0, ds(b * TPB + j, 1)],
                                      sm[:, 1, ds(b * TPB + j, 1)], ALU.subtract, ALU.mult).then_inc(ph1_xn, 1)
                for m in range(4):
                    dst, scale = (q1_hl, SCALE1) if m < 2 else (k1_hl, 1.0)
                    dve.wait_ge(ph1_hi, b * 4 + (m + 1))
                    dve.scalar_tensor_tensor(dst[:, b * 2 + m % 2, LO, :], bank[2 + m][:, :], scale,
                                             f32(dst[:, b * 2 + m % 2, HI, :]), ALU.mult, ALU.subtract)\
                       .then_inc(ph1_lo, 1)
            first_then_loop(dve, project, B)
            meet(dve, 0)

            def step1(it, k):
                n = it * GH + k
                static = isinstance(n, int)
                softmax, values = not static or n < N1, not static or n >= 1

                def row_max(t):
                    qi = TPB - 1 - t
                    dve.wait_ge(a1_s, n * TPB + (t + 1))
                    dve.tensor_reduce(stat1[:, 0, k % 2, t:t + 1], bank[t % 2][:, 0:P * (qi + 1)], AX.X, ALU.max,
                                      negate=True).then_inc(a1_max, 1)

                def take_pt(t):
                    kj = TPB - 1 - t
                    dve.wait_ge(a1_t, n * TPB + (t + 1 - TPB))
                    if not static or n >= 2:
                        dve.wait_ge(a1_pv, n * TPB + (t + 1 - 2 * TPB))
                    dve.tensor_copy(pT1[:, QOFF[kj]:QOFF[kj + 1]], bank[2 + t % 2][:, 0:TB - P * kj])\
                       .then_inc(a1_ptd, 1)

                if softmax:
                    row_max(0)
                    row_max(1)
                if values:
                    take_pt(0)
                if softmax:
                    row_max(2)
                    row_max(3)
                if values:
                    take_pt(2)
                if softmax:
                    dve.wait_ge(a1_exp, n * TPB + TPB)
                    dve.reciprocal(stat1[:, 2, k % 2, :], stat1[:, 1, k % 2, :]).then_inc(a1_rcp, 1)
                if k % GH == 0 and (not static or n >= 1):
                    dve.wait_ge(a1_pv, n * TPB)
                    dve.tensor_copy(oT1[:, it + (k // GH - 1), :], bank[6][:, :]).then_inc(a1_o, 1)

            run_steps(dve, step1, N1 + 1, GH, 2, 5)
            meet(dve, 1)
            for g in range(T // 2):
                dve.wait_ge(m_ys, g + 1)
                link(*[dve.bn_stats(st6[:, i, :], y_sb[:, i, :]) for i in (2 * g, 2 * g + 1)])
            row_stats(LN_EPS)
            link(*[dve.tensor_scalar(u_sb[:, i, :], y_sb[:, i, :], mean[:, i:i + 1], rstd[:, i:i + 1],
                                     ALU.subtract, ALU.mult) for i in range(T)])
            link(*[dve.tensor_tensor(x_sb[:, i:i + TPB, :], x_sb[:, i:i + TPB, :], u_sb[:, i:i + TPB, :], ALU.add)
                   for i in range(0, T, TPB)])
            tile_stats(x_sb)
            row_stats(LN_EPS)
            link(*[dve.tensor_scalar(hs[:, i, :], x_sb[:, i, :], mean[:, i:i + 1], rstd[:, i:i + 1],
                                     ALU.subtract, ALU.mult) for i in range(T)])
            tile_stats(hs)
            row_stats(RMS_EPS, square_mean=True)
            for i in range(T):
                dve.tensor_scalar(y_sb[:, i, :], hs[:, i, :], rstd[:, i:i + 1], None, ALU.mult).then_inc(m_xn, 1)
            dve.wait_ge(small_in, 16)
            for b in range(B):
                for c in range(C):
                    dve.wait_ge(m_hi, b * C + c + 1)
                    cols = slice(TB * b, TB * (b + 1))
                    dve.scalar_tensor_tensor(xT[:, LO, c, cols], bank[b * C + c][:, :], ln_w[:, 0, c:c + 1],
                                             f32(xT[:, HI, c, cols]), ALU.mult, ALU.subtract).then_inc(m_lo, 1)
            meet(dve, 2)

            def step2(it, k):
                n = it * B + k
                static = isinstance(n, int)
                values = not static or 1 <= n <= N2

                def take_pt(t):
                    kj = TPB - 1 - t
                    dve.wait_ge(b_pth, n * TPB + (t + 1 - TPB))
                    dve.tensor_tensor(pT2[:, LO, QOFF[kj]:QOFF[kj + 1]], bank[2 + t % 2][:, 0:TB - P * kj],
                                      f32(pT2[:, HI, QOFF[kj]:QOFF[kj + 1]]), ALU.subtract).then_inc(b_ptl, 1)

                if not static or n < N2:
                    for i in range(3):
                        dve.wait_ge(b_hi, n * 3 + (i + 1))
                        dst = v2[:, k % 2] if i == 2 else qk2[:, i]
                        dve.scalar_tensor_tensor(dst[:, LO, :], bank[4 + i][:, :], SCALE2 if i == 0 else 1.0,
                                                 f32(dst[:, HI, :]), ALU.mult, ALU.subtract).then_inc(b_lo, 1)
                if values:
                    take_pt(0)
                    take_pt(1)
                if not static or n >= 2:
                    b = (k - 2) % B
                    for c in range(C):
                        dve.wait_ge(b_e, n * C + (c + 1 - 2 * C))
                        if static and n == 2 and c == 0:
                            dve.wait_ge(b_acc0, 1)
                        cols = slice(TB * b, TB * (b + 1))
                        dve.tensor_tensor(acc[:, c, cols], acc[:, c, cols], bank[4 + c][:, :], ALU.add)\
                           .then_inc(b_acc, 1)
                if values:
                    take_pt(2)
                    take_pt(3)
                if not static or n < N2:
                    for t in range(TPB):
                        qi = TPB - 1 - t
                        dve.wait_ge(b_s, n * TPB + (t + 1))
                        dve.tensor_reduce(stat2[:, 0, k % 2, t:t + 1], bank[t % 2][:, 0:P * (qi + 1)], AX.X,
                                          ALU.max, negate=True).then_inc(b_max, 1)
                    dve.wait_ge(b_exp, n * TPB + TPB)
                    dve.reciprocal(stat2[:, 2, k % 2, :], stat2[:, 1, k % 2, :]).then_inc(b_rcp, 1)
                if values:
                    dve.wait_ge(b_oh, n * 1)
                    dve.tensor_tensor(o2[:, LO, :], bank[7][:, :], f32(o2[:, HI, :]), ALU.subtract)\
                       .then_inc(b_ol, 1)

            run_steps(dve, step2, N2 + 2, B, 3, 4)
            meet(dve, 3)
            for g in range(T // 2):
                dve.wait_ge(r_tp, g + 1)
                two = hs[:, 2 * g:2 * g + 2, :].rearrange("p j d -> p (j d)")
                dve.tensor_tensor(two, two, bank[g][:, :], ALU.add).then_inc(r_hid, 1)
            dve.wait_ge(r_hid, T // 2)
            tile_stats(hs)
            row_stats(RMS_EPS, square_mean=True)
            for i in range(T):
                dve.tensor_scalar(xn2[:, i, :], hs[:, i, :], rstd[:, i:i + 1], None, ALU.mult).then_inc(r_xn, 1)
            for b in range(B):
                for c in range(C):
                    dve.wait_ge(r_hi, b * C + c + 1)
                    cols = slice(TB * b, TB * (b + 1))
                    dve.scalar_tensor_tensor(xT[:, LO, c, cols], bank[b * C + c][:, :], ln_w[:, 1, c:c + 1],
                                             f32(xT[:, HI, c, cols]), ALU.mult, ALU.subtract).then_inc(r_lo, 1)
            logits = bank[0][:, 0:T * E].rearrange("p (t e) -> p t e", t=T)
            col = sm[:, 7, :]

            def wide(ap):
                return ap.unsqueeze(2).to_broadcast([P, T, E])

            dve.wait_ge(r_lg, 1)
            link(dve.tensor_reduce(col, logits, AX.X, ALU.max))
            dve.tensor_tensor(lg[:, :, :], logits, wide(col), ALU.subtract).then_inc(r_sub, 1)
            dve.wait_ge(r_exp, 1)
            link(dve.tensor_reduce(col, pr[:, :, :], AX.X, ALU.add))
            link(dve.reciprocal(col, col))
            link(dve.tensor_tensor(pr[:, :, :], pr[:, :, :], wide(col), ALU.mult))
            ranks = []
            for e in range(E):
                own = pr[:, :, e:e + 1]
                if e:
                    ranks.append(dve.tensor_tensor(rk[:, :, e, 0:e], pr[:, :, 0:e],
                                                   own.to_broadcast([P, T, e]), ALU.is_ge))
                ranks.append(dve.tensor_tensor(rk[:, :, e, e:E], pr[:, :, e:E],
                                               own.to_broadcast([P, T, E - e]), ALU.is_gt))
            link(*ranks)
            link(dve.tensor_reduce(lg[:, :, :], rk[:, :, :, :], AX.X, ALU.add))
            link(dve.tensor_scalar(lg[:, :, :], lg[:, :, :], float(TOPK), None, ALU.is_lt))
            link(dve.tensor_tensor(pr[:, :, :], pr[:, :, :], lg[:, :, :], ALU.mult))
            link(dve.tensor_reduce(col, pr[:, :, :], AX.X, ALU.add))
            link(dve.reciprocal(col, col))
            dve.memset(wtok[:, :, E:E + 2], 1.0).then_inc(r_w, 1)
            dve.tensor_tensor(wtok[:, :, 0:E], pr[:, :, :], wide(col), ALU.mult).then_inc(r_w, 1)
            for b in range(B):
                dve.wait_ge(r_wh, b + 1)
                cols = slice(TB * b, TB * (b + 1))
                dve.tensor_tensor(wT[32:32 + E + 2, cols], bank[1 + b][0:E + 2, :], f32(wT[0:E + 2, cols]),
                                  ALU.subtract).then_inc(r_wl, 1)
            dve.wait_ge(r_zero, 2)

            def step3(it, k):
                n = it * PER3 + k
                static = isinstance(n, int)
                par = k % 2
                if not static or n < NE:
                    dve.wait_ge(e_silu, n + 1)
                    dve.wait_ge(e_w, n + 1)
                    if not static or n >= 2:
                        dve.wait_ge(e_hlo, n - 1)
                    dve.tensor_tensor(h_t[:, par, :], h_s[:, par, :], bank[4][:, :], ALU.mult).then_inc(e_sw, 1)
                    dve.wait_ge(e_u, n + 1)
                    dve.wait_ge(e_sw, n + 1)
                    dve.tensor_tensor(h_t[:, par, :], h_t[:, par, :], bank[2 + par][:, :], ALU.mult)\
                       .then_inc(e_h, 1)
                if k % MGC == 0 and (not static or n > 0):
                    b = (k // MGC - 1) % B
                    for c in range(C):
                        dve.wait_ge(e_dn, n * C - (C - 1 - c))
                        cols = slice(TB * b, TB * (b + 1))
                        dve.tensor_tensor(acc[:, c, cols], acc[:, c, cols], bank[6 + c][:, :], ALU.add)\
                           .then_inc(e_acc, 1)

            run_steps(dve, step3, NE + 1, PER3, 2, 3)
            for g in range(T // 2):
                dve.wait_ge(f_tp, g + 1)
                two = hs[:, 2 * g:2 * g + 2, :].rearrange("p j d -> p (j d)")
                dve.tensor_tensor(two, two, bank[g][:, :], ALU.add).then_inc(f_y, 1)
            dve.wait_ge(f_y, T // 2)
            tile_stats(hs)
            row_stats(LN_EPS)
            link(*[dve.tensor_scalar(u_out[:, i, :], hs[:, i, :], mean[:, i:i + 1], rstd[:, i:i + 1],
                                     ALU.subtract, ALU.mult) for i in range(T)])
            for i in range(0, T, TPB):
                dve.tensor_tensor(u_out[:, i:i + TPB, :], u_out[:, i:i + TPB, :], x_sb[:, i:i + TPB, :], ALU.add)\
                   .then_inc(f_out, 1)

        @block.tensor
        def _(pe):
            def product(out, pairs, start=True, stop=True, **kw):
                for i, (a, b) in enumerate(pairs):
                    ins = pe.matmul(out, a, b, start=start and i == 0, stop=stop and i == len(pairs) - 1, **kw)
                return ins

            def mask_diagonal(t, qi):
                pe.matmul(bank[t % 2][:, P * qi:P * (qi + 1)], ident_b[:, :], mask_b[:, :], start=True, stop=False,
                          skip_group_check=True)

            pe.wait_ge(const, 6)
            pe.wait_ge(w1_in, 16)
            def project(b):
                pe.wait_ge(ph1_xn, b * TPB + TPB)
                if later(b):
                    pe.wait_ge(ph1_xT, b * C)
                for c in range(C):
                    for j in range(TPB):
                        ins = pe.transpose(bank[c][:, P * j:P * (j + 1)], xn1[:, j, P * c:P * (c + 1)], ident[:, :])
                    ins.then_inc(ph1_tp, 1)
                pe.wait_ge(ph1_xT, b * C + C)
                if later(b):
                    pe.wait_ge(ph1_lo, b * 4)
                for m in range(4):
                    product(bank[2 + m][:, :], [(qkv1[:, c, P * m:P * (m + 1)], xT1[:, c, :]) for c in range(C)])\
                        .then_inc(ph1_mm, 1)
                if later(b):
                    pe.wait_ge(ph1_v, b * 2)
                for i in range(2):
                    for j in (0, 1):
                        rows = slice(P * (2 * i + j), P * (2 * i + j + 1))
                        ins = product(bank[6 + i][:, D * j:D * (j + 1)],
                                      [(xT1[:, c, rows], qkv1[:, c, 2 * D:3 * D]) for c in range(C)])
                    ins.then_inc(ph1_mm, 1)

            first_then_loop(pe, project, B)
            pe.wait_ge(sel_ok, 1)
            meet(pe, 0)

            def stack(g, pair):
                for w, src in enumerate((q1_hl, k1_hl)):
                    product(bank[4 + w][:, :],
                            [(sel[:, P * (4 * pair + 2 * w + a):P * (4 * pair + 2 * w + a + 1)], src[:, g, a, :])
                             for a in (HI, LO)]).then_inc(a1_sel, 1)

            def step1(it, k):
                n = it * GH + k
                static = isinstance(n, int)
                softmax, values = not static or n < N1, not static or n >= 1
                head, prev = k % GH, (k - 1) % GH
                if static and n == 0:
                    stack(0, 0)

                def scores(t):
                    qi = TPB - 1 - t
                    rows = slice(64 * (k % 2), 64 * (k % 2) + 64)
                    if t == 0:
                        pe.wait_ge(a1_stk, n + (2 - k % 2))
                    if not static or n * TPB + t >= 2:
                        pe.wait_ge(a1_exp, n * TPB + (t - 1))
                    m = (k // 2) % 2
                    mask_diagonal(t, qi)
                    pe.matmul(bank[t % 2][:, 0:P * (qi + 1)], stk[rows, m, 0, P * qi:P * (qi + 1)],
                              stk[rows, m, 1, 0:P * (qi + 1)], start=False, stop=True, skip_group_check=True)\
                        .then_inc(a1_s, 1)

                def turn(t):
                    kj = TPB - 1 - t
                    pe.wait_ge(a1_norm, n * TPB + (t + 1 - TPB))
                    if not static or n >= 2 or t >= 2:
                        taken = a1_pta if t % 2 else a1_ptd
                        pe.wait_ge(taken, n * 2 + (t // 2 - 2))
                    for qi in range(kj, TPB):
                        ins = pe.transpose(bank[2 + t % 2][:, P * (qi - kj):P * (qi - kj + 1)],
                                           p1[:, (k - 1) % 2, POFF[qi] + P * kj:POFF[qi] + P * (kj + 1)],
                                           ident[:, :])
                    ins.then_inc(a1_t, 1)

                def values_of(t):
                    kj = TPB - 1 - t
                    pe.wait_ge(a1_pta if t % 2 else a1_ptd, n * 2 + (t // 2 - 1))
                    if t == 0:
                        pe.wait_ge(a1_vpad, n * 1)
                        if prev == 0 and (not static or n > GH):
                            pe.wait_ge(a1_o, it + (k - 1) // GH)
                    pe.matmul(bank[6][:, P * kj:TB], v1_pad[:, kj, prev, :], pT1[:, QOFF[kj]:QOFF[kj + 1]],
                              start=(prev == 0 and t == 0), stop=(prev == GH - 1 and t == TPB - 1),
                              skip_group_check=True).then_inc(a1_pv, 1)

                if softmax:
                    scores(0)
                    scores(1)
                if values:
                    turn(0)
                    turn(1)
                if softmax:
                    scores(2)
                if values:
                    values_of(0)
                if softmax:
                    scores(3)
                if values:
                    turn(2)
                    values_of(1)
                    turn(3)
                    values_of(2)
                    values_of(3)
                if k % 2 == 0 and (not static or n // 2 + 1 < N1 // 2):
                    pe.wait_ge(a1_stk, n + 2)
                    stack(it + (k + 2) // GH, (k // 2 + 1) % PAIRS1)

            run_steps(pe, step1, N1 + 1, GH, 2, 5)
            meet(pe, 1)
            pe.wait_ge(wo1_in, 16)
            for g in range(T // 2):
                for r in range(2):
                    b, j = divmod(2 * g + r, TPB)
                    ins = product(bank[g][:, D * r:D * (r + 1)],
                                  [(oT1[:, 2 * b + c, P * j:P * (j + 1)], wo1[:, c, :]) for c in range(C)])
                ins.then_inc(m_y, 1)

            def turn_all(src, ready, done):
                for b in range(B):
                    pe.wait_ge(ready, TPB * (b + 1))
                    for c in range(C):
                        for j in range(TPB):
                            ins = pe.transpose(bank[b * C + c][:, P * j:P * (j + 1)],
                                               src[:, TPB * b + j, P * c:P * (c + 1)], ident[:, :])
                        ins.then_inc(done, 1)

            def turn_acc(done):
                for g in range(T // 2):
                    for r in range(2):
                        for c in range(C):
                            i = 2 * g + r
                            ins = pe.transpose(bank[g][:, D * r + P * c:D * r + P * (c + 1)],
                                               acc[:, c, P * i:P * (i + 1)], ident[:, :])
                    ins.then_inc(done, 1)

            pe.wait_ge(m_ys, T // 2)
            turn_all(y_sb, m_xn, m_tp)
            meet(pe, 2)

            def step2(it, k):
                n = it * B + k
                static = isinstance(n, int)
                here = not static or n < N2
                prev = not static or 1 <= n <= N2
                b = k % B

                def turn(t):
                    kj = TPB - 1 - t
                    pe.wait_ge(b_norm, n * TPB + (t + 1 - TPB))
                    if not static or n >= 2 or t >= 2:
                        pe.wait_ge(b_ptl, n * TPB + (t - 1 - TPB))
                    for qi in range(kj, TPB):
                        ins = pe.transpose(bank[2 + t % 2][:, P * (qi - kj):P * (qi - kj + 1)],
                                           p2[:, (k - 1) % 2, POFF[qi] + P * kj:POFF[qi] + P * (kj + 1)],
                                           ident[:, :])
                    ins.then_inc(b_t, 1)

                def scores(t):
                    qi = TPB - 1 - t
                    if not static or n * TPB + t >= 2:
                        pe.wait_ge(b_exp, n * TPB + (t - 1))
                    mask_diagonal(t, qi)
                    product(bank[t % 2][:, 0:P * (qi + 1)],
                            [(qk2[:, 0, s, P * qi:P * (qi + 1)], qk2[:, 1, m, 0:P * (qi + 1)]) for s, m in PARTS],
                            start=False, skip_group_check=True).then_inc(b_s, 1)

                def values_of(t):
                    kj = TPB - 1 - t
                    pe.wait_ge(b_ptl, n * TPB + (t + 1 - TPB))
                    if t == 0 and (not static or n >= 2):
                        pe.wait_ge(b_ol, n - 1)
                    product(bank[7][:, P * kj:TB],
                            [(v2[:, (k - 1) % 2, s, P * kj:P * (kj + 1)], pT2[:, m, QOFF[kj]:QOFF[kj + 1]])
                             for s, m in PARTS], start=(t == 0), stop=(t == TPB - 1), skip_group_check=True)\
                        .then_inc(b_pv, 1)

                if here:
                    if b == 0:
                        pe.wait_ge(b_wqkv, it + (k // B + 1))
                    for i in range(2):
                        if not static or n >= 1:
                            pe.wait_ge(b_lo, n * 3 + (i - 2))
                        if not static or n >= 3:
                            pe.wait_ge(b_acc, n * C + (i + 1 - 3 * C))
                        product(bank[4 + i][:, :],
                                [(w2_hl[:, s, P * (C * i + c):P * (C * i + c + 1)], xT[:, m, c, TB * b:TB * (b + 1)])
                                 for c in range(C) for s, m in PARTS]).then_inc(b_qkv, 1)
                    if not static or n >= 1:
                        pe.wait_ge(b_lo, n * 3)
                    for j in range(TPB):
                        rows = slice(TB * b + P * j, TB * b + P * (j + 1))
                        ins = product(bank[6][:, P * j:P * (j + 1)],
                                      [(xT[:, s, c, rows], w2_hl[:, m, P * (2 * C + c):P * (2 * C + c + 1)])
                                       for c in range(C) for s, m in PARTS])
                    ins.then_inc(b_qkv, 1)
                if prev:
                    turn(0)
                    turn(1)
                if not static or n >= 2:
                    if b == 2:
                        pe.wait_ge(b_wo, it + ((k - 2) // B + 1))
                    pe.wait_ge(b_ol, n - 1)
                    for c in range(C):
                        pe.wait_ge(b_lo, n * 3 + (c + 1) if here else N2 * 3)
                        if not static or n >= 3:
                            pe.wait_ge(b_acc, n * C + (c + 1 - 3 * C))
                        product(bank[4 + c][:, :], [(wo2_hl[:, s, P * c:P * (c + 1)], o2[:, m, :]) for s, m in PARTS])\
                            .then_inc(b_e, 1)
                if prev:
                    turn(2)
                    turn(3)
                if here:
                    pe.wait_ge(b_lo, n * 3 + 2)
                    scores(0)
                    scores(1)
                if prev:
                    values_of(0)
                    values_of(1)
                if here:
                    scores(2)
                if prev:
                    values_of(2)
                if here:
                    scores(3)
                if prev:
                    values_of(3)

            run_steps(pe, step2, N2 + 2, B, 3, 4)
            meet(pe, 3)
            turn_acc(r_tp)
            pe.wait_ge(r_hid, T // 2)
            turn_all(xn2, r_xn, r_tp2)
            pe.wait_ge(r_lo, B * C)
            pe.wait_ge(gate_lo, 1)
            for i in range(T):
                ins = product(bank[0][:, E * i:E * (i + 1)],
                              [(xT[:, s, c, P * i:P * (i + 1)], gate_hl[:, m, c, :])
                               for c in range(C) for s, m in PARTS])
            ins.then_inc(r_lg, 1)
            pe.wait_ge(r_w, 2)
            for b in range(B):
                for j in range(TPB):
                    ins = pe.transpose(bank[1 + b][0:E + 2, P * j:P * (j + 1)], wtok[:, TPB * b + j, :], ident[:, :])
                ins.then_inc(r_tp3, 1)
            pe.wait_ge(r_wl, B)

            def step3(it, k):
                n = it * PER3 + k
                static = isinstance(n, int)
                b, c = k % PER3 // MGC, k % MGC
                cols = slice(TB * b, TB * (b + 1))

                def up(out, first):
                    return product(out, [(moe_hl[:, c, s, first + P * d:first + P * (d + 1)], xT[:, m, d, cols])
                                         for d in range(C) for s, m in PARTS])

                if not static or n < NE:
                    if b == 0:
                        pe.wait_ge(e_split, it * MGC + (MGC * (k // PER3) + c + 1))
                    if not static or n >= 2:
                        pe.wait_ge(e_silu, n - 1)
                    up(bank[k % 2][:, :], 0).then_inc(e_g, 1)
                    pe.wait_ge(e_sw, n * 1)
                    pe.matmul(bank[4][:, :], sel_c[:, c, :], wT[:, cols], start=True, stop=True).then_inc(e_w, 1)
                    if not static or n >= 2:
                        pe.wait_ge(e_h, n - 1)
                    up(bank[2 + k % 2][:, :], C * P).then_inc(e_u, 1)
                if not static or n >= 1:
                    cc = (k - 1) % MGC
                    pe.wait_ge(e_hlo, n * 1)
                    for d in range(C):
                        if cc == 0 and (not static or n > MGC):
                            pe.wait_ge(e_acc, it * (C * B) + (k - 1) // MGC * C)
                        product(bank[6 + d][:, :],
                                [(moe_hl[:, cc, s, 2 * C * P + P * d:2 * C * P + P * (d + 1)],
                                  h_hl[:, (k - 1) % 2, m, :]) for s, m in PARTS],
                                start=(cc == 0), stop=(cc == MGC - 1)).then_inc(e_dn, 1)

            run_steps(pe, step3, NE + 1, PER3, 2, 3)
            pe.wait_ge(e_acc, MG * B * C)
            turn_acc(f_tp)


def kernel(**inputs):
    import numpy as np
    import concourse.bacc as bacc
    from concourse.bass_utils import run_bass_kernel_spmd

    x = np.asarray(inputs["L0_attn_x"])
    D = x.shape[2]
    C = D // P

    def rows(w):
        w = np.asarray(w)
        return w.T.reshape(w.shape[1] // P, P, w.shape[0]).transpose(1, 0, 2)

    qkv1 = np.concatenate([rows(inputs[f"L0_attn_{n}"]) for n in ("Wq", "Wk", "Wv")], axis=2)
    wo1 = rows(inputs["L0_attn_Wo"])
    q_w, kv_w = rows(inputs["L0_ffn_q_w"]), rows(inputs["L0_ffn_kv_w"])
    H2 = 16
    q_w = q_w.reshape(P, C, H2, 192)[..., :P]
    k_w = kv_w[..., :H2 * P].reshape(P, C, H2, P)
    v_w = kv_w[..., H2 * P:2 * H2 * P].reshape(P, C, H2, P)
    o_w = rows(inputs["L0_ffn_o_w"]).transpose(1, 0, 2)
    heads = [a.transpose(2, 0, 1, 3).reshape(H2, P, C * P) for a in (q_w, k_w, v_w)]
    qkvo2 = np.concatenate(heads + [o_w], axis=2)
    ln_w = np.stack([np.asarray(inputs[f"L0_ffn_ln{i}_w"]).reshape(C, P).T for i in (1, 2)], axis=1)
    gate = rows(inputs["L0_ffn_gate_w"])

    w1, w2 = np.asarray(inputs["L0_ffn_w1"]), np.asarray(inputs["L0_ffn_w2"])
    sh1, sh2 = np.asarray(inputs["L0_ffn_sh_gu_w"]), np.asarray(inputs["L0_ffn_sh_down_w"])
    EI, SI = w1.shape[1] // 2, sh2.shape[1]
    MG, MGC = 5, 5
    pad = np.zeros((MG * MGC * P - w1.shape[0] * EI - SI, D), w1.dtype)
    g_w = rows(np.concatenate([w1[:, :EI].reshape(-1, D), sh1[:SI], pad]))
    u_w = rows(np.concatenate([w1[:, EI:].reshape(-1, D), sh1[SI:], pad]))
    d_w = np.concatenate([w2.transpose(0, 2, 1).reshape(-1, D), sh2.T, pad])
    chunks = [a.reshape(P, C, MG, MGC, P).transpose(2, 0, 3, 1, 4).reshape(MG, P, MGC, C * P) for a in (g_w, u_w)]
    moe = np.concatenate(chunks + [d_w.reshape(MG, MGC, P, D).transpose(0, 2, 1, 3)], axis=3)

    stack = np.zeros((P, 4, 2, 2, P), np.float32)
    for pair in range(4):
        for half in range(2):
            for w, parts in enumerate((((0, 1), (2, 3)), ((0, 2), (1, 3)))):
                for a in range(2):
                    for part in parts[a]:
                        for d in range(16):
                            stack[32 * pair + 16 * half + d, pair, w, a, 64 * half + 16 * part + d] = 1.0
    arrays = {"x": x, "qkv1": qkv1, "wo1": wo1, "qkvo2": qkvo2, "ln_w": ln_w, "gate": gate, "moe": moe,
              "stack": stack.reshape(P, -1)}
    arrays = {f"in_{n}": np.ascontiguousarray(a) for n, a in arrays.items()}
    nc = bacc.Bacc("TRN2", target_bir_lowering=False, num_devices=1)
    args = [nc.dram_tensor(n, a.shape, mybir.dt.from_np(a.dtype), kind="ExternalInput").ap()
            for n, a in arrays.items()]
    out = nc.dram_tensor("out_0", x.shape, F32, kind="ExternalOutput").ap()
    sandwich_kernel(nc, *args, out)
    return run_bass_kernel_spmd(nc, [arrays], core_ids=[0]).results[0]["out_0"]
```

```python
from contextlib import ExitStack

import concourse.bass as bass
from concourse import mybir

F32 = mybir.dt.float32
F32R = mybir.dt.float32r
BF16 = mybir.dt.bfloat16
ALU = mybir.AluOpType
ACT = mybir.ActivationFunctionType
AX = mybir.AxisListType
ds = bass.ds

P = 128
HI, LO = 0, 1
PARTS = ((HI, HI), (LO, HI), (HI, LO))
MASKED = -1e30
LN_EPS = 1e-5
RMS_EPS = 1e-6


def run_steps(eng, step, total, period, first, ahead):
    loops = (total - first - ahead) // period
    for k in range(first):
        step(0, k)
    with eng.Fori(0, loops) as it:
        for k in range(first, first + period):
            step(it, k)
    for k in range(first, total - loops * period):
        step(loops, k)


def first_then_loop(eng, step, total):
    step(0)
    with eng.Fori(1, total) as i:
        step(i)


def later(i):
    return not isinstance(i, int) or i > 0


def sandwich_kernel(nc, x_d, qkv1_d, wo1_d, qkvo2_d, ln_w_d, gate_d, moe_d, stack_d, out_d):
    B, TB, D = x_d.shape
    C = D // P
    T = B * TB // P
    TPB = TB // P
    H1, H2 = 16, 2 * qkvo2_d.shape[0]
    DH1 = D // H1
    GH = P // DH1
    G1 = B * H1 // GH
    E = gate_d.shape[2]
    EI = 176
    MG, _, MGC, _ = moe_d.shape
    TOPK = 4
    SCALE1 = float(DH1) ** -0.5
    SCALE2 = 192.0 ** -0.5
    WQKV2 = 3 * C * P
    QOFF = [0]
    for kj in range(TPB):
        QOFF.append(QOFF[-1] + TB - P * kj)
    POFF = [P * qi * (qi + 1) // 2 for qi in range(TPB + 1)]
    CAUSAL = QOFF[TPB]

    ctx = ExitStack()
    with ctx:
        def sb(stack, name, shape, dt=F32):
            return stack.enter_context(nc.sbuf_tensor(name, shape, dt))

        def sem(name):
            return ctx.enter_context(nc.semaphore(name))

        bank = [ctx.enter_context(nc.psum_tensor(f"bank{i}", [P, 512], F32)) for i in range(8)]

        x_sb = sb(ctx, "x_sb", [P, T, D])
        hs = sb(ctx, "hs", [P, T, D])
        acc = sb(ctx, "acc", [P, C, B * TB])
        xT = sb(ctx, "xT", [P, 2, C, B * TB], F32R)
        ident = sb(ctx, "ident", [P, P])
        ident_b = sb(ctx, "ident_b", [P, P], BF16)
        mask_f = sb(ctx, "mask_f", [P, P])
        mask_b = sb(ctx, "mask_b", [P, P], BF16)
        ln_w = sb(ctx, "ln_w", [P, 2, C])
        gate_raw = sb(ctx, "gate_raw", [P, C, E])
        gate_hl = sb(ctx, "gate_hl", [P, 2, C, E], F32R)
        wo1 = sb(ctx, "wo1", [P, C, D])
        raw_qkv = sb(ctx, "raw_qkv", [P, 2 * WQKV2])
        raw_o = sb(ctx, "raw_o", [P, 2 * D])
        raw_moe = sb(ctx, "raw_moe", [P, MGC, 3 * C * P])
        st6 = sb(ctx, "st6", [P, T, 6])
        sm = sb(ctx, "sm", [P, 12, T])
        v1 = hs[:, :, :].rearrange("p t d -> p (t d)").rearrange("p (g k n) -> p g k n", g=G1, k=TPB)
        oT1 = acc[:, :, :].rearrange("p c t -> p (c t)").rearrange("p (g t) -> p g t", g=G1)
        q1_hl = xT[:, :, :, :].rearrange("p a c t -> p (a c t)").rearrange("p (g a t) -> p g a t", g=G1, a=2)

        with ExitStack() as l1:
            k1_hl = sb(l1, "k1_hl", [P, G1, 2, TB], F32R)
            v1_pad = sb(l1, "v1_pad", [P, TPB, GH, P])
            p1 = sb(l1, "p1", [P, 2, CAUSAL])
            pT1 = sb(l1, "pT1", [P, CAUSAL])
            stk = sb(l1, "stk", [P, 2, 2, TB], F32R)
            sel_raw = sb(l1, "sel_raw", [P, 16 * P])
            sel = sb(l1, "sel", [P, 16 * P], F32R)
            xn1 = sb(l1, "xn1", [P, TPB, D])
            xT1 = sb(l1, "xT1", [P, C, TB])
            qkv1 = p1[:, :, :].rearrange("p a n -> p (a n)")[:, 0:C * 3 * D].rearrange("p (c n) -> p c n", c=C)
            stat1 = sb(l1, "stat1", [P, 3, 2, TPB])
        with ExitStack() as l12:
            y_sb = sb(l12, "y_sb", [P, T, D])
            u_sb = sb(l12, "u_sb", [P, T, D])
        with ExitStack() as l2:
            w2_hl = sb(l2, "w2_hl", [P, 2, 2 * WQKV2], F32R)
            wo2_hl = sb(l2, "wo2_hl", [P, 2, 2 * D], F32R)
            qk2 = sb(l2, "qk2", [P, 2, 2, TB], F32R)
            v2 = sb(l2, "v2", [P, 2, 2, TPB, 2 * P], F32R)
            p2 = sb(l2, "p2", [P, 2, CAUSAL])
            pT2 = sb(l2, "pT2", [P, 2, CAUSAL], F32R)
            o2 = sb(l2, "o2", [P, 2, TB], F32R)
            stat2 = sb(l2, "stat2", [P, 3, 2, TPB])
        with ExitStack() as l3:
            xn2 = sb(l3, "xn2", [P, T, D])
            moe_hl = sb(l3, "moe_hl", [P, MGC, 2, 3 * C * P], F32R)
            sel_c = sb(l3, "sel_c", [64, MGC, P], F32R)
            sel_f = sb(l3, "sel_f", [64, MG, MGC, P])
            wT = sb(l3, "wT", [64, B * TB], F32R)
            h_s = sb(l3, "h_s", [P, 2, TB])
            h_t = sb(l3, "h_t", [P, 2, TB])
            h_hl = sb(l3, "h_hl", [P, 2, 2, TB], F32R)
            lg = sb(l3, "lg", [P, T, E])
            pr = sb(l3, "pr", [P, T, E])
            rk = sb(l3, "rk", [P, T, E, E], BF16)
            wtok = sb(l3, "wtok", [P, T, E + 2])

        x_in = [sem(f"x_in{b}") for b in range(B)]
        w1_in = sem("w1_in"); wo1_in = sem("wo1_in"); sel_in = sem("sel_in"); small_in = sem("small_in")
        const = sem("const")
        chain = sem("chain")
        root_in = sem("root_in"); root = sem("root")
        sel_ok = sem("sel_ok")
        pool_met = sem("pool_met")
        ph1_xn = sem("ph1_xn"); ph1_tp = sem("ph1_tp"); ph1_xT = sem("ph1_xT"); ph1_mm = sem("ph1_mm")
        ph1_hi = sem("ph1_hi"); ph1_lo = sem("ph1_lo"); ph1_v = sem("ph1_v")
        a1_sel = sem("a1_sel"); a1_stk = sem("a1_stk"); a1_s = sem("a1_s"); a1_max = sem("a1_max")
        a1_exp = sem("a1_exp"); a1_rcp = sem("a1_rcp"); a1_norm = sem("a1_norm"); a1_t = sem("a1_t")
        a1_pta = sem("a1_pta"); a1_ptd = sem("a1_ptd"); a1_pv = sem("a1_pv"); a1_vpad = sem("a1_vpad")
        a1_zero = sem("a1_zero"); a1_o = sem("a1_o")
        m_y = sem("m_y"); m_ys = sem("m_ys"); m_u = sem("m_u"); m_nrm = sem("m_nrm"); m_x1 = sem("m_x1")
        m_hs = sem("m_hs"); m_xn = sem("m_xn"); m_tp = sem("m_tp"); m_hi = sem("m_hi"); m_lo = sem("m_lo")
        b_rawqkv = sem("b_rawqkv"); b_rawo = sem("b_rawo"); b_wqkv = sem("b_wqkv"); b_wo = sem("b_wo")
        b_qkv = sem("b_qkv"); b_hi = sem("b_hi"); b_lo = sem("b_lo"); b_s = sem("b_s"); b_max = sem("b_max")
        b_exp = sem("b_exp"); b_rcp = sem("b_rcp"); b_norm = sem("b_norm"); b_t = sem("b_t")
        b_pth = sem("b_pth"); b_ptl = sem("b_ptl"); b_pv = sem("b_pv"); b_oh = sem("b_oh"); b_ol = sem("b_ol")
        b_e = sem("b_e"); b_acc = sem("b_acc")
        r_tp = sem("r_tp"); r_hid = sem("r_hid"); r_xn = sem("r_xn"); r_tp2 = sem("r_tp2"); r_hi = sem("r_hi")
        r_lo = sem("r_lo"); r_lg = sem("r_lg"); r_sub = sem("r_sub"); r_exp = sem("r_exp"); r_w = sem("r_w")
        r_tp3 = sem("r_tp3"); r_wh = sem("r_wh"); r_wl = sem("r_wl"); r_gate = sem("r_gate")
        r_sel = sem("r_sel"); r_zero = sem("r_zero")
        e_raw = sem("e_raw"); e_split = sem("e_split"); e_g = sem("e_g"); e_w = sem("e_w"); e_u = sem("e_u")
        e_silu = sem("e_silu"); e_sw = sem("e_sw"); e_h = sem("e_h"); e_hh = sem("e_hh"); e_hlo = sem("e_hlo")
        e_dn = sem("e_dn"); e_acc = sem("e_acc")
        f_tp = sem("f_tp"); f_y = sem("f_y"); f_u = sem("f_u"); f_nrm = sem("f_nrm"); f_out = sem("f_out")
        stored = sem("stored")
        b_half = sem("b_half"); b_acc0 = sem("b_acc0"); e_half = sem("e_half"); e_sel = sem("e_sel"); gate_ok = sem("gate_ok"); gate_lo = sem("gate_lo"); gate_in = sem("gate_in")
        fence = [sem(f"fence{i}") for i in range(4)]

        def meet(eng, i):
            eng.drain().then_inc(fence[i], 1)
            eng.wait_ge(fence[i], 5)

        S1_BANK, S1_COL = (0, 1, 2, 2), (0, 0, 0, 2 * P)
        PT1_BANK, STK_BANK, O1_BANK = (3, 4), (5, 6), 7

        def s1(t):
            return bank[S1_BANK[t]][:, S1_COL[t]:S1_COL[t] + P * (TPB - t)]

        def s2(t):
            return bank[t][:, 0:P * (TPB - t)]

        def v2_half(k, part):
            j = 2 - 2 * (k % 2)
            return v2[:, k // 2 % 2, part, j:j + 2, :].rearrange("p j n -> p (j n)")

        def pool_wait(pool, sem_, value):
            pool.wait_ge(sem_, value)
            if not isinstance(value, int):
                pool.sem_inc(pool_met, 1)

        def f32(ap):
            return ap.bitcast(F32)

        block = ctx.enter_context(nc.Block())
        PAIRS1 = GH // 2
        N1 = G1 * GH
        PER2 = 2 * B
        N2 = H2 * B
        PER3 = B * MGC
        NE = MG * PER3
        u_out = xn2

        @block.sync
        def _(sp):
            for b in range(B):
                sp.dma_start(x_sb[:, TPB * b:TPB * (b + 1), :],
                             x_d[b].rearrange("(j p) d -> p j d", p=P)).then_inc(x_in[b], 16)
            sp.dma_start(qkv1, qkv1_d).then_inc(w1_in, 16)
            sp.dma_start(sel_raw[:, :], stack_d).then_inc(sel_in, 16)
            sp.dma_start(wo1[:, :, :], wo1_d).then_inc(wo1_in, 16)
            sp.dma_start(ln_w[:, :, :], ln_w_d).then_inc(small_in, 16)
            sp.dma_start(gate_raw[:, :, :], gate_d).then_inc(gate_in, 16)
            sp.dma_start(raw_qkv[:, :], qkvo2_d[0, :, 0:2 * WQKV2]).then_inc(b_rawqkv, 16)
            sp.dma_start(raw_o[:, :], qkvo2_d[0, :, 2 * WQKV2:]).then_inc(b_rawo, 16)
            sp.dma_start(raw_moe[:, :, :], moe_d[0]).then_inc(e_raw, 16)
            meet(sp, 0)
            meet(sp, 1)
            meet(sp, 2)
            with sp.Fori(1, H2 // 2) as h:
                sp.wait_ge(b_wqkv, h * 1)
                sp.dma_start(raw_qkv[:, :], qkvo2_d[ds(h, 1), :, 0:2 * WQKV2].rearrange("a p n -> p (a n)"))\
                    .then_inc(b_rawqkv, 16)
                sp.wait_ge(b_wo, h * 1)
                sp.dma_start(raw_o[:, :], qkvo2_d[ds(h, 1), :, 2 * WQKV2:].rearrange("a p n -> p (a n)"))\
                    .then_inc(b_rawo, 16)
            meet(sp, 3)
            with sp.Fori(1, MG) as g:
                sp.wait_ge(e_split, g * MGC)
                sp.dma_start(raw_moe[:, :, :], moe_d[ds(g, 1)].rearrange("a p c n -> p (a c) n"))\
                    .then_inc(e_raw, 16)
            for b in range(B):
                sp.wait_ge(f_out, b + 1)
                sp.dma_start(out_d[b].rearrange("(j p) d -> p j d", p=P),
                             u_out[:, TPB * b:TPB * (b + 1), :]).then_inc(stored, 16)
            sp.wait_ge(stored, 16 * B)

        @block.gpsimd
        def _(pool):
            pool.memset(ident[:, :], 0.0).then_inc(const, 1)
            pool.memset(mask_f[:, :], 0.0).then_inc(const, 1)
            pool.wait_ge(const, 2)
            pool.affine_select(out=ident[:, :], in_=ident[:, :], compare_op=ALU.not_equal, fill=1.0, base=0,
                               pattern=[[-1, P]], channel_multiplier=1).then_inc(const, 1)
            pool.affine_select(out=mask_f[:, :], in_=mask_f[:, :], compare_op=ALU.is_ge, fill=MASKED, base=0,
                               pattern=[[-1, P]], channel_multiplier=1).then_inc(const, 1)
            pool.wait_ge(const, 4)
            pool.tensor_copy(ident_b[:, :], ident[:, :]).then_inc(const, 1)
            pool.tensor_copy(mask_b[:, :], mask_f[:, :]).then_inc(const, 1)
            pool.memset(v1_pad[:, :, :, :], 0.0).then_inc(a1_zero, 1)
            pool.wait_ge(a1_zero, 1)
            meet(pool, 0)

            def fill_v(g, head):
                pool.tensor_copy(v1_pad[:, :, head, DH1 * head:DH1 * (head + 1)],
                                 v1[:, g, :, DH1 * head:DH1 * (head + 1)]).then_inc(a1_vpad, 1)

            for head in range(GH):
                fill_v(0, head)

            def step1(it, k):
                n = it * GH + k
                if isinstance(n, int) and n >= N1:
                    return
                if not isinstance(n, int) or (n >= 2 and n + GH - 2 < N1):
                    pool_wait(pool, a1_pv, (n - 1) * TPB)
                    fill_v(it + (k + GH - 2) // GH, (k - 2) % GH)

            run_steps(pool, step1, N1, GH, 2, GH - 2)
            meet(pool, 1)
            pool.wait_ge(m_y, T // 2)
            pool.memset(acc[:, :, :], 0.0).then_inc(b_acc0, 1)
            meet(pool, 2)

            def split2(raw, hl, count, done):
                pool.tensor_copy(hl[:, HI, :], raw[:, :]).then_inc(b_half, 1)
                pool_wait(pool, b_half, count)
                pool.tensor_tensor(hl[:, LO, :], raw[:, :], f32(hl[:, HI, :]), ALU.subtract).then_inc(done, 1)

            pool_wait(pool, b_rawqkv, 16)
            split2(raw_qkv, w2_hl, 1, b_wqkv)
            pool_wait(pool, b_rawo, 16)
            split2(raw_o, wo2_hl, 2, b_wo)

            def step2(it, k):
                n = it * PER2 + k
                static = isinstance(n, int)
                if static and n >= N2 + 2:
                    return
                if k % PER2 == PER2 - 1 and (not static or n + 1 < N2):
                    pair = it + (k + 1) // PER2
                    pool_wait(pool, b_rawqkv, pair * 16 + 16)
                    pool_wait(pool, b_qkv, n * 3 + 3)
                    split2(raw_qkv, w2_hl, pair * 2 + 1, b_wqkv)
                if k % PER2 == 1 and (not static or PER2 < n < N2):
                    pair = it + k // PER2
                    pool_wait(pool, b_rawo, pair * 16 + 16)
                    pool_wait(pool, b_e, (n - 1) * C)
                    split2(raw_o, wo2_hl, pair * 2 + 2, b_wo)

            run_steps(pool, step2, N2, PER2, 2, 2)
            meet(pool, 3)

            pool.memset(sel_f[:, :, :, :], 1.0).then_inc(r_sel, 1)
            pool.memset(f32(wT[:, :]), 0.0).then_inc(r_zero, 1)
            pool.wait_ge(r_sel, 1)
            cnt = 1
            for half in range(2):
                part = sel_f[32 * half:32 * half + 32, :, :, :].rearrange("p g c n -> p (g c n)")
                width = MG * MGC * P
                for base, sign in ((0, 1), (EI - 1, -1)):
                    pool.affine_select(out=part, in_=part, compare_op=ALU.is_ge, fill=0.0, base=base,
                                       pattern=[[sign, width]], channel_multiplier=-sign * EI).then_inc(r_sel, 1)
                    cnt += 1
                    pool.wait_ge(r_sel, cnt)

            def split_moe(g, c, count):
                pool.tensor_copy(sel_c[:, c, :], sel_f[:, g, c, :]).then_inc(e_sel, 1)
                pool_wait(pool, e_half, count)
                pool.tensor_tensor(moe_hl[:, c, LO, :], raw_moe[:, c, :], f32(moe_hl[:, c, HI, :]),
                                   ALU.subtract).then_inc(e_split, 1)

            pool_wait(pool, e_raw, 16)
            for c in range(MGC):
                split_moe(0, c, c + 1)
            pool.wait_ge(r_tp, T // 2)
            pool.memset(acc[:, :, :], 0.0).then_inc(r_zero, 1)

            def step3(it, k):
                n = it * PER3 + k
                static = isinstance(n, int)
                if not static or n < NE:
                    pool_wait(pool, e_hh, n + 1)
                    pool.tensor_tensor(h_hl[:, k % 2, LO, :], h_t[:, k % 2, :], f32(h_hl[:, k % 2, HI, :]),
                                       ALU.subtract).then_inc(e_hlo, 1)
                m = k - 2
                if 0 <= m < PER3 and m // MGC == B - 1 and (not static or it + 1 < MG):
                    c = m % MGC
                    pool_wait(pool, e_raw, it * 16 + 32)
                    pool_wait(pool, e_dn, (n - 1) * C)
                    split_moe(it + 1, c, it * MGC + (MGC + c + 1))

            run_steps(pool, step3, NE + 2, PER3, 2, 4)

        @block.scalar
        def _(act):
            roots = [0]

            def take_root():
                roots[0] += 1
                act.wait_ge(root_in, roots[0])
                act.activation(sm[:, 5, :], sm[:, 3, :], ACT.Sqrt).then_inc(root, 1)

            take_root()
            act.wait_ge(sel_in, 16)
            act.activation(sel[:, :], sel_raw[:, :], ACT.Copy).then_inc(sel_ok, 1)
            act.wait_ge(gate_in, 16)
            act.activation(gate_hl[:, HI, :, :], gate_raw[:, :, :], ACT.Copy).then_inc(gate_ok, 1)
            def project(b):
                for c in range(C):
                    act.wait_ge(ph1_tp, b * C + (c + 1))
                    if later(b):
                        act.wait_ge(ph1_mm, b * 6)
                    act.activation(xT1[:, c, :], bank[c][:, :], ACT.Copy).then_inc(ph1_xT, 1)
                for m in range(4):
                    dst, scale = (q1_hl, SCALE1) if m < 2 else (k1_hl, 1.0)
                    act.wait_ge(ph1_mm, b * 6 + (m + 1))
                    act.activation(dst[:, b * 2 + m % 2, HI, :], bank[2 + m][:, :], ACT.Copy, scale=scale)\
                       .then_inc(ph1_hi, 1)
                for i in range(2):
                    act.wait_ge(ph1_mm, b * 6 + (5 + i))
                    for c in range(C):
                        ins = act.activation(
                            v1[:, b * 2 + c, 2 * i:2 * i + 2, :],
                            bank[6 + i][:, :].rearrange("p (j c n) -> p c j n", j=2, c=C)[:, c], ACT.Copy)
                    ins.then_inc(ph1_v, 1)
            first_then_loop(act, project, B)
            meet(act, 0)

            def take_stack(m_par, count):
                for w in range(2):
                    act.wait_ge(a1_sel, count + w + 1)
                    act.activation(stk[:, m_par, w, :], bank[STK_BANK[w]][:, :], ACT.Copy).then_inc(a1_stk, 1)

            def step1(it, k):
                n = it * GH + k
                static = isinstance(n, int)
                if static and n == 0:
                    take_stack(0, 0)
                def exp(t):
                    qi = TPB - 1 - t
                    act.wait_ge(a1_max, n * TPB + (t + 1 if t < 2 else TPB))
                    if t == 0 and (not static or n >= 2):
                        act.wait_ge(a1_t, (n - 1) * TPB)
                    act.activation(p1[:, k % 2, POFF[qi]:POFF[qi + 1]], s1(t), ACT.Exp,
                                   bias=stat1[:, 0, k % 2, t:t + 1],
                                   accum_out=stat1[:, 1, k % 2, t:t + 1]).then_inc(a1_exp, 1)

                def take_pt(t):
                    kj = TPB - 1 - t
                    act.wait_ge(a1_t, n * TPB + (t + 1 - TPB))
                    if not static or n >= 2:
                        act.wait_ge(a1_pv, n * TPB + (t + 1 - 2 * TPB))
                    act.activation(pT1[:, QOFF[kj]:QOFF[kj + 1]], bank[PT1_BANK[t % 2]][:, 0:TB - P * kj], ACT.Copy)\
                       .then_inc(a1_pta, 1)

                softmax, values = not static or n < N1, not static or n >= 1
                if values:
                    take_pt(1)
                if softmax:
                    exp(0)
                    exp(1)
                if values:
                    take_pt(3)
                if softmax:
                    exp(2)
                    exp(3)
                if k % 2 == 0 and (not static or n // 2 + 1 < N1 // 2):
                    if not static or n >= 2:
                        act.wait_ge(a1_s, n * TPB)
                    take_stack((k // 2 + 1) % 2, n + 2)

            run_steps(act, step1, N1 + 1, GH, 2, 5)
            meet(act, 1)
            for g in range(T // 2):
                act.wait_ge(m_y, g + 1)
                act.activation(y_sb[:, 2 * g:2 * g + 2, :].rearrange("p j d -> p (j d)"), bank[g][:, :], ACT.Copy)\
                   .then_inc(m_ys, 1)
            take_root()
            take_root()
            take_root()
            act.wait_ge(small_in, 16)
            for b in range(B):
                for c in range(C):
                    act.wait_ge(m_tp, b * C + c + 1)
                    act.activation(xT[:, HI, c, TB * b:TB * (b + 1)], bank[b * C + c][:, :], ACT.Copy,
                                   scale=ln_w[:, 0, c:c + 1]).then_inc(m_hi, 1)
            meet(act, 2)

            def step2(it, k):
                n = it * PER2 + k
                static = isinstance(n, int)
                here, prev = not static or n < N2, not static or 1 <= n <= N2
                if here:
                    for i in range(3):
                        act.wait_ge(b_qkv, n * 3 + (i + 1))
                        if i == 0 and (not static or n >= 1):
                            act.wait_ge(b_s, n * TPB)
                        if i == 2 and k % 2 == 0 and (not static or n >= 4):
                            act.wait_ge(b_pv, (n - 2) * TPB)
                        dst = v2_half(k, HI) if i == 2 else qk2[:, i, HI, :]
                        act.activation(dst, bank[4 + i][:, :], ACT.Copy, scale=(SCALE2 if i == 0 else 1.0))\
                           .then_inc(b_hi, 1)
                if prev:
                    for t in range(TPB):
                        kj = TPB - 1 - t
                        act.wait_ge(b_t, n * TPB + (t + 1 - TPB))
                        if not static or n >= 2:
                            act.wait_ge(b_pv, n * TPB + (t + 1 - 2 * TPB))
                        act.activation(pT2[:, HI, QOFF[kj]:QOFF[kj + 1]], bank[t][:, 0:TB - P * kj],
                                       ACT.Copy).then_inc(b_pth, 1)
                if here:
                    for t in range(TPB):
                        qi = TPB - 1 - t
                        act.wait_ge(b_max, n * TPB + (t + 1))
                        if t == 0 and (not static or n >= 2):
                            act.wait_ge(b_t, (n - 1) * TPB)
                        act.activation(p2[:, k % 2, POFF[qi]:POFF[qi + 1]], s2(t),
                                       ACT.Exp, bias=stat2[:, 0, k % 2, t:t + 1],
                                       accum_out=stat2[:, 1, k % 2, t:t + 1]).then_inc(b_exp, 1)
                    act.wait_ge(b_rcp, n + 1)
                    for t in range(TPB):
                        qi = TPB - 1 - t
                        pt = p2[:, k % 2, POFF[qi]:POFF[qi + 1]]
                        act.activation(pt, pt, ACT.Copy, scale=stat2[:, 2, k % 2, t:t + 1]).then_inc(b_norm, 1)
                if prev:
                    act.wait_ge(b_pv, n * TPB)
                    if not static or n >= 2:
                        act.wait_ge(b_e, (n - 1) * C)
                    act.activation(o2[:, HI, :], bank[7][:, :], ACT.Copy).then_inc(b_oh, 1)

            run_steps(act, step2, N2 + 2, PER2, 4, 4)
            meet(act, 3)
            act.wait_ge(e_raw, 16)
            for c in range(MGC):
                act.activation(moe_hl[:, c, HI, :], raw_moe[:, c, :], ACT.Copy).then_inc(e_half, 1)
            take_root()
            for b in range(B):
                for c in range(C):
                    act.wait_ge(r_tp2, b * C + c + 1)
                    act.activation(xT[:, HI, c, TB * b:TB * (b + 1)], bank[b * C + c][:, :], ACT.Copy,
                                   scale=ln_w[:, 1, c:c + 1]).then_inc(r_hi, 1)
            act.wait_ge(r_sub, 1)
            act.activation(pr[:, :, :], lg[:, :, :], ACT.Exp).then_inc(r_exp, 1)
            act.wait_ge(r_zero, 1)
            for b in range(B):
                act.wait_ge(r_tp3, b + 1)
                act.activation(wT[0:E + 2, TB * b:TB * (b + 1)], bank[1 + b][0:E + 2, :], ACT.Copy)\
                   .then_inc(r_wh, 1)

            def moe_hi(c):
                act.activation(moe_hl[:, c, HI, :], raw_moe[:, c, :], ACT.Copy).then_inc(e_half, 1)

            def step3(it, k):
                n = it * PER3 + k
                static = isinstance(n, int)
                m = k - 2
                if 0 <= m < PER3 and m // MGC == B - 1 and (not static or it + 1 < MG):
                    act.wait_ge(e_raw, it * 16 + 32)
                    act.wait_ge(e_dn, (n - 1) * C)
                    moe_hi(m % MGC)
                if static and n >= NE:
                    return
                act.wait_ge(e_g, n + 1)
                act.activation(h_s[:, k % 2, :], bank[k % 2][:, :], ACT.Silu).then_inc(e_silu, 1)
                act.wait_ge(e_h, n + 1)
                if not static or n >= 2:
                    act.wait_ge(e_dn, (n - 1) * C)
                act.activation(h_hl[:, k % 2, HI, :], h_t[:, k % 2, :], ACT.Copy).then_inc(e_hh, 1)

            run_steps(act, step3, NE, PER3, 2, 3)
            take_root()

        @block.vector
        def _(dve):
            links = [0]

            def link(*instructions):
                for ins in instructions:
                    ins.then_inc(chain, 1)
                links[0] += len(instructions)
                dve.wait_ge(chain, links[0])

            roots = [0]
            mean, rstd, dif, var, tmp, rt, sq = (sm[:, i, :] for i in (0, 1, 2, 3, 4, 5, 6))

            def row_stats(eps, square_mean=False):
                link(dve.tensor_tensor(mean, st6[:, :, 1], st6[:, :, 4], ALU.add),
                     dve.tensor_tensor(dif, st6[:, :, 1], st6[:, :, 4], ALU.subtract),
                     dve.tensor_tensor(var, st6[:, :, 2], st6[:, :, 5], ALU.add))
                link(dve.tensor_tensor(dif, dif, dif, ALU.mult),
                     dve.tensor_scalar(mean, mean, 0.5, None, ALU.mult))
                link(dve.scalar_tensor_tensor(var, dif, D / 4.0, var, ALU.mult, ALU.add),
                     dve.tensor_tensor(sq, mean, mean, ALU.mult))
                if square_mean:
                    link(dve.tensor_scalar(var, var, 1.0 / D, eps, ALU.mult, ALU.add))
                    dve.tensor_tensor(var, var, sq, ALU.add).then_inc(root_in, 1)
                else:
                    dve.tensor_scalar(var, var, 1.0 / D, eps, ALU.mult, ALU.add).then_inc(root_in, 1)
                roots[0] += 1
                dve.wait_ge(root, roots[0])
                link(dve.reciprocal(rstd, rt))
                link(dve.tensor_tensor(tmp, rstd, rstd, ALU.mult))
                link(dve.tensor_tensor(tmp, tmp, var, ALU.mult))
                link(dve.tensor_scalar(tmp, tmp, -0.5, 1.5, ALU.mult, ALU.add))
                link(dve.tensor_tensor(rstd, rstd, tmp, ALU.mult))

            def tile_stats(src):
                link(*[dve.bn_stats(st6[:, i, :], src[:, i, :]) for i in range(T)])

            for b in range(B):
                dve.wait_ge(x_in[b], 16)
                link(*[dve.bn_stats(st6[:, i, :], x_sb[:, i, :]) for i in range(TPB * b, TPB * (b + 1))])
            row_stats(LN_EPS)
            dve.wait_ge(gate_ok, 1)
            dve.tensor_tensor(gate_hl[:, LO, :, :], gate_raw[:, :, :], f32(gate_hl[:, HI, :, :]), ALU.subtract)\
               .then_inc(gate_lo, 1)
            def project(b):
                if later(b):
                    dve.wait_ge(ph1_tp, b * C)
                for j in range(TPB):
                    dve.tensor_scalar(xn1[:, j, :], x_sb[:, b * TPB + j, :], sm[:, 0, ds(b * TPB + j, 1)],
                                      sm[:, 1, ds(b * TPB + j, 1)], ALU.subtract, ALU.mult).then_inc(ph1_xn, 1)
                for m in range(4):
                    dst, scale = (q1_hl, SCALE1) if m < 2 else (k1_hl, 1.0)
                    dve.wait_ge(ph1_hi, b * 4 + (m + 1))
                    dve.scalar_tensor_tensor(dst[:, b * 2 + m % 2, LO, :], bank[2 + m][:, :], scale,
                                             f32(dst[:, b * 2 + m % 2, HI, :]), ALU.mult, ALU.subtract)\
                       .then_inc(ph1_lo, 1)
            first_then_loop(dve, project, B)
            meet(dve, 0)

            def step1(it, k):
                n = it * GH + k
                static = isinstance(n, int)
                softmax, values = not static or n < N1, not static or n >= 1

                def row_max(t):
                    qi = TPB - 1 - t
                    dve.wait_ge(a1_s, n * TPB + (t + 1 if t < 2 else TPB))
                    dve.tensor_reduce(stat1[:, 0, k % 2, t:t + 1], s1(t), AX.X, ALU.max,
                                      negate=True).then_inc(a1_max, 1)

                def take_pt(t):
                    kj = TPB - 1 - t
                    dve.wait_ge(a1_t, n * TPB + (t + 1 - TPB))
                    if not static or n >= 2:
                        dve.wait_ge(a1_pv, n * TPB + (t + 1 - 2 * TPB))
                    dve.tensor_copy(pT1[:, QOFF[kj]:QOFF[kj + 1]], bank[PT1_BANK[t % 2]][:, 0:TB - P * kj])\
                       .then_inc(a1_ptd, 1)

                if values:
                    take_pt(0)
                if softmax:
                    for t in range(TPB - 1):
                        row_max(t)
                if values:
                    take_pt(2)
                if softmax:
                    row_max(TPB - 1)
                if softmax:
                    for i, (first, last) in enumerate(((0, 1), (1, TPB))):
                        dve.wait_ge(a1_exp, n * TPB + last)
                        dve.reciprocal(stat1[:, 2, k % 2, first:last], stat1[:, 1, k % 2, first:last])\
                           .then_inc(a1_rcp, 1)
                        dve.wait_ge(a1_rcp, n * 2 + (i + 1))
                        for t in range(first, last):
                            qi = TPB - 1 - t
                            pt = p1[:, k % 2, POFF[qi]:POFF[qi + 1]]
                            dve.tensor_scalar(pt, pt, stat1[:, 2, k % 2, t:t + 1], None, ALU.mult)\
                               .then_inc(a1_norm, 1)
                if k % GH == 0 and (not static or n >= 1):
                    dve.wait_ge(a1_pv, n * TPB)
                    dve.tensor_copy(oT1[:, it + (k // GH - 1), :], bank[O1_BANK][:, :]).then_inc(a1_o, 1)

            run_steps(dve, step1, N1 + 1, GH, 2, 5)
            meet(dve, 1)
            for g in range(T // 2):
                dve.wait_ge(m_ys, g + 1)
                link(*[dve.bn_stats(st6[:, i, :], y_sb[:, i, :]) for i in (2 * g, 2 * g + 1)])
            row_stats(LN_EPS)
            link(*[dve.tensor_scalar(u_sb[:, i, :], y_sb[:, i, :], mean[:, i:i + 1], rstd[:, i:i + 1],
                                     ALU.subtract, ALU.mult) for i in range(T)])
            link(*[dve.tensor_tensor(x_sb[:, i:i + TPB, :], x_sb[:, i:i + TPB, :], u_sb[:, i:i + TPB, :], ALU.add)
                   for i in range(0, T, TPB)])
            tile_stats(x_sb)
            row_stats(LN_EPS)
            link(*[dve.tensor_scalar(hs[:, i, :], x_sb[:, i, :], mean[:, i:i + 1], rstd[:, i:i + 1],
                                     ALU.subtract, ALU.mult) for i in range(T)])
            tile_stats(hs)
            row_stats(RMS_EPS, square_mean=True)
            for i in range(T):
                dve.tensor_scalar(y_sb[:, i, :], hs[:, i, :], rstd[:, i:i + 1], None, ALU.mult).then_inc(m_xn, 1)
            dve.wait_ge(small_in, 16)
            for b in range(B):
                for c in range(C):
                    dve.wait_ge(m_hi, b * C + c + 1)
                    cols = slice(TB * b, TB * (b + 1))
                    dve.scalar_tensor_tensor(xT[:, LO, c, cols], bank[b * C + c][:, :], ln_w[:, 0, c:c + 1],
                                             f32(xT[:, HI, c, cols]), ALU.mult, ALU.subtract).then_inc(m_lo, 1)
            meet(dve, 2)

            def step2(it, k):
                n = it * PER2 + k
                static = isinstance(n, int)
                here, prev = not static or n < N2, not static or 1 <= n <= N2
                if here:
                    for i in range(3):
                        dve.wait_ge(b_hi, n * 3 + (i + 1))
                        hi, lo = (v2_half(k, HI), v2_half(k, LO)) if i == 2 else (qk2[:, i, HI, :], qk2[:, i, LO, :])
                        dve.scalar_tensor_tensor(lo, bank[4 + i][:, :], SCALE2 if i == 0 else 1.0,
                                                 f32(hi), ALU.mult, ALU.subtract).then_inc(b_lo, 1)
                if prev:
                    for t in range(TPB):
                        kj = TPB - 1 - t
                        dve.wait_ge(b_pth, n * TPB + (t + 1 - TPB))
                        dve.tensor_tensor(pT2[:, LO, QOFF[kj]:QOFF[kj + 1]], bank[t][:, 0:TB - P * kj],
                                          f32(pT2[:, HI, QOFF[kj]:QOFF[kj + 1]]), ALU.subtract).then_inc(b_ptl, 1)
                if here:
                    for t in range(TPB):
                        dve.wait_ge(b_s, n * TPB + (t + 1))
                        dve.tensor_reduce(stat2[:, 0, k % 2, t:t + 1], s2(t), AX.X,
                                          ALU.max, negate=True).then_inc(b_max, 1)
                if not static or n >= 2:
                    b = (k - 2) // 2 % B
                    for c in range(C):
                        dve.wait_ge(b_e, n * C + (c + 1 - 2 * C))
                        if static and n == 2 and c == 0:
                            dve.wait_ge(b_acc0, 1)
                        cols = slice(TB * b, TB * (b + 1))
                        dve.tensor_tensor(acc[:, c, cols], acc[:, c, cols], bank[4 + c][:, :], ALU.add)\
                           .then_inc(b_acc, 1)
                if here:
                    dve.wait_ge(b_exp, n * TPB + TPB)
                    dve.reciprocal(stat2[:, 2, k % 2, :], stat2[:, 1, k % 2, :]).then_inc(b_rcp, 1)
                if prev:
                    dve.wait_ge(b_oh, n * 1)
                    dve.tensor_tensor(o2[:, LO, :], bank[7][:, :], f32(o2[:, HI, :]), ALU.subtract)\
                       .then_inc(b_ol, 1)

            run_steps(dve, step2, N2 + 2, PER2, 4, 4)
            meet(dve, 3)
            for g in range(T // 2):
                dve.wait_ge(r_tp, g + 1)
                two = hs[:, 2 * g:2 * g + 2, :].rearrange("p j d -> p (j d)")
                dve.tensor_tensor(two, two, bank[g][:, :], ALU.add).then_inc(r_hid, 1)
            dve.wait_ge(r_hid, T // 2)
            tile_stats(hs)
            row_stats(RMS_EPS, square_mean=True)
            for i in range(T):
                dve.tensor_scalar(xn2[:, i, :], hs[:, i, :], rstd[:, i:i + 1], None, ALU.mult).then_inc(r_xn, 1)
            for b in range(B):
                for c in range(C):
                    dve.wait_ge(r_hi, b * C + c + 1)
                    cols = slice(TB * b, TB * (b + 1))
                    dve.scalar_tensor_tensor(xT[:, LO, c, cols], bank[b * C + c][:, :], ln_w[:, 1, c:c + 1],
                                             f32(xT[:, HI, c, cols]), ALU.mult, ALU.subtract).then_inc(r_lo, 1)
            logits = bank[0][:, 0:T * E].rearrange("p (t e) -> p t e", t=T)
            col = sm[:, 7, :]

            def wide(ap):
                return ap.unsqueeze(2).to_broadcast([P, T, E])

            dve.wait_ge(r_lg, 1)
            link(dve.tensor_reduce(col, logits, AX.X, ALU.max))
            dve.tensor_tensor(lg[:, :, :], logits, wide(col), ALU.subtract).then_inc(r_sub, 1)
            dve.wait_ge(r_exp, 1)
            link(dve.tensor_reduce(col, pr[:, :, :], AX.X, ALU.add))
            link(dve.reciprocal(col, col))
            link(dve.tensor_tensor(pr[:, :, :], pr[:, :, :], wide(col), ALU.mult))
            ranks = []
            for e in range(E):
                own = pr[:, :, e:e + 1]
                if e:
                    ranks.append(dve.tensor_tensor(rk[:, :, e, 0:e], pr[:, :, 0:e],
                                                   own.to_broadcast([P, T, e]), ALU.is_ge))
                ranks.append(dve.tensor_tensor(rk[:, :, e, e:E], pr[:, :, e:E],
                                               own.to_broadcast([P, T, E - e]), ALU.is_gt))
            link(*ranks)
            link(dve.tensor_reduce(lg[:, :, :], rk[:, :, :, :], AX.X, ALU.add))
            link(dve.tensor_scalar(lg[:, :, :], lg[:, :, :], float(TOPK), None, ALU.is_lt))
            link(dve.tensor_tensor(pr[:, :, :], pr[:, :, :], lg[:, :, :], ALU.mult))
            link(dve.tensor_reduce(col, pr[:, :, :], AX.X, ALU.add))
            link(dve.reciprocal(col, col))
            dve.memset(wtok[:, :, E:E + 2], 1.0).then_inc(r_w, 1)
            dve.tensor_tensor(wtok[:, :, 0:E], pr[:, :, :], wide(col), ALU.mult).then_inc(r_w, 1)
            for b in range(B):
                dve.wait_ge(r_wh, b + 1)
                cols = slice(TB * b, TB * (b + 1))
                dve.tensor_tensor(wT[32:32 + E + 2, cols], bank[1 + b][0:E + 2, :], f32(wT[0:E + 2, cols]),
                                  ALU.subtract).then_inc(r_wl, 1)
            dve.wait_ge(r_zero, 2)

            def step3(it, k):
                n = it * PER3 + k
                static = isinstance(n, int)
                par = k % 2
                if not static or n < NE:
                    dve.wait_ge(e_silu, n + 1)
                    dve.wait_ge(e_w, n + 1)
                    if not static or n >= 2:
                        dve.wait_ge(e_hlo, n - 1)
                    dve.tensor_tensor(h_t[:, par, :], h_s[:, par, :], bank[4][:, :], ALU.mult).then_inc(e_sw, 1)
                    dve.wait_ge(e_u, n + 1)
                    dve.wait_ge(e_sw, n + 1)
                    dve.tensor_tensor(h_t[:, par, :], h_t[:, par, :], bank[2 + par][:, :], ALU.mult)\
                       .then_inc(e_h, 1)
                if k % MGC == 0 and (not static or n > 0):
                    b = (k // MGC - 1) % B
                    for c in range(C):
                        dve.wait_ge(e_dn, n * C - (C - 1 - c))
                        cols = slice(TB * b, TB * (b + 1))
                        dve.tensor_tensor(acc[:, c, cols], acc[:, c, cols], bank[6 + c][:, :], ALU.add)\
                           .then_inc(e_acc, 1)

            run_steps(dve, step3, NE + 1, PER3, 2, 3)
            for g in range(T // 2):
                dve.wait_ge(f_tp, g + 1)
                two = hs[:, 2 * g:2 * g + 2, :].rearrange("p j d -> p (j d)")
                dve.tensor_tensor(two, two, bank[g][:, :], ALU.add).then_inc(f_y, 1)
            dve.wait_ge(f_y, T // 2)
            tile_stats(hs)
            row_stats(LN_EPS)
            link(*[dve.tensor_scalar(u_out[:, i, :], hs[:, i, :], mean[:, i:i + 1], rstd[:, i:i + 1],
                                     ALU.subtract, ALU.mult) for i in range(T)])
            for i in range(0, T, TPB):
                dve.tensor_tensor(u_out[:, i:i + TPB, :], u_out[:, i:i + TPB, :], x_sb[:, i:i + TPB, :], ALU.add)\
                   .then_inc(f_out, 1)

        @block.tensor
        def _(pe):
            def product(out, pairs, start=True, stop=True, **kw):
                for i, (a, b) in enumerate(pairs):
                    ins = pe.matmul(out, a, b, start=start and i == 0, stop=stop and i == len(pairs) - 1, **kw)
                return ins

            def mask_diagonal(scores, qi):
                pe.matmul(scores[:, P * qi:P * (qi + 1)], ident_b[:, :], mask_b[:, :], start=True, stop=False,
                          skip_group_check=True)

            pe.wait_ge(const, 6)
            pe.wait_ge(w1_in, 16)
            def project(b):
                pe.wait_ge(ph1_xn, b * TPB + TPB)
                if later(b):
                    pe.wait_ge(ph1_xT, b * C)
                for c in range(C):
                    for j in range(TPB):
                        ins = pe.transpose(bank[c][:, P * j:P * (j + 1)], xn1[:, j, P * c:P * (c + 1)], ident[:, :])
                    ins.then_inc(ph1_tp, 1)
                pe.wait_ge(ph1_xT, b * C + C)
                if later(b):
                    pe.wait_ge(ph1_lo, b * 4)
                for m in range(4):
                    product(bank[2 + m][:, :], [(qkv1[:, c, P * m:P * (m + 1)], xT1[:, c, :]) for c in range(C)])\
                        .then_inc(ph1_mm, 1)
                if later(b):
                    pe.wait_ge(ph1_v, b * 2)
                for i in range(2):
                    for j in (0, 1):
                        rows = slice(P * (2 * i + j), P * (2 * i + j + 1))
                        ins = product(bank[6 + i][:, D * j:D * (j + 1)],
                                      [(xT1[:, c, rows], qkv1[:, c, 2 * D:3 * D]) for c in range(C)])
                    ins.then_inc(ph1_mm, 1)

            first_then_loop(pe, project, B)
            pe.wait_ge(sel_ok, 1)
            meet(pe, 0)

            def stack(g, pair):
                for w, src in enumerate((q1_hl, k1_hl)):
                    product(bank[STK_BANK[w]][:, :],
                            [(sel[:, P * (4 * pair + 2 * w + a):P * (4 * pair + 2 * w + a + 1)], src[:, g, a, :])
                             for a in (HI, LO)]).then_inc(a1_sel, 1)

            def step1(it, k):
                n = it * GH + k
                static = isinstance(n, int)
                softmax, values = not static or n < N1, not static or n >= 1
                head, prev = k % GH, (k - 1) % GH
                if static and n == 0:
                    stack(0, 0)

                def scores(t):
                    qi = TPB - 1 - t
                    rows = slice(64 * (k % 2), 64 * (k % 2) + 64)
                    if t == 0:
                        pe.wait_ge(a1_stk, n + (2 - k % 2))
                    if not static or n >= 1:
                        pe.wait_ge(a1_exp, n * TPB + (t + 1 if t < 2 else TPB) - TPB)
                    m = (k // 2) % 2
                    mask_diagonal(s1(t), qi)
                    pe.matmul(s1(t), stk[rows, m, 0, P * qi:P * (qi + 1)], stk[rows, m, 1, 0:P * (qi + 1)],
                              start=False, stop=True, skip_group_check=True).then_inc(a1_s, 1)

                def turn(t):
                    kj = TPB - 1 - t
                    pe.wait_ge(a1_norm, n * TPB + (t + 1 - TPB))
                    if not static or n >= 2 or t >= 2:
                        taken = a1_pta if t % 2 else a1_ptd
                        pe.wait_ge(taken, n * 2 + (t // 2 - 2))
                    for qi in range(kj, TPB):
                        ins = pe.transpose(bank[PT1_BANK[t % 2]][:, P * (qi - kj):P * (qi - kj + 1)],
                                           p1[:, (k - 1) % 2, POFF[qi] + P * kj:POFF[qi] + P * (kj + 1)],
                                           ident[:, :])
                    ins.then_inc(a1_t, 1)

                def values_of(t):
                    kj = TPB - 1 - t
                    pe.wait_ge(a1_pta if t % 2 else a1_ptd, n * 2 + (t // 2 - 1))
                    if t == 0:
                        pe.wait_ge(a1_vpad, n * 1)
                        if prev == 0 and (not static or n > GH):
                            pe.wait_ge(a1_o, it + (k - 1) // GH)
                    pe.matmul(bank[O1_BANK][:, P * kj:TB], v1_pad[:, kj, prev, :], pT1[:, QOFF[kj]:QOFF[kj + 1]],
                              start=(prev == 0 and t == 0), stop=(prev == GH - 1 and t == TPB - 1),
                              skip_group_check=True).then_inc(a1_pv, 1)

                if values:
                    turn(0)
                    turn(1)
                if softmax:
                    for t in range(TPB):
                        scores(t)
                if values:
                    values_of(0)
                    turn(2)
                    values_of(1)
                    turn(3)
                    values_of(2)
                    values_of(3)
                if k % 2 == 0 and (not static or n // 2 + 1 < N1 // 2):
                    pe.wait_ge(a1_stk, n + 2)
                    stack(it + (k + 2) // GH, (k // 2 + 1) % PAIRS1)

            run_steps(pe, step1, N1 + 1, GH, 2, 5)
            meet(pe, 1)
            pe.wait_ge(wo1_in, 16)
            for g in range(T // 2):
                for r in range(2):
                    b, j = divmod(2 * g + r, TPB)
                    ins = product(bank[g][:, D * r:D * (r + 1)],
                                  [(oT1[:, 2 * b + c, P * j:P * (j + 1)], wo1[:, c, :]) for c in range(C)])
                ins.then_inc(m_y, 1)

            def turn_all(src, ready, done):
                for b in range(B):
                    pe.wait_ge(ready, TPB * (b + 1))
                    for c in range(C):
                        for j in range(TPB):
                            ins = pe.transpose(bank[b * C + c][:, P * j:P * (j + 1)],
                                               src[:, TPB * b + j, P * c:P * (c + 1)], ident[:, :])
                        ins.then_inc(done, 1)

            def turn_acc(done):
                for g in range(T // 2):
                    for r in range(2):
                        for c in range(C):
                            i = 2 * g + r
                            ins = pe.transpose(bank[g][:, D * r + P * c:D * r + P * (c + 1)],
                                               acc[:, c, P * i:P * (i + 1)], ident[:, :])
                    ins.then_inc(done, 1)

            pe.wait_ge(m_ys, T // 2)
            turn_all(y_sb, m_xn, m_tp)
            meet(pe, 2)

            def step2(it, k):
                n = it * PER2 + k
                static = isinstance(n, int)
                here = not static or n < N2
                prev = not static or 1 <= n <= N2
                b, head = k // 2 % B, k % 2

                def turn(t):
                    kj = TPB - 1 - t
                    pe.wait_ge(b_norm, n * TPB + (t + 1 - TPB))
                    for qi in range(kj, TPB):
                        ins = pe.transpose(bank[t][:, P * (qi - kj):P * (qi - kj + 1)],
                                           p2[:, (k - 1) % 2, POFF[qi] + P * kj:POFF[qi] + P * (kj + 1)],
                                           ident[:, :])
                    ins.then_inc(b_t, 1)

                def scores(t):
                    qi = TPB - 1 - t
                    if prev:
                        pe.wait_ge(b_ptl, n * TPB + (t + 1 - TPB))
                    mask_diagonal(s2(t), qi)
                    product(s2(t),
                            [(qk2[:, 0, s, P * qi:P * (qi + 1)], qk2[:, 1, m, 0:P * (qi + 1)]) for s, m in PARTS],
                            start=False, skip_group_check=True).then_inc(b_s, 1)

                def values_of(t):
                    kj = TPB - 1 - t
                    pe.wait_ge(b_ptl, n * TPB + (t + 1 - TPB))
                    if t == 0 and (not static or n >= 2):
                        pe.wait_ge(b_ol, n - 1)
                    if t == 2 and k % 2 == 1 and here:
                        pe.wait_ge(b_lo, n * 3 + 3)
                    own = slice(P * ((k - 1) % 2), P * ((k - 1) % 2 + 1))
                    product(bank[7][:, P * kj:TB],
                            [(v2[:, (k - 1) // 2 % 2, s, kj, own], pT2[:, m, QOFF[kj]:QOFF[kj + 1]])
                             for s, m in PARTS], start=(t == 0), stop=(t == TPB - 1), skip_group_check=True)\
                        .then_inc(b_pv, 1)

                if here:
                    if b == 0 and head == 0:
                        pe.wait_ge(b_wqkv, it + (k // PER2 + 1))
                    for i in range(2):
                        if not static or n >= 1:
                            pe.wait_ge(b_lo, n * 3 + (i - 2))
                        if not static or n >= 3:
                            pe.wait_ge(b_acc, n * C + (i + 1 - 3 * C))
                        product(bank[4 + i][:, :],
                                [(w2_hl[:, s, P * (C * (2 * i + head) + c):P * (C * (2 * i + head) + c + 1)],
                                  xT[:, m, c, TB * b:TB * (b + 1)])
                                 for c in range(C) for s, m in PARTS]).then_inc(b_qkv, 1)
                    if not static or n >= 1:
                        pe.wait_ge(b_lo, n * 3)
                    for j in (0, 1):
                        first = TB * b + P * (2 - 2 * head + j)
                        ins = product(bank[6][:, 2 * P * j:2 * P * (j + 1)],
                                      [(xT[:, s, c, first:first + P],
                                        w2_hl[:, m, P * (4 * C + 2 * c):P * (4 * C + 2 * c + 2)])
                                       for c in range(C) for s, m in PARTS])
                    ins.then_inc(b_qkv, 1)
                if prev:
                    for t in range(TPB):
                        turn(t)
                if not static or n >= 2:
                    if k % PER2 == 2:
                        pe.wait_ge(b_wo, it + ((k - 2) // PER2 + 1))
                    pe.wait_ge(b_ol, n - 1)
                    for c in range(C):
                        pe.wait_ge(b_lo, n * 3 + (c + 1) if here else N2 * 3)
                        if not static or n >= 3:
                            pe.wait_ge(b_acc, n * C + (c + 1 - 3 * C))
                        product(bank[4 + c][:, :], [(wo2_hl[:, s, D * head + P * c:D * head + P * (c + 1)], o2[:, m, :])
                                                    for s, m in PARTS]).then_inc(b_e, 1)
                if here:
                    pe.wait_ge(b_lo, n * 3 + 2)
                    for t in range(TPB):
                        scores(t)
                if prev:
                    for t in range(TPB):
                        values_of(t)

            run_steps(pe, step2, N2 + 2, PER2, 4, 4)
            meet(pe, 3)
            turn_acc(r_tp)
            pe.wait_ge(r_hid, T // 2)
            turn_all(xn2, r_xn, r_tp2)
            pe.wait_ge(r_lo, B * C)
            pe.wait_ge(gate_lo, 1)
            for i in range(T):
                ins = product(bank[0][:, E * i:E * (i + 1)],
                              [(xT[:, s, c, P * i:P * (i + 1)], gate_hl[:, m, c, :])
                               for c in range(C) for s, m in PARTS])
            ins.then_inc(r_lg, 1)
            pe.wait_ge(r_w, 2)
            for b in range(B):
                for j in range(TPB):
                    ins = pe.transpose(bank[1 + b][0:E + 2, P * j:P * (j + 1)], wtok[:, TPB * b + j, :], ident[:, :])
                ins.then_inc(r_tp3, 1)
            pe.wait_ge(r_wl, B)

            def step3(it, k):
                n = it * PER3 + k
                static = isinstance(n, int)
                b, c = k % PER3 // MGC, k % MGC
                cols = slice(TB * b, TB * (b + 1))

                def up(out, first):
                    return product(out, [(moe_hl[:, c, s, first + P * d:first + P * (d + 1)], xT[:, m, d, cols])
                                         for d in range(C) for s, m in PARTS])

                if not static or n < NE:
                    if b == 0:
                        pe.wait_ge(e_split, it * MGC + (MGC * (k // PER3) + c + 1))
                    if not static or n >= 2:
                        pe.wait_ge(e_silu, n - 1)
                    up(bank[k % 2][:, :], 0).then_inc(e_g, 1)
                    pe.wait_ge(e_sw, n * 1)
                    pe.matmul(bank[4][:, :], sel_c[:, c, :], wT[:, cols], start=True, stop=True).then_inc(e_w, 1)
                    if not static or n >= 2:
                        pe.wait_ge(e_h, n - 1)
                    up(bank[2 + k % 2][:, :], C * P).then_inc(e_u, 1)
                if not static or n >= 1:
                    cc = (k - 1) % MGC
                    pe.wait_ge(e_hlo, n * 1)
                    for d in range(C):
                        if cc == 0 and (not static or n > MGC):
                            pe.wait_ge(e_acc, it * (C * B) + (k - 1) // MGC * C)
                        product(bank[6 + d][:, :],
                                [(moe_hl[:, cc, s, 2 * C * P + P * d:2 * C * P + P * (d + 1)],
                                  h_hl[:, (k - 1) % 2, m, :]) for s, m in PARTS],
                                start=(cc == 0), stop=(cc == MGC - 1)).then_inc(e_dn, 1)

            run_steps(pe, step3, NE + 1, PER3, 2, 3)
            pe.wait_ge(e_acc, MG * B * C)
            turn_acc(f_tp)


def kernel(**inputs):
    import numpy as np
    import concourse.bacc as bacc
    from concourse.bass_utils import run_bass_kernel_spmd

    x = np.asarray(inputs["L0_attn_x"])
    D = x.shape[2]
    C = D // P

    def rows(w):
        w = np.asarray(w)
        return w.T.reshape(w.shape[1] // P, P, w.shape[0]).transpose(1, 0, 2)

    qkv1 = np.concatenate([rows(inputs[f"L0_attn_{n}"]) for n in ("Wq", "Wk", "Wv")], axis=2)
    wo1 = rows(inputs["L0_attn_Wo"])
    q_w, kv_w = rows(inputs["L0_ffn_q_w"]), rows(inputs["L0_ffn_kv_w"])
    H2 = 16
    q_w = q_w.reshape(P, C, H2, 192)[..., :P]
    k_w = kv_w[..., :H2 * P].reshape(P, C, H2, P)
    v_w = kv_w[..., H2 * P:2 * H2 * P].reshape(P, C, H2, P)
    o_w = rows(inputs["L0_ffn_o_w"]).transpose(1, 0, 2)
    q_w, k_w, v_w = (a.reshape(P, C, H2 // 2, 2, P) for a in (q_w, k_w, v_w))
    parts = [a.transpose(2, 0, 3, 1, 4) for a in (q_w, k_w)] + [v_w.transpose(2, 0, 1, 3, 4),
                                                                o_w.reshape(H2 // 2, 2, P, D).transpose(0, 2, 1, 3)]
    qkvo2 = np.concatenate([a.reshape(H2 // 2, P, -1) for a in parts], axis=2)
    ln_w = np.stack([np.asarray(inputs[f"L0_ffn_ln{i}_w"]).reshape(C, P).T for i in (1, 2)], axis=1)
    gate = rows(inputs["L0_ffn_gate_w"])

    w1, w2 = np.asarray(inputs["L0_ffn_w1"]), np.asarray(inputs["L0_ffn_w2"])
    sh1, sh2 = np.asarray(inputs["L0_ffn_sh_gu_w"]), np.asarray(inputs["L0_ffn_sh_down_w"])
    EI, SI = w1.shape[1] // 2, sh2.shape[1]
    MG, MGC = 5, 5
    pad = np.zeros((MG * MGC * P - w1.shape[0] * EI - SI, D), w1.dtype)
    g_w = rows(np.concatenate([w1[:, :EI].reshape(-1, D), sh1[:SI], pad]))
    u_w = rows(np.concatenate([w1[:, EI:].reshape(-1, D), sh1[SI:], pad]))
    d_w = np.concatenate([w2.transpose(0, 2, 1).reshape(-1, D), sh2.T, pad])
    chunks = [a.reshape(P, C, MG, MGC, P).transpose(2, 0, 3, 1, 4).reshape(MG, P, MGC, C * P) for a in (g_w, u_w)]
    moe = np.concatenate(chunks + [d_w.reshape(MG, MGC, P, D).transpose(0, 2, 1, 3)], axis=3)

    stack = np.zeros((P, 4, 2, 2, P), np.float32)
    for pair in range(4):
        for half in range(2):
            for w, parts in enumerate((((0, 1), (2, 3)), ((0, 2), (1, 3)))):
                for a in range(2):
                    for part in parts[a]:
                        for d in range(16):
                            stack[32 * pair + 16 * half + d, pair, w, a, 64 * half + 16 * part + d] = 1.0
    arrays = {"x": x, "qkv1": qkv1, "wo1": wo1, "qkvo2": qkvo2, "ln_w": ln_w, "gate": gate, "moe": moe,
              "stack": stack.reshape(P, -1)}
    arrays = {f"in_{n}": np.ascontiguousarray(a) for n, a in arrays.items()}
    nc = bacc.Bacc("TRN2", target_bir_lowering=False, num_devices=1)
    args = [nc.dram_tensor(n, a.shape, mybir.dt.from_np(a.dtype), kind="ExternalInput").ap()
            for n, a in arrays.items()]
    out = nc.dram_tensor("out_0", x.shape, F32, kind="ExternalOutput").ap()
    sandwich_kernel(nc, *args, out)
    return run_bass_kernel_spmd(nc, [arrays], core_ids=[0]).results[0]["out_0"]
```

```python
from contextlib import ExitStack

import concourse.bass as bass
from concourse import mybir

F32 = mybir.dt.float32
F32R = mybir.dt.float32r
BF16 = mybir.dt.bfloat16
I32 = mybir.dt.int32
ALU = mybir.AluOpType
ACT = mybir.ActivationFunctionType
AX = mybir.AxisListType
ds = bass.ds

P = 128
HI, LO = 0, 1
PARTS = ((HI, HI), (LO, HI), (HI, LO))
MASKED = -1e30
LN_EPS = 1e-5
RMS_EPS = 1e-6
ROOT_GUESS = 1597463007.0


def run_steps(eng, step, total, period, first, ahead):
    loops = (total - first - ahead) // period
    for k in range(first):
        step(0, k)
    with eng.Fori(0, loops) as it:
        for k in range(first, first + period):
            step(it, k)
    for k in range(first, total - loops * period):
        step(loops, k)


def sandwich_kernel(nc, x_d, qkv1_d, wo1_d, qkvo2_d, ln_w_d, gate_d, moe_d, stack_d, out_d):
    B, TB, D = x_d.shape
    C = D // P
    T = B * TB // P
    TPB = TB // P
    H1, H2 = 16, 2 * qkvo2_d.shape[0]
    DH1 = D // H1
    GH = P // DH1
    G1 = B * H1 // GH
    E = gate_d.shape[2]
    EI = 176
    MG, _, MGC, _ = moe_d.shape
    TOPK = 4
    SCALE1 = float(DH1) ** -0.5
    SCALE2 = 192.0 ** -0.5
    WQKV2 = 3 * C * P
    QOFF = [0]
    for kj in range(TPB):
        QOFF.append(QOFF[-1] + TB - P * kj)
    POFF = [P * qi * (qi + 1) // 2 for qi in range(TPB + 1)]
    CAUSAL = QOFF[TPB]

    ctx = ExitStack()
    with ctx:
        def sb(stack, name, shape, dt=F32):
            return stack.enter_context(nc.sbuf_tensor(name, shape, dt))

        def sem(name):
            return ctx.enter_context(nc.semaphore(name))

        bank = [ctx.enter_context(nc.psum_tensor(f"bank{i}", [P, 512], F32)) for i in range(8)]

        x_sb = sb(ctx, "x_sb", [P, T, D])
        hs = sb(ctx, "hs", [P, T, D])
        acc = sb(ctx, "acc", [P, C, B * TB])
        xT = sb(ctx, "xT", [P, B, 2, C, TB], F32R)
        ident = sb(ctx, "ident", [P, P])
        ident_b = sb(ctx, "ident_b", [P, P], BF16)
        mask_f = sb(ctx, "mask_f", [P, P])
        mask_b = sb(ctx, "mask_b", [P, P], BF16)
        ln_w = sb(ctx, "ln_w", [P, 2, C])
        gate_raw = sb(ctx, "gate_raw", [P, C, E])
        gate_hl = sb(ctx, "gate_hl", [P, C, 2, E], F32R)
        wo1 = sb(ctx, "wo1", [P, C, D])
        raw_qkv = sb(ctx, "raw_qkv", [P, 2 * WQKV2])
        raw_o = sb(ctx, "raw_o", [P, 2 * D])
        raw_moe = sb(ctx, "raw_moe", [P, MGC, 3 * C * P])
        st6 = sb(ctx, "st6", [P, T, 6])
        sm = sb(ctx, "sm", [P, 12, T])
        mid = sb(ctx, "mid", [P, TPB, D])
        mid6 = sb(ctx, "mid6", [P, TPB, 6])
        midst = sb(ctx, "midst", [P, 9, TPB])
        v1 = hs[:, :, :].rearrange("p t d -> p (t d)").rearrange("p (g k n) -> p g k n", g=G1, k=TPB)
        oT1 = acc[:, 0, 0:C * TB].rearrange("p (c t) -> p c t", c=C)
        q1_hl = xT[:, :, :, :, :].rearrange("p b a c t -> p (b a c t)").rearrange("p (g a t) -> p g a t", g=G1, a=2)

        with ExitStack() as first:
            sel_raw = sb(first, "sel_raw", [P, 16 * P])
            xn1 = sb(first, "xn1", [P, 2, TPB, D])
        with ExitStack() as last:
            xn2 = sb(last, "xn2", [P, T, D])
        w2_hl = sb(ctx, "w2_hl", [P, 2, 2 * WQKV2], F32R)
        wo2_hl = sb(ctx, "wo2_hl", [P, 2, 2 * D], F32R)

        with ExitStack() as l1:
            k1_hl = sb(l1, "k1_hl", [P, G1, 2, TB], F32R)
            sel = sb(l1, "sel", [P, 16 * P], F32R)
            with ExitStack() as l0:
                qkv1 = sb(l0, "qkv1", [P, C, 3 * D])
                qkv1_hl = sb(l0, "qkv1_hl", [P, 2, C, 3 * D], F32R)
                xT1 = sb(l0, "xT1", [P, 2, 2, C, TB], F32R)
            v1_pad = sb(l1, "v1_pad", [P, TPB, GH, P])
            p1 = sb(l1, "p1", [P, 2, CAUSAL])
            pT1 = sb(l1, "pT1", [P, CAUSAL])
            stk = sb(l1, "stk", [P, 2, 2, TB], F32R)
            stat1 = sb(l1, "stat1", [P, 3, 2, TPB])
        with ExitStack() as l2:
            qk2 = sb(l2, "qk2", [P, 2, 2, TB], F32R)
            v2 = sb(l2, "v2", [P, 2, 2, TPB, 2 * P], F32R)
            p2 = sb(l2, "p2", [P, 2, CAUSAL])
            pT2 = sb(l2, "pT2", [P, 2, CAUSAL], F32R)
            o2 = sb(l2, "o2", [P, 2, TB], F32R)
            stat2 = sb(l2, "stat2", [P, 3, 2, TPB])
        with ExitStack() as l3:
            moe_hl = sb(l3, "moe_hl", [P, MGC, 2, 3 * C * P], F32R)
            sel_c = sb(l3, "sel_c", [64, MGC, P], F32R)
            sel_f = sb(l3, "sel_f", [64, MG, MGC, P])
            wT = sb(l3, "wT", [64, B * TB], F32R)
            h_s = sb(l3, "h_s", [P, 2, TB])
            h_t = sb(l3, "h_t", [P, 2, TB])
            h_hl = sb(l3, "h_hl", [P, 2, 2, TB], F32R)
            wtok = sb(l3, "wtok", [P, T, E + 2])
            with ExitStack() as logit:
                lgT = sb(logit, "lgT", [2 * E, B * TB])
            rk = sb(l3, "rk", [P, T, E, E], BF16)

        xn_mid = raw_moe[:, :, :].rearrange("p c n -> p (c n)")[:, 0:TPB * D].rearrange("p (j d) -> p j d", j=TPB)
        lg, pr = (raw_o[:, T * E * i:T * E * (i + 1)].rearrange("p (t e) -> p t e", t=T) for i in range(2))

        x_in = [sem(f"x_in{b}") for b in range(B)]
        w1_in = sem("w1_in"); wo1_in = sem("wo1_in"); sel_in = sem("sel_in"); small_in = sem("small_in")
        const = sem("const")
        chain = sem("chain")
        root_in = sem("root_in"); root = sem("root")
        sel_ok = sem("sel_ok")
        pool_met = sem("pool_met")
        ph1_xn = sem("ph1_xn"); ph1_tp = sem("ph1_tp"); ph1_xT = sem("ph1_xT"); ph1_mm = sem("ph1_mm")
        ph1_tlo = sem("ph1_tlo"); ph1_wh = sem("ph1_wh"); ph1_wl = sem("ph1_wl"); ph1_hi = sem("ph1_hi"); ph1_lo = sem("ph1_lo"); ph1_v = sem("ph1_v")
        a1_sel = sem("a1_sel"); a1_stk = sem("a1_stk"); a1_s = sem("a1_s"); a1_max = sem("a1_max")
        a1_exp = sem("a1_exp"); a1_rcp = sem("a1_rcp"); a1_norm = sem("a1_norm"); a1_t = sem("a1_t")
        a1_pta = sem("a1_pta"); a1_ptd = sem("a1_ptd"); a1_pv = sem("a1_pv"); a1_vpad = sem("a1_vpad")
        a1_zero = sem("a1_zero"); a1_o = sem("a1_o")
        m_y = sem("m_y"); m_ys = sem("m_ys"); m_st = sem("m_st"); m_link = sem("m_link"); m_x1 = sem("m_x1")
        m_xna = sem("m_xna"); m_xnd = sem("m_xnd"); m_nrm = sem("m_nrm"); m_ua = sem("m_ua"); m_ud = sem("m_ud"); m_rms = sem("m_rms"); m_hs = sem("m_hs"); m_tp = sem("m_tp"); m_hi = sem("m_hi"); m_lo = sem("m_lo")
        b_rawqkv = sem("b_rawqkv"); b_rawo = sem("b_rawo"); b_wqkv = sem("b_wqkv"); b_wo = sem("b_wo")
        b_qkv = sem("b_qkv"); b_hi = sem("b_hi"); b_lo = sem("b_lo"); b_s = sem("b_s"); b_max = sem("b_max")
        b_exp = sem("b_exp"); b_rcp = sem("b_rcp"); b_norm = sem("b_norm"); b_t = sem("b_t")
        b_pth = sem("b_pth"); b_ptl = sem("b_ptl"); b_pv = sem("b_pv"); b_oh = sem("b_oh"); b_ol = sem("b_ol")
        b_e = sem("b_e"); b_acc = sem("b_acc")
        r_tp = sem("r_tp"); r_hid = sem("r_hid"); r_xn = sem("r_xn"); r_tp2 = sem("r_tp2"); r_hi = sem("r_hi")
        r_sq = sem("r_sq"); r_rms = sem("r_rms"); r_xna = sem("r_xna"); r_lgT = sem("r_lgT"); r_lgl = sem("r_lgl")
        r_row = sem("r_row"); r_lo = sem("r_lo"); r_lg = sem("r_lg"); r_sub = sem("r_sub"); r_exp = sem("r_exp"); r_w = sem("r_w")
        r_tp3 = sem("r_tp3"); r_wh = sem("r_wh"); r_wl = sem("r_wl"); r_gate = sem("r_gate")
        r_sel = sem("r_sel"); r_zero = sem("r_zero")
        e_raw = sem("e_raw"); e_split = sem("e_split"); e_g = sem("e_g"); e_w = sem("e_w"); e_u = sem("e_u")
        e_silu = sem("e_silu"); e_sw = sem("e_sw"); e_h = sem("e_h"); e_hh = sem("e_hh"); e_hlo = sem("e_hlo")
        e_dn = sem("e_dn"); e_acc = sem("e_acc")
        f_last = sem("f_last"); f_tp = sem("f_tp"); f_y = sem("f_y"); f_u = sem("f_u"); f_nrm = sem("f_nrm"); f_out = sem("f_out")
        stored = sem("stored")
        b_half = sem("b_half"); b_acc0 = sem("b_acc0"); e_half = sem("e_half"); e_sel = sem("e_sel"); gate_ok = sem("gate_ok"); gate_lo = sem("gate_lo"); gate_in = sem("gate_in")
        fence = [sem(f"fence{i}") for i in range(3)]

        def meet(eng, i):
            eng.drain().then_inc(fence[i], 1)
            eng.wait_ge(fence[i], 5)

        S1_BANK, S1_COL = (0, 1, 2, 2), (0, 0, 0, 2 * P)
        PT1_BANK, STK_BANK, O1_BANK = (3, 4), (5, 6), 7

        def s1(t):
            return bank[S1_BANK[t]][:, S1_COL[t]:S1_COL[t] + P * (TPB - t)]

        def s2(t):
            return bank[t][:, 0:P * (TPB - t)]

        def v2_half(k, part):
            j = 2 - 2 * (k % 2)
            return v2[:, k // 2 % 2, part, j:j + 2, :].rearrange("p j n -> p (j n)")

        def pool_wait(pool, sem_, value):
            pool.wait_ge(sem_, value)
            if not isinstance(value, int):
                pool.sem_inc(pool_met, 1)

        def f32(ap):
            return ap.bitcast(F32)

        def batch_tiles(ap, batch, extra, j, n=1):
            return ap[:, ds(batch * TPB + (extra * TPB + j), n), :].rearrange("p j d -> p (j d)")

        block = ctx.enter_context(nc.Block())
        PER1 = 2 * GH
        MID_Y = (1, 3)
        MID_X1, MID_U = 4, 6
        MID_STAT = 8
        MID_RMS, MID_XN = 8, 11
        MID_HS = (12, 15)
        MID_T = 13
        LAST_Y_BANK = (7, 3)
        LAST_U, LAST_STAT, LAST_XN, LAST_HS, LAST_T = 0, 1, 3, (4, 5), (4, 5)
        PAIRS1 = GH // 2
        N1 = G1 * GH
        PER2 = 2 * B
        N2 = H2 * B
        PER3 = B * MGC
        NE = MG * PER3
        SHC = 2 * EI // P
        SHU = SHC * B
        u_out = xn2

        def place(k):
            if k < SHU:
                b, r, w = k // SHC, k % SHC, SHC
                return b, r, r == 0, r == w - 1, b
            if k < PER3:
                w = MGC - SHC
                b, r = (k - SHU) // w, (k - SHU) % w
                return b, SHC + r, r == 0, r == w - 1, B + b
            b, r = k % PER3 // MGC, k % MGC
            return b, r, r == 0, r == MGC - 1, B * (1 + k // PER3) + b

        @block.sync
        def _(sp):
            for b in range(B):
                sp.dma_start(x_sb[:, TPB * b:TPB * (b + 1), :],
                             x_d[b].rearrange("(j p) d -> p j d", p=P)).then_inc(x_in[b], 16)
                if b == 0:
                    sp.dma_start(qkv1[:, :, :], qkv1_d).then_inc(w1_in, 16)
            sp.dma_start(sel_raw[:, :], stack_d).then_inc(sel_in, 16)
            sp.dma_start(wo1[:, :, :], wo1_d).then_inc(wo1_in, 16)
            sp.dma_start(ln_w[:, :, :], ln_w_d).then_inc(small_in, 16)
            sp.dma_start(gate_raw[:, :, :], gate_d).then_inc(gate_in, 16)
            sp.dma_start(raw_qkv[:, :], qkvo2_d[0, :, 0:2 * WQKV2]).then_inc(b_rawqkv, 16)
            sp.dma_start(raw_o[:, :], qkvo2_d[0, :, 2 * WQKV2:]).then_inc(b_rawo, 16)
            meet(sp, 0)
            meet(sp, 1)
            sp.wait_ge(m_tp, C * B)
            sp.dma_start(raw_moe[:, :, :], moe_d[0]).then_inc(e_raw, 16)
            with sp.Fori(1, H2 // 2) as h:
                sp.wait_ge(b_wqkv, h * 3)
                sp.dma_start(raw_qkv[:, :], qkvo2_d[ds(h, 1), :, 0:2 * WQKV2].rearrange("a p n -> p (a n)"))\
                    .then_inc(b_rawqkv, 16)
                sp.wait_ge(b_wo, h * 1)
                sp.dma_start(raw_o[:, :], qkvo2_d[ds(h, 1), :, 2 * WQKV2:].rearrange("a p n -> p (a n)"))\
                    .then_inc(b_rawo, 16)
            meet(sp, 2)
            with sp.Fori(1, MG) as g:
                sp.wait_ge(e_split, g * MGC)
                sp.dma_start(raw_moe[:, :, :], moe_d[ds(g, 1)].rearrange("a p c n -> p (a c) n"))\
                    .then_inc(e_raw, 16)
            for b in range(B):
                if b < B - 1:
                    sp.wait_ge(f_out, b + 1)
                else:
                    sp.wait_ge(f_last, 1)
                sp.dma_start(out_d[b].rearrange("(j p) d -> p j d", p=P),
                             u_out[:, TPB * b:TPB * (b + 1), :]).then_inc(stored, 16)
            sp.wait_ge(stored, 16 * B)

        @block.gpsimd
        def _(pool):
            pool.memset(ident[:, :], 0.0).then_inc(const, 1)
            pool.memset(mask_f[:, :], 0.0).then_inc(const, 1)
            pool.wait_ge(const, 2)
            pool.affine_select(out=ident[:, :], in_=ident[:, :], compare_op=ALU.not_equal, fill=1.0, base=0,
                               pattern=[[-1, P]], channel_multiplier=1).then_inc(const, 1)
            pool.affine_select(out=mask_f[:, :], in_=mask_f[:, :], compare_op=ALU.is_ge, fill=MASKED, base=0,
                               pattern=[[-1, P]], channel_multiplier=1).then_inc(const, 1)
            pool.wait_ge(const, 4)
            pool.tensor_copy(ident_b[:, :], ident[:, :]).then_inc(const, 1)
            pool.tensor_copy(mask_b[:, :], mask_f[:, :]).then_inc(const, 1)
            for i, cols in enumerate((slice(0, 2 * D), slice(2 * D, 3 * D))):
                pool.wait_ge(ph1_wh, i + 1)
                pool.tensor_tensor(qkv1_hl[:, LO, :, cols], qkv1[:, :, cols], f32(qkv1_hl[:, HI, :, cols]),
                                   ALU.subtract).then_inc(ph1_wl, 1)
            meet(pool, 0)
            pool.memset(v1_pad[:, :, :, :], 0.0).then_inc(a1_zero, 1)
            pool.wait_ge(a1_zero, 1)

            def fill_v(g, head):
                pool.tensor_copy(v1_pad[:, :, head, DH1 * head:DH1 * (head + 1)],
                                 v1[:, g, :, DH1 * head:DH1 * (head + 1)]).then_inc(a1_vpad, 1)

            for head in range(GH):
                fill_v(0, head)

            def split2(raw, hi, lo, count, done):
                pool.tensor_copy(hi, raw).then_inc(b_half, 1)
                pool_wait(pool, b_half, count)
                pool.tensor_tensor(lo, raw, f32(hi), ALU.subtract).then_inc(done, 1)

            def split_qk(head, count):
                split2(*(w[:, 0:4 * C * P].rearrange("p (i h n) -> p i h n", i=2, h=2)[:, :, head, :]
                         for w in (raw_qkv, w2_hl[:, HI], w2_hl[:, LO])), count, b_wqkv)

            def split_v(count):
                split2(raw_qkv[:, 4 * C * P:], w2_hl[:, HI, 4 * C * P:], w2_hl[:, LO, 4 * C * P:], count, b_wqkv)

            def split_o(count):
                split2(raw_o[:, :], wo2_hl[:, HI, :], wo2_hl[:, LO, :], count, b_wo)

            pool_wait(pool, b_rawqkv, 16)
            split_qk(0, 1)
            split_v(2)
            split_qk(1, 3)
            pool_wait(pool, b_rawo, 16)
            split_o(4)

            links = [0]
            LINKS = 65

            def link(batch, extra, *instructions):
                for ins in instructions:
                    ins.then_inc(m_link, 1)
                links[0] += len(instructions)
                pool_wait(pool, m_link, batch * LINKS + (extra * LINKS + links[0]))

            mean, rstd, dif, var, tmp, rr, offset, scale2, offset2 = (midst[:, i, :] for i in range(9))

            def rsqrt(batch, extra, dst):
                link(batch, extra, pool.tensor_scalar(dst.bitcast(I32), var.bitcast(I32), -0.5, ROOT_GUESS,
                                                      ALU.mult, ALU.add))
                for _ in range(3):
                    link(batch, extra, pool.tensor_tensor(tmp, dst, dst, ALU.mult))
                    link(batch, extra, pool.tensor_tensor(tmp, tmp, var, ALU.mult))
                    link(batch, extra, pool.tensor_scalar(tmp, tmp, -0.5, 1.5, ALU.mult, ALU.add))
                    link(batch, extra, pool.tensor_tensor(dst, dst, tmp, ALU.mult))

            def row_stats(batch, extra):
                link(batch, extra, pool.tensor_tensor(mean, mid6[:, :, 1], mid6[:, :, 4], ALU.add),
                     pool.tensor_tensor(dif, mid6[:, :, 1], mid6[:, :, 4], ALU.subtract),
                     pool.tensor_tensor(var, mid6[:, :, 2], mid6[:, :, 5], ALU.add))
                link(batch, extra, pool.tensor_tensor(dif, dif, dif, ALU.mult),
                     pool.tensor_scalar(mean, mean, 0.5, None, ALU.mult))
                link(batch, extra, pool.tensor_scalar(dif, dif, D / 4.0, None, ALU.mult))
                link(batch, extra, pool.tensor_tensor(var, var, dif, ALU.add))
                link(batch, extra, pool.tensor_scalar(var, var, 1.0 / D, LN_EPS, ALU.mult, ALU.add))
                rsqrt(batch, extra, rstd)

            def norm_y(batch, extra):
                links[0] = 0
                pool_wait(pool, m_st, batch * (2 * TPB) + (extra * 2 * TPB + TPB))
                row_stats(batch, extra)
                link(batch, extra, pool.tensor_tensor(offset, mean, rstd, ALU.mult))
                pool.tensor_scalar(offset, offset, -1.0, None, ALU.mult).then_inc(m_nrm, 1)

            def make_x1(batch, extra):
                for half_done in (m_ua, m_ud):
                    pool_wait(pool, half_done, batch * 2 + (extra * 2 + 2))
                x1, mid_ = batch_tiles(x_sb, batch, extra, 0, TPB), mid[:, :, :].rearrange("p j d -> p (j d)")
                pool.tensor_tensor(mid_, x1, mid_, ALU.add).then_inc(m_x1, 1)
                pool_wait(pool, m_x1, batch + (extra + 1))
                link(batch, extra, pool.tensor_copy(x1, mid_))

            def norm_x1(batch, extra):
                pool_wait(pool, m_st, batch * (2 * TPB) + (extra * 2 * TPB + 2 * TPB))
                row_stats(batch, extra)
                link(batch, extra, pool.tensor_tensor(tmp, rstd, rstd, ALU.mult),
                     pool.tensor_scalar(var, var, -LN_EPS, None, ALU.add),
                     pool.tensor_tensor(offset, mean, rstd, ALU.mult))
                link(batch, extra, pool.tensor_tensor(var, var, tmp, ALU.mult),
                     pool.tensor_scalar(offset, offset, -1.0, None, ALU.mult))
                link(batch, extra, pool.tensor_scalar(var, var, RMS_EPS, None, ALU.add))
                rsqrt(batch, extra, rr)
                link(batch, extra, pool.tensor_tensor(scale2, rstd, rr, ALU.mult))
                link(batch, extra, pool.tensor_tensor(offset2, offset, rr, ALU.mult))
                pool.sem_inc(m_rms, 1)
                assert links[0] == LINKS, links[0]

            def step1(it, k):
                n = it * PER1 + k
                static = isinstance(n, int)
                if not static or (n >= 2 and n + GH - 2 < N1):
                    pool_wait(pool, a1_pv, (n - 1) * TPB)
                    fill_v(it * 2 + (k + GH - 2) // GH, (k - 2) % GH)
                if k >= PER1 and k % PER1 == MID_X1:
                    norm_y(it, k // PER1 - 1)
                    make_x1(it, k // PER1 - 1)
                if k >= PER1 and k % PER1 == MID_RMS:
                    norm_x1(it, k // PER1 - 1)

            run_steps(pool, step1, N1, PER1, PER1 + 2, GH - 2)
            meet(pool, 1)
            norm_y(B - 1, 0)
            pool.wait_ge(m_y, 2 * B)
            pool.memset(acc[:, :, :], 0.0).then_inc(b_acc0, 1)
            make_x1(B - 1, 0)
            norm_x1(B - 1, 0)
            def step2(it, k):
                n = it * PER2 + k
                static = isinstance(n, int)
                if static and n >= N2 + 2:
                    return
                if k % PER2 == PER2 - 2 and (not static or n + 2 < N2):
                    pair = it + (k + 2) // PER2
                    pool_wait(pool, b_rawqkv, pair * 16 + 16)
                    pool_wait(pool, b_qkv, n * 3 + 2)
                    split_qk(0, pair * 4 + 1)
                if k % PER2 == PER2 - 1 and (not static or n + 1 < N2):
                    pair = it + (k + 1) // PER2
                    pool_wait(pool, b_qkv, n * 3 + 3)
                    split_v(pair * 4 + 2)
                    split_qk(1, pair * 4 + 3)
                if k % PER2 == 1 and (not static or PER2 < n < N2):
                    pair = it + k // PER2
                    pool_wait(pool, b_rawo, pair * 16 + 16)
                    pool_wait(pool, b_e, (n - 1) * C)
                    split_o(pair * 4 + 4)

            run_steps(pool, step2, N2, PER2, 2, 2)
            meet(pool, 2)

            pool.memset(f32(wT[:, :]), 0.0).then_inc(r_zero, 1)

            def split_moe(c, count):
                pool_wait(pool, e_half, count)
                pool.tensor_tensor(moe_hl[:, c, LO, :], raw_moe[:, c, :], f32(moe_hl[:, c, HI, :]),
                                   ALU.subtract).then_inc(e_split, 1)

            def take_rows(g, c):
                pool.tensor_copy(sel_c[:, c, :], sel_f[:, g, c, :]).then_inc(e_sel, 1)

            def all_rows(g0, g1):
                pool.memset(sel_f[:, g0:g1, :, :], 1.0).then_inc(r_sel, 1)

            def bound_rows(g0, g1, half, first_edge, count):
                pool.wait_ge(r_sel, count)
                part = sel_f[32 * half:32 * half + 32, g0:g1, :, :].rearrange("p g c n -> p (g c n)")
                skipped = g0 * MGC * P
                base, sign = (skipped, 1) if first_edge else (EI - 1 - skipped, -1)
                pool.affine_select(out=part, in_=part, compare_op=ALU.is_ge, fill=0.0, base=base,
                                   pattern=[[sign, (g1 - g0) * MGC * P]], channel_multiplier=-sign * EI)\
                    .then_inc(r_sel, 1)

            pool_wait(pool, e_raw, 16)
            for c in range(SHC):
                split_moe(c, c + 1)
            pool.wait_ge(r_tp, T // 2)
            pool.memset(acc[:, :, :], 0.0).then_inc(r_zero, 1)
            all_rows(0, 1)
            for i in range(4):
                bound_rows(0, 1, i // 2, i % 2 == 0, i + 1)
            pool.wait_ge(r_sel, 5)
            for c in range(SHC, MGC):
                take_rows(0, c)

            def step3(it, k):
                n = it * PER3 + k
                static = isinstance(n, int)
                if not static or n < NE:
                    pool_wait(pool, e_hh, n + 1)
                    pool.tensor_tensor(h_hl[:, k % 2, LO, :], h_t[:, k % 2, :], f32(h_hl[:, k % 2, HI, :]),
                                       ALU.subtract).then_inc(e_hlo, 1)
                if static and n == 0:
                    all_rows(1, MG)
                if static and 1 <= n <= 4:
                    pool.wait_ge(e_hlo, n + 1)
                    bound_rows(1, MG, (n - 1) // 2, n % 2 == 1, n + 5)
                    pool.wait_ge(r_sel, n + 6)
                if static and 5 <= n < 5 + MGC - SHC:
                    split_moe(n - 5 + SHC, n - 5 + SHC + 1)
                m = k - 2
                if m >= 0 and m % PER3 >= PER3 - MGC and (not static or it + m // PER3 + 1 < MG):
                    c = m % MGC
                    pool_wait(pool, e_raw, it * 16 + 16 * (m // PER3 + 2))
                    pool_wait(pool, e_dn, (n - 1) * C)
                    take_rows(it + (m // PER3 + 1), c)
                    split_moe(c, it * MGC + (MGC * (m // PER3 + 1) + c + 1))

            run_steps(pool, step3, NE + 2, PER3, PER3 + 2, 4)
            for b in range(B - 1):
                pool.wait_ge(f_u, TPB * (b + 1))
                tiles = slice(TPB * b, TPB * (b + 1))
                pool.tensor_tensor(u_out[:, tiles, :], u_out[:, tiles, :], x_sb[:, tiles, :], ALU.add)\
                    .then_inc(f_out, 1)

        @block.scalar
        def _(act):
            roots = [0]

            def take_root(cols=slice(0, T)):
                roots[0] += 1
                act.wait_ge(root_in, roots[0])
                act.activation(sm[:, 5, cols], sm[:, 3, cols], ACT.Sqrt).then_inc(root, 1)

            def load_root_table():
                act.activation(sm[:, 11, 0:1], ident[:, 0:1], ACT.Sqrt)

            def take_xT1(b):
                for c in range(C):
                    act.wait_ge(ph1_tp, b * C + (c + 1))
                    if b >= 2:
                        act.wait_ge(ph1_mm, (b - 1) * 6)
                    act.activation(xT1[:, b % 2, HI, c, :], bank[c][:, :], ACT.Copy).then_inc(ph1_xT, 1)

            take_root(slice(0, TPB))
            act.wait_ge(w1_in, 16)
            for cols in (slice(0, 2 * D), slice(2 * D, 3 * D)):
                act.activation(qkv1_hl[:, HI, :, cols], qkv1[:, :, cols], ACT.Copy).then_inc(ph1_wh, 1)
            take_xT1(0)
            take_root(slice(TPB, T))
            for b in range(B):
                for m in range(4):
                    dst, scale = (q1_hl, SCALE1) if m < 2 else (k1_hl, 1.0)
                    act.wait_ge(ph1_mm, b * 6 + (m + 1))
                    act.activation(dst[:, b * 2 + m % 2, HI, :], bank[2 + m][:, :], ACT.Copy, scale=scale)\
                       .then_inc(ph1_hi, 1)
                if b == 0:
                    act.wait_ge(sel_in, 16)
                    act.activation(sel[:, :], sel_raw[:, :], ACT.Copy).then_inc(sel_ok, 1)
                if b + 1 < B:
                    take_xT1(b + 1)
                else:
                    act.wait_ge(gate_in, 16)
                    act.activation(gate_hl[:, :, HI, :], gate_raw[:, :, :], ACT.Copy).then_inc(gate_ok, 1)
                for i in range(2):
                    act.wait_ge(ph1_mm, b * 6 + (5 + i))
                    for c in range(C):
                        ins = act.activation(
                            v1[:, b * 2 + c, 2 * i:2 * i + 2, :],
                            bank[6 + i][:, :].rearrange("p (j c n) -> p c j n", j=2, c=C)[:, c], ACT.Copy)
                    ins.then_inc(ph1_v, 1)
            meet(act, 0)

            def take_stack(m_par, count):
                for w in range(2):
                    act.wait_ge(a1_sel, count + w + 1)
                    act.activation(stk[:, m_par, w, :], bank[STK_BANK[w]][:, :], ACT.Copy).then_inc(a1_stk, 1)

            def take_y(batch, extra, half, bank_):
                act.wait_ge(m_y, batch * 2 + (extra * 2 + half + 1))
                if half == 0 and (not isinstance(batch, int) or batch + extra):
                    act.wait_ge(m_hs, batch * TPB + extra * TPB)
                act.activation(mid[:, 2 * half:2 * half + 2, :].rearrange("p j d -> p (j d)"), bank_[:, :], ACT.Copy)\
                   .then_inc(m_ys, 1)

            def scale_u(batch, extra):
                act.wait_ge(m_nrm, batch + (extra + 1))
                for j in (0, 1):
                    act.activation(mid[:, j, :], mid[:, j, :], ACT.Identity, bias=midst[:, 6, j:j + 1],
                                   scale=midst[:, 1, j:j + 1]).then_inc(m_ua, 1)

            def scale_xn(batch, extra):
                act.wait_ge(m_rms, batch + (extra + 1))
                for j in (0, 1):
                    act.activation(xn_mid[:, j, :], mid[:, j, :], ACT.Identity, bias=midst[:, 8, j:j + 1],
                                   scale=midst[:, 7, j:j + 1]).then_inc(m_xna, 1)

            def scale_hs(batch, extra, half):
                for j in (2 * half, 2 * half + 1):
                    act.activation(batch_tiles(hs, batch, extra, j), mid[:, j, :], ACT.Identity,
                                   bias=midst[:, 6, j:j + 1], scale=midst[:, 1, j:j + 1]).then_inc(m_hs, 1)

            def take_xT(batch, extra, banks):
                for c in banks:
                    act.wait_ge(m_tp, batch * C + (extra * C + c + 1))
                    act.activation(xT[:, ds(batch + extra, 1), HI, c, :].rearrange("p a t -> p (a t)"),
                                   bank[banks[c]][:, :], ACT.Copy, scale=ln_w[:, 0, c:c + 1]).then_inc(m_hi, 1)

            act.wait_ge(small_in, 16)

            def step1(it, k):
                n = it * PER1 + k
                static = isinstance(n, int)
                if static and n == 0:
                    take_stack(0, 0)

                def exp(t):
                    qi = TPB - 1 - t
                    act.wait_ge(a1_max, n * TPB + (t + 1 if t < 2 else TPB))
                    if t == 0 and (not static or n >= 2):
                        act.wait_ge(a1_t, (n - 1) * TPB)
                    act.activation(p1[:, k % 2, POFF[qi]:POFF[qi + 1]], s1(t), ACT.Exp,
                                   bias=stat1[:, 0, k % 2, t:t + 1],
                                   accum_out=stat1[:, 1, k % 2, t:t + 1]).then_inc(a1_exp, 1)

                def take_pt(t):
                    kj = TPB - 1 - t
                    act.wait_ge(a1_t, n * TPB + (t + 1 - TPB))
                    if not static or n >= 2:
                        act.wait_ge(a1_pv, n * TPB + (t + 1 - 2 * TPB))
                    act.activation(pT1[:, QOFF[kj]:QOFF[kj + 1]], bank[PT1_BANK[t % 2]][:, 0:TB - P * kj], ACT.Copy)\
                       .then_inc(a1_pta, 1)

                softmax, values = not static or n < N1, not static or n >= 1
                if values:
                    take_pt(1)
                if softmax:
                    exp(0)
                    exp(1)
                if values:
                    take_pt(3)
                if softmax:
                    exp(2)
                    exp(3)
                if k % 2 == 0 and (not static or n // 2 + 1 < N1 // 2):
                    if not static or n >= 2:
                        act.wait_ge(a1_s, n * TPB)
                    take_stack((k // 2 + 1) % 2, n + 2)
                if k >= PER1 and k % PER1 in MID_Y:
                    half = MID_Y.index(k % PER1)
                    take_y(it, k // PER1 - 1, half, bank[STK_BANK[half]])
                if k >= PER1 and k % PER1 == MID_U:
                    scale_u(it, k // PER1 - 1)
                if k >= PER1 and k % PER1 == MID_XN:
                    scale_xn(it, k // PER1 - 1)
                if k >= PER1 and k % PER1 in MID_HS:
                    scale_hs(it, k // PER1 - 1, MID_HS.index(k % PER1))
                if k >= PER1 and k % PER1 == MID_T:
                    take_xT(it, k // PER1 - 1, dict(enumerate(STK_BANK)))

            run_steps(act, step1, N1 + 1, PER1, PER1 + 2, 5)
            meet(act, 1)
            for half in range(2):
                take_y(B - 1, 0, half, bank[LAST_Y_BANK[half]])
            def step2(it, k):
                n = it * PER2 + k
                static = isinstance(n, int)
                here, prev = not static or n < N2, not static or 1 <= n <= N2
                if here:
                    for i in range(3):
                        act.wait_ge(b_qkv, n * 3 + (i + 1))
                        if i == 0 and (not static or n >= 1):
                            act.wait_ge(b_s, n * TPB)
                        if i == 2 and k % 2 == 0 and (not static or n >= 4):
                            act.wait_ge(b_pv, (n - 2) * TPB)
                        dst = v2_half(k, HI) if i == 2 else qk2[:, i, HI, :]
                        act.activation(dst, bank[4 + i][:, :], ACT.Copy, scale=(SCALE2 if i == 0 else 1.0))\
                           .then_inc(b_hi, 1)
                if prev:
                    for t in range(TPB):
                        kj = TPB - 1 - t
                        act.wait_ge(b_t, n * TPB + (t + 1 - TPB))
                        if not static or n >= 2:
                            act.wait_ge(b_pv, n * TPB + (t + 1 - 2 * TPB))
                        act.activation(pT2[:, HI, QOFF[kj]:QOFF[kj + 1]], bank[t][:, 0:TB - P * kj],
                                       ACT.Copy).then_inc(b_pth, 1)
                if here:
                    for t in range(TPB):
                        qi = TPB - 1 - t
                        act.wait_ge(b_max, n * TPB + (t + 1))
                        if t == 0 and (not static or n >= 2):
                            act.wait_ge(b_t, (n - 1) * TPB)
                        act.activation(p2[:, k % 2, POFF[qi]:POFF[qi + 1]], s2(t),
                                       ACT.Exp, bias=stat2[:, 0, k % 2, t:t + 1],
                                       accum_out=stat2[:, 1, k % 2, t:t + 1]).then_inc(b_exp, 1)
                    act.wait_ge(b_rcp, n + 1)
                    for t in range(TPB):
                        qi = TPB - 1 - t
                        pt = p2[:, k % 2, POFF[qi]:POFF[qi + 1]]
                        act.activation(pt, pt, ACT.Copy, scale=stat2[:, 2, k % 2, t:t + 1]).then_inc(b_norm, 1)
                if prev:
                    act.wait_ge(b_pv, n * TPB)
                    if not static or n >= 2:
                        act.wait_ge(b_e, (n - 1) * C)
                    act.activation(o2[:, HI, :], bank[7][:, :], ACT.Copy).then_inc(b_oh, 1)
                if static and n == LAST_U:
                    scale_u(B - 1, 0)
                if static and n == LAST_XN:
                    scale_xn(B - 1, 0)
                if static and n in LAST_HS:
                    scale_hs(B - 1, 0, LAST_HS.index(n))
                if static and n in LAST_T:
                    take_xT(B - 1, 0, {LAST_T.index(n): 6})

            run_steps(act, step2, N2 + 2, PER2, 6, 4)
            meet(act, 2)
            def moe_hi(c):
                act.activation(moe_hl[:, c, HI, :], raw_moe[:, c, :], ACT.Copy).then_inc(e_half, 1)

            load_root_table()
            act.wait_ge(e_raw, 16)
            for c in range(SHC):
                moe_hi(c)
            for i in range(T):
                act.wait_ge(r_hid, i // 2 + 1)
                act.activation(xn2[:, i, :], hs[:, i, :], ACT.Square, accum_out=sm[:, 10, i:i + 1]).then_inc(r_sq, 1)
            take_root()
            act.wait_ge(r_rms, 1)
            act.wait_ge(r_sq, T)

            def norm_half(b):
                for i in (TPB * b + 2, TPB * b + 3):
                    act.activation(xn2[:, i, :], hs[:, i, :], ACT.Copy, scale=sm[:, 1, i:i + 1]).then_inc(r_xna, 1)

            def take_xT(b):
                for c in range(C):
                    act.wait_ge(r_tp2, b * C + c + 1)
                    act.activation(xT[:, b, HI, c, :], bank[b * C + c][:, :], ACT.Copy,
                                   scale=ln_w[:, 1, c:c + 1]).then_inc(r_hi, 1)

            for b in range(B):
                norm_half(b)
                if b:
                    take_xT(b - 1)
            take_xT(B - 1)

            def take_weights(b):
                act.wait_ge(r_tp3, b + 1)
                act.activation(wT[0:E + 2, TB * b:TB * (b + 1)], bank[4 if b == 0 else 5][0:E + 2, :], ACT.Copy)\
                   .then_inc(r_wh, 1)

            def step3(it, k):
                n = it * PER3 + k
                static = isinstance(n, int)
                m = k - 2
                if m >= 0 and m % PER3 >= PER3 - MGC and (not static or it + m // PER3 + 1 < MG):
                    act.wait_ge(e_raw, it * 16 + 16 * (m // PER3 + 2))
                    act.wait_ge(e_dn, (n - 1) * C)
                    moe_hi(m % MGC)
                if static and n >= NE:
                    return
                act.wait_ge(e_g, n + 1)
                act.activation(h_s[:, k % 2, :], bank[k % 2][:, :], ACT.Silu).then_inc(e_silu, 1)
                if static and n < B // 2:
                    for b in (2 * n, 2 * n + 1):
                        act.wait_ge(r_row, b + 1)
                        act.activation(lgT[:, TB * b:TB * (b + 1)], bank[4 + b % 2][0:2 * E, :], ACT.Copy)\
                           .then_inc(r_lgT, 1)
                act.wait_ge(e_h, n + 1)
                if not static or n >= 2:
                    act.wait_ge(e_dn, (n - 1) * C)
                act.activation(h_hl[:, k % 2, HI, :], h_t[:, k % 2, :], ACT.Copy).then_inc(e_hh, 1)
                if static and 2 <= n < 2 + MGC - SHC:
                    moe_hi(n - 2 + SHC)
                if static and n == 1:
                    act.wait_ge(r_lg, 1)
                    act.activation(pr[:, :, :], bank[5][:, :].rearrange("p (t a e) -> p t a e", t=T, a=2)[:, :, 1, :],
                                   ACT.Copy).then_inc(r_lgl, 1)
                    act.wait_ge(r_sub, 1)
                    act.activation(pr[:, :, :], lg[:, :, :], ACT.Exp).then_inc(r_exp, 1)
                if static and n == SHU - 1:
                    act.wait_ge(r_zero, 1)
                    take_weights(0)
                    take_weights(1)
                if static and SHU <= n < SHU + B - 2:
                    take_weights(n - SHU + 2)

            run_steps(act, step3, NE, PER3, PER3 + 2, 3)
            take_root(slice(0, TPB * (B - 1)))
            act.wait_ge(f_nrm, 1)
            for i in range(TPB * (B - 1)):
                act.activation(u_out[:, i, :], hs[:, i, :], ACT.Identity, bias=sm[:, 7, i:i + 1],
                               scale=sm[:, 1, i:i + 1]).then_inc(f_u, 1)
            take_root(slice(TPB * (B - 1), T))

        @block.vector
        def _(dve):
            links = [0]

            def link(*instructions):
                for ins in instructions:
                    ins.then_inc(chain, 1)
                links[0] += len(instructions)
                dve.wait_ge(chain, links[0])

            roots = [0]
            mean, rstd, dif, var, tmp, rt, sq = (sm[:, i, :] for i in (0, 1, 2, 3, 4, 5, 6))

            def rsqrt(dst, cols):
                roots[0] += 1
                dve.wait_ge(root, roots[0])
                link(dve.reciprocal(dst[:, cols], rt[:, cols]))
                link(dve.tensor_tensor(tmp[:, cols], dst[:, cols], dst[:, cols], ALU.mult))
                link(dve.tensor_tensor(tmp[:, cols], tmp[:, cols], var[:, cols], ALU.mult))
                link(dve.tensor_scalar(tmp[:, cols], tmp[:, cols], -0.5, 1.5, ALU.mult, ALU.add))
                link(dve.tensor_tensor(dst[:, cols], dst[:, cols], tmp[:, cols], ALU.mult))

            def row_stats(eps, square_mean=False, cols=slice(0, T)):
                mean_, dif_, var_, sq_, st = (a[:, cols] for a in (mean, dif, var, sq, st6))
                link(dve.tensor_tensor(mean_, st[:, :, 1], st[:, :, 4], ALU.add),
                     dve.tensor_tensor(dif_, st[:, :, 1], st[:, :, 4], ALU.subtract),
                     dve.tensor_tensor(var_, st[:, :, 2], st[:, :, 5], ALU.add))
                link(dve.tensor_tensor(dif_, dif_, dif_, ALU.mult),
                     dve.tensor_scalar(mean_, mean_, 0.5, None, ALU.mult))
                link(dve.scalar_tensor_tensor(var_, dif_, D / 4.0, var_, ALU.mult, ALU.add),
                     dve.tensor_tensor(sq_, mean_, mean_, ALU.mult))
                if square_mean:
                    link(dve.tensor_scalar(var_, var_, 1.0 / D, eps, ALU.mult, ALU.add))
                    dve.tensor_tensor(var_, var_, sq_, ALU.add).then_inc(root_in, 1)
                else:
                    dve.tensor_scalar(var_, var_, 1.0 / D, eps, ALU.mult, ALU.add).then_inc(root_in, 1)
                rsqrt(rstd, cols)

            def tile_stats(src):
                link(*[dve.bn_stats(st6[:, i, :], src[:, i, :]) for i in range(T)])

            def load_stats(b):
                dve.wait_ge(x_in[b], 16)
                link(*[dve.bn_stats(st6[:, i, :], x_sb[:, i, :]) for i in range(TPB * b, TPB * (b + 1))])

            def norm(b):
                if b >= 2:
                    dve.wait_ge(ph1_tp, (b - 1) * C)
                for j in range(TPB):
                    i = b * TPB + j
                    dve.tensor_scalar(xn1[:, b % 2, j, :], x_sb[:, i, :], mean[:, i:i + 1], rstd[:, i:i + 1],
                                      ALU.subtract, ALU.mult).then_inc(ph1_xn, 1)

            load_stats(0)
            row_stats(LN_EPS, cols=slice(0, TPB))
            norm(0)
            for b in range(B):
                for c in range(C):
                    dve.wait_ge(ph1_xT, b * C + (c + 1))
                    dve.tensor_tensor(xT1[:, b % 2, LO, c, :], bank[c][:, :], f32(xT1[:, b % 2, HI, c, :]),
                                      ALU.subtract).then_inc(ph1_tlo, 1)
                if b == 0:
                    for later_b in range(1, B):
                        load_stats(later_b)
                    row_stats(LN_EPS, cols=slice(TPB, T))
                if b + 1 < B:
                    norm(b + 1)
                for m in range(4):
                    dst, scale = (q1_hl, SCALE1) if m < 2 else (k1_hl, 1.0)
                    dve.wait_ge(ph1_hi, b * 4 + (m + 1))
                    dve.scalar_tensor_tensor(dst[:, b * 2 + m % 2, LO, :], bank[2 + m][:, :], scale,
                                             f32(dst[:, b * 2 + m % 2, HI, :]), ALU.mult, ALU.subtract)\
                       .then_inc(ph1_lo, 1)
            dve.wait_ge(gate_ok, 1)
            dve.tensor_tensor(gate_hl[:, :, LO, :], gate_raw[:, :, :], f32(gate_hl[:, :, HI, :]), ALU.subtract)\
               .then_inc(gate_lo, 1)
            meet(dve, 0)

            def mid_stats(half):
                for j in (2 * half, 2 * half + 1):
                    dve.bn_stats(mid6[:, j, :], mid[:, j, :]).then_inc(m_st, 1)

            def y_stats(batch, extra, half):
                dve.wait_ge(m_ys, batch * 2 + (extra * 2 + half + 1))
                mid_stats(half)

            def x1_stats(batch, extra):
                dve.wait_ge(m_x1, batch + (extra + 1))
                mid_stats(0)
                mid_stats(1)

            def scale_u(batch, extra):
                dve.wait_ge(m_nrm, batch + (extra + 1))
                for j in (2, 3):
                    dve.tensor_scalar(mid[:, j, :], mid[:, j, :], midst[:, 1, j:j + 1], midst[:, 6, j:j + 1],
                                      ALU.mult, ALU.add).then_inc(m_ud, 1)

            def scale_xn(batch, extra):
                dve.wait_ge(m_rms, batch + (extra + 1))
                for j in (2, 3):
                    dve.tensor_scalar(xn_mid[:, j, :], mid[:, j, :], midst[:, 7, j:j + 1], midst[:, 8, j:j + 1],
                                      ALU.mult, ALU.add).then_inc(m_xnd, 1)

            def take_xT(batch, extra, banks):
                for c in banks:
                    dve.wait_ge(m_hi, batch * C + (extra * C + c + 1))
                    hi, lo = (xT[:, ds(batch + extra, 1), a, c, :].rearrange("p a t -> p (a t)") for a in (HI, LO))
                    dve.scalar_tensor_tensor(lo, bank[banks[c]][:, :], ln_w[:, 0, c:c + 1], f32(hi),
                                             ALU.mult, ALU.subtract).then_inc(m_lo, 1)

            dve.wait_ge(small_in, 16)

            def step1(it, k):
                n = it * PER1 + k
                static = isinstance(n, int)
                softmax, values = not static or n < N1, not static or n >= 1

                def row_max(t):
                    qi = TPB - 1 - t
                    dve.wait_ge(a1_s, n * TPB + (t + 1 if t < 2 else TPB))
                    dve.tensor_reduce(stat1[:, 0, k % 2, t:t + 1], s1(t), AX.X, ALU.max,
                                      negate=True).then_inc(a1_max, 1)

                def take_pt(t):
                    kj = TPB - 1 - t
                    dve.wait_ge(a1_t, n * TPB + (t + 1 - TPB))
                    if not static or n >= 2:
                        dve.wait_ge(a1_pv, n * TPB + (t + 1 - 2 * TPB))
                    dve.tensor_copy(pT1[:, QOFF[kj]:QOFF[kj + 1]], bank[PT1_BANK[t % 2]][:, 0:TB - P * kj])\
                       .then_inc(a1_ptd, 1)

                if values:
                    take_pt(0)
                if softmax:
                    for t in range(TPB - 1):
                        row_max(t)
                if values:
                    take_pt(2)
                if softmax:
                    row_max(TPB - 1)
                if softmax:
                    for i, (first, last) in enumerate(((0, 1), (1, TPB))):
                        dve.wait_ge(a1_exp, n * TPB + last)
                        dve.reciprocal(stat1[:, 2, k % 2, first:last], stat1[:, 1, k % 2, first:last])\
                           .then_inc(a1_rcp, 1)
                        dve.wait_ge(a1_rcp, n * 2 + (i + 1))
                        for t in range(first, last):
                            qi = TPB - 1 - t
                            pt = p1[:, k % 2, POFF[qi]:POFF[qi + 1]]
                            dve.tensor_scalar(pt, pt, stat1[:, 2, k % 2, t:t + 1], None, ALU.mult)\
                               .then_inc(a1_norm, 1)
                if k % GH == 0 and (not static or n >= 1):
                    dve.wait_ge(a1_pv, n * TPB)
                    if not static or n > PER1:
                        dve.wait_ge(m_y, it * 2 + 2 * ((k - GH) // PER1))
                    dve.tensor_copy(oT1[:, (k // GH - 1) % 2, :], bank[O1_BANK][:, :]).then_inc(a1_o, 1)
                if k >= PER1 and k % PER1 - 1 in MID_Y:
                    y_stats(it, k // PER1 - 1, MID_Y.index(k % PER1 - 1))
                if k >= PER1 and k % PER1 == MID_U:
                    scale_u(it, k // PER1 - 1)
                if k >= PER1 and k % PER1 == MID_STAT:
                    x1_stats(it, k // PER1 - 1)
                if k >= PER1 and k % PER1 == MID_XN:
                    scale_xn(it, k // PER1 - 1)
                if k >= PER1 and k % PER1 == MID_T:
                    take_xT(it, k // PER1 - 1, dict(enumerate(STK_BANK)))

            run_steps(dve, step1, N1 + 1, PER1, PER1 + 2, 5)
            meet(dve, 1)
            for half in range(2):
                y_stats(B - 1, 0, half)
            offset = sm[:, 7, :]

            def step2(it, k):
                n = it * PER2 + k
                static = isinstance(n, int)
                here, prev = not static or n < N2, not static or 1 <= n <= N2
                if here:
                    for i in range(3):
                        dve.wait_ge(b_hi, n * 3 + (i + 1))
                        hi, lo = (v2_half(k, HI), v2_half(k, LO)) if i == 2 else (qk2[:, i, HI, :], qk2[:, i, LO, :])
                        dve.scalar_tensor_tensor(lo, bank[4 + i][:, :], SCALE2 if i == 0 else 1.0,
                                                 f32(hi), ALU.mult, ALU.subtract).then_inc(b_lo, 1)
                if prev:
                    for t in range(TPB):
                        kj = TPB - 1 - t
                        dve.wait_ge(b_pth, n * TPB + (t + 1 - TPB))
                        dve.tensor_tensor(pT2[:, LO, QOFF[kj]:QOFF[kj + 1]], bank[t][:, 0:TB - P * kj],
                                          f32(pT2[:, HI, QOFF[kj]:QOFF[kj + 1]]), ALU.subtract).then_inc(b_ptl, 1)
                if here:
                    for t in range(TPB):
                        dve.wait_ge(b_s, n * TPB + (t + 1))
                        dve.tensor_reduce(stat2[:, 0, k % 2, t:t + 1], s2(t), AX.X,
                                          ALU.max, negate=True).then_inc(b_max, 1)
                if not static or n >= 2:
                    b = (k - 2) // 2 % B
                    for c in range(C):
                        dve.wait_ge(b_e, n * C + (c + 1 - 2 * C))
                        if static and n == 2 and c == 0:
                            dve.wait_ge(b_acc0, 1)
                        cols = slice(TB * b, TB * (b + 1))
                        dve.tensor_tensor(acc[:, c, cols], acc[:, c, cols], bank[4 + c][:, :], ALU.add)\
                           .then_inc(b_acc, 1)
                if here:
                    dve.wait_ge(b_exp, n * TPB + TPB)
                    dve.reciprocal(stat2[:, 2, k % 2, :], stat2[:, 1, k % 2, :]).then_inc(b_rcp, 1)
                if prev:
                    dve.wait_ge(b_oh, n * 1)
                    dve.tensor_tensor(o2[:, LO, :], bank[7][:, :], f32(o2[:, HI, :]), ALU.subtract)\
                       .then_inc(b_ol, 1)
                if static and n == LAST_U:
                    scale_u(B - 1, 0)
                if static and n == LAST_STAT:
                    x1_stats(B - 1, 0)
                if static and n == LAST_XN:
                    scale_xn(B - 1, 0)
                if static and n in LAST_T:
                    take_xT(B - 1, 0, {LAST_T.index(n): 6})

            run_steps(dve, step2, N2 + 2, PER2, 6, 4)
            meet(dve, 2)
            for g in range(T // 2):
                dve.wait_ge(r_tp, g + 1)
                two = hs[:, 2 * g:2 * g + 2, :].rearrange("p j d -> p (j d)")
                dve.tensor_tensor(two, two, bank[g][:, :], ALU.add).then_inc(r_hid, 1)
            dve.wait_ge(r_sq, T)
            dve.tensor_scalar(var, sm[:, 10, :], 1.0 / D, RMS_EPS, ALU.mult, ALU.add).then_inc(root_in, 1)
            dve.wait_ge(root_in, roots[0] + 1)
            rsqrt(rstd, slice(0, T))
            dve.memset(wtok[:, :, 0:2], 1.0).then_inc(r_rms, 1)

            def norm_half2(b):
                for i in (TPB * b, TPB * b + 1):
                    dve.tensor_scalar(xn2[:, i, :], hs[:, i, :], rstd[:, i:i + 1], None, ALU.mult).then_inc(r_xn, 1)

            def take_xT2(b):
                for c in range(C):
                    dve.wait_ge(r_hi, b * C + c + 1)
                    dve.scalar_tensor_tensor(xT[:, b, LO, c, :], bank[b * C + c][:, :], ln_w[:, 1, c:c + 1],
                                             f32(xT[:, b, HI, c, :]), ALU.mult, ALU.subtract).then_inc(r_lo, 1)

            for b in range(B):
                norm_half2(b)
                if b:
                    take_xT2(b - 1)
            take_xT2(B - 1)

            col = sm[:, 11, :]

            def wide(ap):
                return ap.unsqueeze(2).to_broadcast([P, T, E])

            def logits_less_max():
                dve.wait_ge(r_lgl, 1)
                link(dve.tensor_tensor(lg[:, :, :], pr[:, :, :],
                                       bank[5][:, :].rearrange("p (t a e) -> p t a e", t=T, a=2)[:, :, 0, :], ALU.add))
                link(dve.tensor_reduce(col, lg[:, :, :], AX.X, ALU.max))
                dve.tensor_tensor(lg[:, :, :], lg[:, :, :], wide(col), ALU.subtract).then_inc(r_sub, 1)

            def probabilities():
                dve.wait_ge(r_exp, 1)
                link(dve.tensor_reduce(col, pr[:, :, :], AX.X, ALU.add))
                link(dve.reciprocal(col, col))
                link(dve.tensor_tensor(pr[:, :, :], pr[:, :, :], wide(col), ALU.mult))

            def compare(experts):
                above = []
                for e in experts:
                    own = pr[:, :, e:e + 1]
                    if e:
                        above.append(dve.tensor_tensor(rk[:, :, e, 0:e], pr[:, :, 0:e],
                                                       own.to_broadcast([P, T, e]), ALU.is_ge))
                    above.append(dve.tensor_tensor(rk[:, :, e, e:E], pr[:, :, e:E],
                                                   own.to_broadcast([P, T, E - e]), ALU.is_gt))
                link(*above)

            def count_ranks():
                w = E // 2
                while w > 1:
                    link(dve.tensor_tensor(rk[:, :, :, 0:w], rk[:, :, :, 0:w], rk[:, :, :, w:2 * w], ALU.add))
                    w //= 2
                link(dve.tensor_tensor(lg[:, :, :], rk[:, :, :, 0], rk[:, :, :, 1], ALU.add))

            def weights():
                link(dve.tensor_scalar(lg[:, :, :], lg[:, :, :], float(TOPK), None, ALU.is_lt))
                link(dve.tensor_tensor(pr[:, :, :], pr[:, :, :], lg[:, :, :], ALU.mult))
                link(dve.tensor_reduce(col, pr[:, :, :], AX.X, ALU.add))
                link(dve.reciprocal(col, col))
                dve.tensor_tensor(wtok[:, :, 2:], pr[:, :, :], wide(col), ALU.mult).then_inc(r_w, 1)

            def take_weights(b):
                dve.wait_ge(r_wh, b + 1)
                cols = slice(TB * b, TB * (b + 1))
                dve.tensor_tensor(wT[32:32 + E + 2, cols], bank[4 if b == 0 else 5][0:E + 2, :], f32(wT[0:E + 2, cols]),
                                  ALU.subtract).then_inc(r_wl, 1)

            def final_tiles(g, bank_):
                dve.wait_ge(f_tp, g + 1)
                two = hs[:, 2 * g:2 * g + 2, :].rearrange("p j d -> p (j d)")
                dve.tensor_tensor(two, two, bank_[:, :], ALU.add).then_inc(f_y, 1)
                dve.wait_ge(f_y, g + 1)
                link(*[dve.bn_stats(st6[:, i, :], hs[:, i, :]) for i in (2 * g, 2 * g + 1)])

            def step3(it, k):
                n = it * PER3 + k
                static = isinstance(n, int)
                par = k % 2
                if not static or n < NE:
                    dve.wait_ge(e_silu, n + 1)
                    if k >= SHU:
                        dve.wait_ge(e_w, n - (SHU - 1))
                    if not static or n >= 2:
                        dve.wait_ge(e_hlo, n - 1)
                    gated = h_s[:, par, :]
                    if k >= SHU:
                        gated = h_t[:, par, :]
                        dve.tensor_tensor(gated, h_s[:, par, :], bank[4][:, :], ALU.mult).then_inc(e_sw, 1)
                    dve.wait_ge(e_u, n + 1)
                    if k >= SHU:
                        dve.wait_ge(e_sw, n - (SHU - 1))
                    dve.tensor_tensor(h_t[:, par, :], gated, bank[2 + par][:, :], ALU.mult).then_inc(e_h, 1)
                if k and place(k - 1)[3]:
                    b = place(k - 1)[0]
                    if static and n == SHC:
                        dve.wait_ge(r_zero, 2)
                    for c in range(C):
                        dve.wait_ge(e_dn, n * C - (C - 1 - c))
                        cols = slice(TB * b, TB * (b + 1))
                        dve.tensor_tensor(acc[:, c, cols], acc[:, c, cols], bank[6 + c][:, :], ALU.add)\
                           .then_inc(e_acc, 1)
                if static and n == 1:
                    logits_less_max()
                if static and n == 2:
                    probabilities()
                    compare(range(0, 4))
                if static and n == 3:
                    compare(range(4, 9))
                if static and n == 4:
                    compare(range(9, 14))
                if static and n == 5:
                    compare(range(14, E))
                    count_ranks()
                if static and n == 6:
                    weights()
                if static and n == SHU - 1:
                    take_weights(0)
                    take_weights(1)
                if static and SHU <= n < SHU + B - 2:
                    take_weights(n - SHU + 2)
                r = n - (NE - PER3) if static else 0
                if r > MGC and r < PER3 and r % MGC in (1, 2):
                    final_tiles(2 * (r // MGC - 1) + r % MGC - 1, bank[5])
                if static and n == NE - 1:
                    row_stats(LN_EPS, cols=slice(0, TPB * (B - 1)))
                    done = slice(0, TPB * (B - 1))
                    dve.scalar_tensor_tensor(offset[:, done], mean[:, done], -1.0, rstd[:, done], ALU.mult, ALU.mult)\
                       .then_inc(f_nrm, 1)

            run_steps(dve, step3, NE + 1, PER3, PER3 + 2, 3)
            for g in (T // 2 - 2, T // 2 - 1):
                final_tiles(g, bank[g % 2])
            row_stats(LN_EPS, cols=slice(T - TPB, T))
            link(*[dve.tensor_scalar(u_out[:, i, :], hs[:, i, :], mean[:, i:i + 1], rstd[:, i:i + 1],
                                     ALU.subtract, ALU.mult) for i in range(T - TPB, T)])
            dve.tensor_tensor(u_out[:, T - TPB:, :], u_out[:, T - TPB:, :], x_sb[:, T - TPB:, :], ALU.add)\
               .then_inc(f_last, 1)

        @block.tensor
        def _(pe):
            def product(out, pairs, start=True, stop=True, **kw):
                for i, (a, b) in enumerate(pairs):
                    ins = pe.matmul(out, a, b, start=start and i == 0, stop=stop and i == len(pairs) - 1, **kw)
                return ins

            def mask_diagonal(scores, qi):
                pe.matmul(scores[:, P * qi:P * (qi + 1)], ident_b[:, :], mask_b[:, :], start=True, stop=False,
                          skip_group_check=True)

            pe.wait_ge(const, 6)
            def turn_x(b):
                pe.wait_ge(ph1_xn, b * TPB + TPB)
                if b:
                    pe.wait_ge(ph1_tlo, b * C)
                for c in range(C):
                    for j in range(TPB):
                        ins = pe.transpose(bank[c][:, P * j:P * (j + 1)], xn1[:, b % 2, j, P * c:P * (c + 1)],
                                           ident[:, :])
                    ins.then_inc(ph1_tp, 1)

            turn_x(0)
            for b in range(B):
                pe.wait_ge(ph1_tlo, b * C + C)
                if b == 0:
                    pe.wait_ge(ph1_wl, 1)
                else:
                    pe.wait_ge(ph1_lo, b * 4)
                for m in range(4):
                    product(bank[2 + m][:, :], [(qkv1_hl[:, s, c, P * m:P * (m + 1)], xT1[:, b % 2, r, c, :])
                                                for c in range(C) for s, r in PARTS]).then_inc(ph1_mm, 1)
                if b + 1 < B:
                    turn_x(b + 1)
                if b == 0:
                    pe.wait_ge(ph1_wl, 2)
                else:
                    pe.wait_ge(ph1_v, b * 2)
                for i in range(2):
                    for j in (0, 1):
                        rows = slice(P * (2 * i + j), P * (2 * i + j + 1))
                        ins = product(bank[6 + i][:, D * j:D * (j + 1)],
                                      [(xT1[:, b % 2, s, c, rows], qkv1_hl[:, r, c, 2 * D:3 * D])
                                       for c in range(C) for s, r in PARTS])
                    ins.then_inc(ph1_mm, 1)
            pe.wait_ge(sel_ok, 1)
            meet(pe, 0)

            def stack(g, pair):
                for w, src in enumerate((q1_hl, k1_hl)):
                    product(bank[STK_BANK[w]][:, :],
                            [(sel[:, P * (4 * pair + 2 * w + a):P * (4 * pair + 2 * w + a + 1)], src[:, g, a, :])
                             for a in (HI, LO)]).then_inc(a1_sel, 1)

            def project_y(half, bank_):
                for r in range(2):
                    j = 2 * half + r
                    ins = product(bank_[:, D * r:D * (r + 1)], [(oT1[:, c, P * j:P * (j + 1)], wo1[:, c, :])
                                                                for c in range(C)])
                ins.then_inc(m_y, 1)

            def turn_mid(batch, extra, banks):
                for half_done in (m_xna, m_xnd):
                    pe.wait_ge(half_done, batch * 2 + (extra * 2 + 2))
                for c in banks:
                    for j in range(TPB):
                        ins = pe.transpose(bank[banks[c]][:, P * j:P * (j + 1)], xn_mid[:, j, P * c:P * (c + 1)],
                                           ident[:, :])
                    ins.then_inc(m_tp, 1)

            pe.wait_ge(wo1_in, 16)

            def step1(it, k):
                n = it * PER1 + k
                static = isinstance(n, int)
                softmax, values = not static or n < N1, not static or n >= 1
                head, prev = k % GH, (k - 1) % GH
                if static and n == 0:
                    stack(0, 0)

                def scores(t):
                    qi = TPB - 1 - t
                    rows = slice(64 * (k % 2), 64 * (k % 2) + 64)
                    if t == 0:
                        pe.wait_ge(a1_stk, n + (2 - k % 2))
                    if not static or n >= 1:
                        pe.wait_ge(a1_exp, n * TPB + (t + 1 if t < 2 else TPB) - TPB)
                    m = (k // 2) % 2
                    if t < 2:
                        mask_diagonal(s1(t), qi)
                    elif t == 2:
                        pe.matmul(bank[S1_BANK[2]][:, P:3 * P], ident_b[:, :],
                                  mask_b[:, :].unsqueeze(1).to_broadcast([P, 2, P]), start=True, stop=False,
                                  skip_group_check=True)
                    pe.matmul(s1(t), stk[rows, m, 0, P * qi:P * (qi + 1)], stk[rows, m, 1, 0:P * (qi + 1)],
                              start=False, stop=True, skip_group_check=True).then_inc(a1_s, 1)

                def turn(t):
                    kj = TPB - 1 - t
                    pe.wait_ge(a1_norm, n * TPB + (t + 1 - TPB))
                    if not static or n >= 2 or t >= 2:
                        taken = a1_pta if t % 2 else a1_ptd
                        pe.wait_ge(taken, n * 2 + (t // 2 - 2))
                    for qi in range(kj, TPB):
                        ins = pe.transpose(bank[PT1_BANK[t % 2]][:, P * (qi - kj):P * (qi - kj + 1)],
                                           p1[:, (k - 1) % 2, POFF[qi] + P * kj:POFF[qi] + P * (kj + 1)],
                                           ident[:, :])
                    ins.then_inc(a1_t, 1)

                def values_of(t):
                    kj = TPB - 1 - t
                    pe.wait_ge(a1_pta if t % 2 else a1_ptd, n * 2 + (t // 2 - 1))
                    if t == 0:
                        pe.wait_ge(a1_vpad, n * 1)
                        if prev == 0 and (not static or n > GH):
                            pe.wait_ge(a1_o, it * 2 + (k - 1) // GH)
                    pe.matmul(bank[O1_BANK][:, P * kj:TB], v1_pad[:, kj, prev, :], pT1[:, QOFF[kj]:QOFF[kj + 1]],
                              start=(prev == 0 and t == 0), stop=(prev == GH - 1 and t == TPB - 1),
                              skip_group_check=True).then_inc(a1_pv, 1)

                if values:
                    turn(0)
                    turn(1)
                if softmax:
                    for t in range(TPB):
                        scores(t)
                if values:
                    values_of(0)
                    turn(2)
                    values_of(1)
                    turn(3)
                if k % 2 == 0 and (not static or n // 2 + 1 < N1 // 2):
                    pe.wait_ge(a1_stk, n + 2)
                    if k >= PER1 and k % PER1 - 1 in MID_Y:
                        pe.wait_ge(m_ys, it * 2 + (2 * (k // PER1 - 1) + MID_Y.index(k % PER1 - 1) + 1))
                    if k >= PER1 and k % PER1 - 1 == MID_T:
                        pe.wait_ge(m_lo, it * C + C * (k // PER1))
                    stack(it * 2 + (k + 2) // GH, (k // 2 + 1) % PAIRS1)
                if k >= PER1 and k % PER1 in MID_Y:
                    half = MID_Y.index(k % PER1)
                    pe.wait_ge(a1_stk, n + 3)
                    pe.wait_ge(a1_o, it * 2 + 2 * (k // PER1))
                    project_y(half, bank[STK_BANK[half]])
                if k >= PER1 and k % PER1 == MID_T:
                    pe.wait_ge(a1_stk, n + 3)
                    turn_mid(it, k // PER1 - 1, dict(enumerate(STK_BANK)))
                if values:
                    values_of(2)
                    values_of(3)

            run_steps(pe, step1, N1 + 1, PER1, PER1 + 2, 5)
            meet(pe, 1)
            for half in range(2):
                project_y(half, bank[LAST_Y_BANK[half]])

            def turn_acc(g, bank_, done):
                for r in range(2):
                    for c in range(C):
                        i = 2 * g + r
                        ins = pe.transpose(bank_[:, D * r + P * c:D * r + P * (c + 1)],
                                           acc[:, c, P * i:P * (i + 1)], ident[:, :])
                ins.then_inc(done, 1)

            def step2(it, k):
                n = it * PER2 + k
                static = isinstance(n, int)
                here = not static or n < N2
                prev = not static or 1 <= n <= N2
                b, head = k // 2 % B, k % 2

                def turn(t):
                    kj = TPB - 1 - t
                    pe.wait_ge(b_norm, n * TPB + (t + 1 - TPB))
                    for qi in range(kj, TPB):
                        ins = pe.transpose(bank[t][:, P * (qi - kj):P * (qi - kj + 1)],
                                           p2[:, (k - 1) % 2, POFF[qi] + P * kj:POFF[qi] + P * (kj + 1)],
                                           ident[:, :])
                    ins.then_inc(b_t, 1)

                def scores(t):
                    qi = TPB - 1 - t
                    if prev:
                        pe.wait_ge(b_ptl, n * TPB + (t + 1 - TPB))
                    mask_diagonal(s2(t), qi)
                    product(s2(t),
                            [(qk2[:, 0, s, P * qi:P * (qi + 1)], qk2[:, 1, m, 0:P * (qi + 1)]) for s, m in PARTS],
                            start=False, skip_group_check=True).then_inc(b_s, 1)

                def values_of(t):
                    kj = TPB - 1 - t
                    pe.wait_ge(b_ptl, n * TPB + (t + 1 - TPB))
                    if t == 0 and (not static or n >= 2):
                        pe.wait_ge(b_ol, n - 1)
                    if t == 2 and k % 2 == 1 and here:
                        pe.wait_ge(b_lo, n * 3 + 3)
                    own = slice(P * ((k - 1) % 2), P * ((k - 1) % 2 + 1))
                    product(bank[7][:, P * kj:TB],
                            [(v2[:, (k - 1) // 2 % 2, s, kj, own], pT2[:, m, QOFF[kj]:QOFF[kj + 1]])
                             for s, m in PARTS], start=(t == 0), stop=(t == TPB - 1), skip_group_check=True)\
                        .then_inc(b_pv, 1)

                if here:
                    if b == 0:
                        pe.wait_ge(b_wqkv, it * 3 + (k // PER2 * 3 + (3 if head else 1)))
                    if k == LAST_T[-1] + 1:
                        pe.wait_ge(m_lo, C * B)
                    for i in range(2):
                        if not static or n >= 1:
                            pe.wait_ge(b_lo, n * 3 + (i - 2))
                        if not static or n >= 3:
                            pe.wait_ge(b_acc, n * C + (i + 1 - 3 * C))
                        product(bank[4 + i][:, :],
                                [(w2_hl[:, s, P * (C * (2 * i + head) + c):P * (C * (2 * i + head) + c + 1)],
                                  xT[:, b, m, c, :])
                                 for c in range(C) for s, m in PARTS]).then_inc(b_qkv, 1)
                    if b == 0 and head == 0:
                        pe.wait_ge(b_wqkv, it * 3 + (k // PER2 * 3 + 2))
                    if not static or n >= 1:
                        pe.wait_ge(b_lo, n * 3)
                    if static and n - 1 in LAST_T:
                        pe.wait_ge(m_lo, C * (B - 1) + LAST_T.index(n - 1) + 1)
                    for j in (0, 1):
                        first = P * (2 - 2 * head + j)
                        ins = product(bank[6][:, 2 * P * j:2 * P * (j + 1)],
                                      [(xT[:, b, s, c, first:first + P],
                                        w2_hl[:, m, P * (4 * C + 2 * c):P * (4 * C + 2 * c + 2)])
                                       for c in range(C) for s, m in PARTS])
                    ins.then_inc(b_qkv, 1)
                if prev:
                    for t in range(TPB):
                        turn(t)
                if not static or n >= 2:
                    if k % PER2 == 2:
                        pe.wait_ge(b_wo, it + ((k - 2) // PER2 + 1))
                    pe.wait_ge(b_ol, n - 1)
                    for c in range(C):
                        pe.wait_ge(b_lo, n * 3 + (c + 1) if here else N2 * 3)
                        if not static or n >= 3:
                            pe.wait_ge(b_acc, n * C + (c + 1 - 3 * C))
                        product(bank[4 + c][:, :], [(wo2_hl[:, s, D * head + P * c:D * head + P * (c + 1)], o2[:, m, :])
                                                    for s, m in PARTS]).then_inc(b_e, 1)
                if here:
                    pe.wait_ge(b_lo, n * 3 + 2)
                    if static and n == 0:
                        pe.wait_ge(m_ys, 2 * B)
                    for t in range(TPB):
                        scores(t)
                if static and n in LAST_T:
                    pe.wait_ge(b_lo, n * 3 + 3)
                    turn_mid(B - 1, 0, {LAST_T.index(n): 6})
                if prev:
                    for t in range(TPB):
                        values_of(t)

            run_steps(pe, step2, N2 + 2, PER2, 6, 4)
            meet(pe, 2)
            for g in range(T // 2):
                turn_acc(g, bank[g], r_tp)
            pe.wait_ge(r_hid, T // 2)

            def turn_xn(b):
                pe.wait_ge(r_xn, 2 * (b + 1))
                pe.wait_ge(r_xna, 2 * (b + 1))
                for c in range(C):
                    for j in range(TPB):
                        ins = pe.transpose(bank[b * C + c][:, P * j:P * (j + 1)],
                                           xn2[:, TPB * b + j, P * c:P * (c + 1)], ident[:, :])
                    ins.then_inc(r_tp2, 1)

            for b in range(B - 1):
                turn_xn(b)

            def logits(b):
                if b >= 2:
                    pe.wait_ge(r_lgT, b - 1)
                product(bank[4 + b % 2][0:2 * E, :],
                        [(gate_hl[:, d, :, :].rearrange("p a e -> p (a e)"), xT[:, b, m, d, :])
                         for d in range(C) for m in (HI, LO)]).then_inc(r_row, 1)

            def turn_weights(b):
                if b == 0:
                    pe.wait_ge(r_w, 1)
                if b >= 2:
                    pe.wait_ge(r_wl, b)
                for j in range(TPB):
                    ins = pe.transpose(bank[4 if b == 0 else 5][0:E + 2, P * j:P * (j + 1)], wtok[:, TPB * b + j, :],
                                       ident[:, :])
                ins.then_inc(r_tp3, 1)

            def step3(it, k):
                n = it * PER3 + k
                static = isinstance(n, int)
                b, c, opens, _, _ = place(k)
                cols = slice(TB * b, TB * (b + 1))

                def up(out, first):
                    return product(out, [(moe_hl[:, c, s, first + P * d:first + P * (d + 1)], xT[:, b, m, d, :])
                                         for d in range(C) for s, m in PARTS])

                if not static or n < NE:
                    if b == 0:
                        pe.wait_ge(e_split, it * MGC + (MGC * (k // PER3) + c + 1))
                    if static and n == 0:
                        pe.wait_ge(r_lo, C)
                    if not static or n >= 2:
                        pe.wait_ge(e_silu, n - 1)
                    up(bank[k % 2][:, :], 0).then_inc(e_g, 1)
                    if k >= SHU:
                        if not static or n > SHU:
                            pe.wait_ge(e_sw, n - SHU)
                        if static and n < PER3 and opens:
                            pe.wait_ge(r_wl, b + 1)
                        pe.matmul(bank[4][:, :], sel_c[:, c, :], wT[:, cols], start=True, stop=True).then_inc(e_w, 1)
                    if static and n == 0:
                        turn_xn(B - 1)
                        pe.wait_ge(r_lo, 2 * C)
                    if not static or n >= 2:
                        pe.wait_ge(e_h, n - 1)
                    up(bank[2 + k % 2][:, :], C * P).then_inc(e_u, 1)
                if static and n == 1:
                    logits(2)
                    logits(3)
                if not static or n >= 1:
                    _, cc, opens, closes, runs = place(k - 1)
                    pe.wait_ge(e_hlo, n * 1)
                    for d in range(C):
                        if opens and (not static or n > 1):
                            pe.wait_ge(e_acc, it * (C * B) + C * runs)
                        product(bank[6 + d][:, :],
                                [(moe_hl[:, cc, s, 2 * C * P + P * d:2 * C * P + P * (d + 1)],
                                  h_hl[:, (k - 1) % 2, m, :]) for s, m in PARTS],
                                start=opens, stop=closes).then_inc(e_dn, 1)
                if static and n == 0:
                    pe.wait_ge(gate_lo, 1)
                    pe.wait_ge(r_lo, C * B)
                    logits(0)
                    logits(1)
                if static and n == 1:
                    pe.wait_ge(r_lgT, B)
                    for i in range(T):
                        ins = pe.transpose(bank[5][:, 2 * E * i:2 * E * (i + 1)], lgT[:, P * i:P * (i + 1)],
                                           ident[0:2 * E, 0:2 * E])
                    ins.then_inc(r_lg, 1)
                if static and n == SHU - 1:
                    turn_weights(0)
                    turn_weights(1)
                if static and SHU <= n < SHU + B - 2:
                    turn_weights(n - SHU + 2)
                r = n - (NE - PER3) if static else 0
                if r > MGC and r < PER3 and r % MGC in (1, 2):
                    g = 2 * (r // MGC - 1) + r % MGC - 1
                    pe.wait_ge(e_acc, C * (B * MG + r // MGC))
                    if g:
                        pe.wait_ge(f_y, g)
                    turn_acc(g, bank[5], f_tp)

            run_steps(pe, step3, NE + 1, PER3, PER3 + 2, 3)
            pe.wait_ge(e_acc, (MG + 1) * B * C)
            for g in (T // 2 - 2, T // 2 - 1):
                turn_acc(g, bank[g % 2], f_tp)


def kernel(**inputs):
    import numpy as np
    import concourse.bacc as bacc
    from concourse.bass_utils import run_bass_kernel_spmd

    x = np.asarray(inputs["L0_attn_x"])
    D = x.shape[2]
    C = D // P

    def rows(w):
        w = np.asarray(w)
        return w.T.reshape(w.shape[1] // P, P, w.shape[0]).transpose(1, 0, 2)

    qkv1 = np.concatenate([rows(inputs[f"L0_attn_{n}"]) for n in ("Wq", "Wk", "Wv")], axis=2)
    wo1 = rows(inputs["L0_attn_Wo"])
    q_w, kv_w = rows(inputs["L0_ffn_q_w"]), rows(inputs["L0_ffn_kv_w"])
    H2 = 16
    q_w = q_w.reshape(P, C, H2, 192)[..., :P]
    k_w = kv_w[..., :H2 * P].reshape(P, C, H2, P)
    v_w = kv_w[..., H2 * P:2 * H2 * P].reshape(P, C, H2, P)
    o_w = rows(inputs["L0_ffn_o_w"]).transpose(1, 0, 2)
    q_w, k_w, v_w = (a.reshape(P, C, H2 // 2, 2, P) for a in (q_w, k_w, v_w))
    parts = [a.transpose(2, 0, 3, 1, 4) for a in (q_w, k_w)] + [v_w.transpose(2, 0, 1, 3, 4),
                                                                o_w.reshape(H2 // 2, 2, P, D).transpose(0, 2, 1, 3)]
    qkvo2 = np.concatenate([a.reshape(H2 // 2, P, -1) for a in parts], axis=2)
    ln_w = np.stack([np.asarray(inputs[f"L0_ffn_ln{i}_w"]).reshape(C, P).T for i in (1, 2)], axis=1)
    gate = rows(inputs["L0_ffn_gate_w"])

    w1, w2 = np.asarray(inputs["L0_ffn_w1"]), np.asarray(inputs["L0_ffn_w2"])
    sh1, sh2 = np.asarray(inputs["L0_ffn_sh_gu_w"]), np.asarray(inputs["L0_ffn_sh_down_w"])
    EI, SI = w1.shape[1] // 2, sh2.shape[1]
    MG, MGC = 5, 5
    pad = np.zeros((MG * MGC * P - w1.shape[0] * EI - SI, D), w1.dtype)
    g_w = rows(np.concatenate([sh1[:SI], w1[:, :EI].reshape(-1, D), pad]))
    u_w = rows(np.concatenate([sh1[SI:], w1[:, EI:].reshape(-1, D), pad]))
    d_w = np.concatenate([sh2.T, w2.transpose(0, 2, 1).reshape(-1, D), pad])
    chunks = [a.reshape(P, C, MG, MGC, P).transpose(2, 0, 3, 1, 4).reshape(MG, P, MGC, C * P) for a in (g_w, u_w)]
    moe = np.concatenate(chunks + [d_w.reshape(MG, MGC, P, D).transpose(0, 2, 1, 3)], axis=3)

    stack = np.zeros((P, 4, 2, 2, P), np.float32)
    for pair in range(4):
        for half in range(2):
            for w, parts in enumerate((((0, 1), (2, 3)), ((0, 2), (1, 3)))):
                for a in range(2):
                    for part in parts[a]:
                        for d in range(16):
                            stack[32 * pair + 16 * half + d, pair, w, a, 64 * half + 16 * part + d] = 1.0
    arrays = {"x": x, "qkv1": qkv1, "wo1": wo1, "qkvo2": qkvo2, "ln_w": ln_w, "gate": gate, "moe": moe,
              "stack": stack.reshape(P, -1)}
    arrays = {f"in_{n}": np.ascontiguousarray(a) for n, a in arrays.items()}
    nc = bacc.Bacc("TRN2", target_bir_lowering=False, num_devices=1)
    args = [nc.dram_tensor(n, a.shape, mybir.dt.from_np(a.dtype), kind="ExternalInput").ap()
            for n, a in arrays.items()]
    out = nc.dram_tensor("out_0", x.shape, F32, kind="ExternalOutput").ap()
    sandwich_kernel(nc, *args, out)
    return run_bass_kernel_spmd(nc, [arrays], core_ids=[0]).results[0]["out_0"]
```
